# Optimizing a Trainium2 kernel written in Bass

```python
import numpy as np
import jax
import jax.numpy as jnp

def _softmax(x, axis=-1):
    return jax.nn.softmax(x, axis=axis)

def _gelu(x):
    return jax.nn.gelu(x, approximate=True)

def _silu(x):
    return jax.nn.silu(x)

def _sigmoid(x):
    return jax.nn.sigmoid(x)

def _layernorm(x, axis=-1, eps=1e-05):
    m = jnp.mean(x, axis=axis, keepdims=True)
    v = jnp.var(x, axis=axis, keepdims=True)
    return (x - m) / jnp.sqrt(v + eps)

def _scatter_add(tgt, idx, src, axis=0):
    return tgt.at[idx].add(src)

def _segment_sum(src, seg, n):
    return jax.ops.segment_sum(src, seg, n)
kernel_name = 'mk_sandwich_d2_jaxref_r8_bc1ee3'

def setup_inputs(seed: int=0):
    np.random.seed(seed)
    _w = jnp.asarray

    def _L0_attn_setup():
        import jax, jax.numpy as jnp
        import numpy as np
        D_MODEL = 128
        N_HEADS = 16
        HEAD_DIM = D_MODEL // N_HEADS
        SCALE = HEAD_DIM ** (-0.5)
        MIN_VAL = jnp.finfo(jnp.float32).min

        def _split_heads(y):
            B, T, _ = y.shape
            return y.reshape(B, T, N_HEADS, HEAD_DIM).transpose(0, 2, 1, 3)
        key = jax.random.key(seed)
        ks = jax.random.split(key, 7)
        B, T = (1, 256)
        s = D_MODEL ** (-0.5)
        return {'x': jax.random.normal(ks[0], (B, T, D_MODEL), dtype=jnp.float32), 'Wq': jax.random.normal(ks[1], (D_MODEL, D_MODEL), dtype=jnp.float32) * s, 'Wk1': jax.random.normal(ks[2], (D_MODEL, D_MODEL), dtype=jnp.float32) * s, 'Wk2': jax.random.normal(ks[3], (D_MODEL, D_MODEL), dtype=jnp.float32) * s, 'Wv': jax.random.normal(ks[4], (D_MODEL, D_MODEL), dtype=jnp.float32) * s, 'Wo': jax.random.normal(ks[5], (D_MODEL, D_MODEL), dtype=jnp.float32) * s, 'lambda_logit': jnp.zeros((N_HEADS,), dtype=jnp.float32)}
    _L0_attn_in = _L0_attn_setup()

    def _L0_ffn_setup():
        import jax, jax.numpy as jnp
        import numpy as np
        DIM = 128
        DEPTH = 2
        HEADS = 8
        DIM_HEAD = 64
        WINDOW = 64
        INNER = HEADS * DIM_HEAD
        HID = int(DIM * 4 * 2 / 3)
        B, N = (2, 1024)
        QK_SCALE = 8.0

        def shift_token(t):
            t1, t2 = jnp.split(t, 2, axis=-1)
            t2 = jnp.pad(t2, ((0, 0), (1, 0), (0, 0)))[:, :-1]
            return jnp.concatenate([t1, t2], axis=-1)

        def l2norm(t):
            return t / jnp.clip(jnp.linalg.norm(t, axis=-1, keepdims=True), 1e-12)

        def rotate_half(x):
            x1, x2 = jnp.split(x, 2, axis=-1)
            return jnp.concatenate([-x2, x1], axis=-1)

        def rotary_xpos(q, k):
            n = q.shape[-2]
            half_idx = jnp.arange(0, DIM_HEAD, 2, dtype=jnp.float32)
            inv_freq = 1.0 / 10000.0 ** (half_idx / DIM_HEAD)
            t = jnp.arange(n, dtype=jnp.float32)
            freqs = t[:, None] * inv_freq[None, :]
            freqs = jnp.concatenate([freqs, freqs], axis=-1)
            base = (half_idx + 0.4 * DIM_HEAD) / (1.4 * DIM_HEAD)
            power = (t - n // 2) / float(WINDOW // 2)
            scale = base[None, :] ** power[:, None]
            scale = jnp.concatenate([scale, scale], axis=-1)
            cos, sin = (jnp.cos(freqs), jnp.sin(freqs))
            q = q * cos * scale + rotate_half(q) * sin * scale
            k = k * cos / scale + rotate_half(k) * sin / scale
            return (q, k)

        def local_attention(q, k, v):
            b, h, n, d = q.shape
            w = n // WINDOW
            bq = q.reshape(b, h, w, WINDOW, d) * QK_SCALE
            bk = k.reshape(b, h, w, WINDOW, d)
            bv = v.reshape(b, h, w, WINDOW, d)

            def look_around(t):
                p = jnp.pad(t, ((0, 0), (0, 0), (1, 0), (0, 0), (0, 0)))
                return jnp.concatenate([p[:, :, :w], p[:, :, 1:]], axis=3)
            bk, bv = (look_around(bk), look_around(bv))
            bt = jnp.arange(n).reshape(w, WINDOW)
            btp = jnp.pad(bt, ((1, 0), (0, 0)), constant_values=-1)
            btk = jnp.concatenate([btp[:w], btp[1:]], axis=1)
            sim = jnp.einsum('bhwid,bhwjd->bhwij', bq, bk)
            i = bt[:, :, None]
            j = btk[:, None, :]
            mask = (i < j) | (i > j + WINDOW) | (j == -1)
            sim = jnp.where(mask, -jnp.finfo(sim.dtype).max, sim)
            attn = jax.nn.softmax(sim, axis=-1)
            out = jnp.einsum('bhwij,bhwjd->bhwid', attn, bv)
            return out.reshape(b, h, n, d)

        def _layer(x, wqkv, qs, ksc, wo, lg, lb, w1, b1, w2, b2):
            b, n, _ = x.shape
            h = shift_token(x)
            qkv = h @ wqkv
            q, k, v = jnp.split(qkv, 3, axis=-1)
            to_heads = lambda t: t.reshape(b, n, HEADS, DIM_HEAD).transpose(0, 2, 1, 3)
            q, k, v = (to_heads(q), to_heads(k), to_heads(v))
            q = l2norm(q) * qs
            k = l2norm(k) * ksc
            q, k = rotary_xpos(q, k)
            o = local_attention(q, k, v)
            o = o.transpose(0, 2, 1, 3).reshape(b, n, INNER)
            x = x + o @ wo
            h = shift_token(x)
            mu = h.mean(-1, keepdims=True)
            var = h.var(-1, keepdims=True)
            h = (h - mu) / jnp.sqrt(var + 1e-05) * lg + lb
            h = h @ w1 + b1
            a, g = jnp.split(h, 2, axis=-1)
            h = a * jax.nn.gelu(g, approximate=False)
            x = x + h @ w2 + b2
            return x
        key = jax.random.key(seed)
        ks = jax.random.split(key, 6)
        return {'x': jax.random.normal(ks[0], (B, N, DIM), jnp.float32), 'wqkv': jax.random.normal(ks[1], (DEPTH, DIM, 3 * INNER), jnp.float32) * 0.02, 'q_scale': jnp.ones((DEPTH, DIM_HEAD), jnp.float32), 'k_scale': jnp.ones((DEPTH, DIM_HEAD), jnp.float32), 'wo': jax.random.normal(ks[2], (DEPTH, INNER, DIM), jnp.float32) * 0.02, 'ln_g': jnp.ones((DEPTH, DIM), jnp.float32), 'ln_b': jnp.zeros((DEPTH, DIM), jnp.float32), 'w1': jax.random.normal(ks[3], (DEPTH, DIM, 2 * HID), jnp.float32) * 0.02, 'b1': jnp.zeros((DEPTH, 2 * HID), jnp.float32), 'w2': jax.random.normal(ks[4], (DEPTH, HID, DIM), jnp.float32) * 0.02, 'b2': jnp.zeros((DEPTH, DIM), jnp.float32)}
    _L0_ffn_in = _L0_ffn_setup()

    def _L1_attn_setup():
        import jax, jax.numpy as jnp
        import numpy as np
        key = jax.random.key(seed)
        ks = jax.random.split(key, 6)
        Bsz, S, H, N = (4, 512, 128, 32)
        return {'x': jax.random.normal(ks[0], (Bsz, S, H), jnp.float32), 'A': jax.random.normal(ks[1], (N, N), jnp.float32) * 0.01, 'Bm': jax.random.normal(ks[2], (N, N), jnp.float32) * 0.01, 'C': jax.random.normal(ks[3], (H, N), jnp.float32) * 0.01, 'D': jnp.full((H,), 0.01, jnp.float32), 'W_in': jax.random.normal(ks[4], (N, H), jnp.float32) / np.sqrt(H).astype(np.float32), 'b_in': jnp.zeros((N,), jnp.float32)}
    _L1_attn_in = _L1_attn_setup()

    def _L1_ffn_setup():
        import jax, jax.numpy as jnp
        import numpy as np
        TOP_K = 2
        key = jax.random.key(seed)
        k0, k1, k2, k3, k4 = jax.random.split(key, 5)
        B, S, D, H, E = (4, 256, 128, 256, 8)
        x = jax.random.normal(k0, (B, S, D), dtype=jnp.float32)
        router_w = jax.random.normal(k1, (E, D), dtype=jnp.float32) * D ** (-0.5)
        w_gate = jax.random.normal(k2, (E, D, H), dtype=jnp.float32) * D ** (-0.5)
        w_up = jax.random.normal(k3, (E, D, H), dtype=jnp.float32) * D ** (-0.5)
        w_down = jax.random.normal(k4, (E, H, D), dtype=jnp.float32) * H ** (-0.5)
        return {'x': x, 'router_w': router_w, 'w_gate': w_gate, 'w_up': w_up, 'w_down': w_down}
    _L1_ffn_in = _L1_ffn_setup()
    _d = {'L0_attn_x': _L0_attn_in['x'], 'L0_attn_Wq': _L0_attn_in['Wq'], 'L0_attn_Wk1': _L0_attn_in['Wk1'], 'L0_attn_Wk2': _L0_attn_in['Wk2'], 'L0_attn_Wv': _L0_attn_in['Wv'], 'L0_attn_Wo': _L0_attn_in['Wo'], 'L0_attn_lambda_logit': _L0_attn_in['lambda_logit'], 'L0_ffn_wqkv': _L0_ffn_in['wqkv'], 'L0_ffn_q_scale': _L0_ffn_in['q_scale'], 'L0_ffn_k_scale': _L0_ffn_in['k_scale'], 'L0_ffn_wo': _L0_ffn_in['wo'], 'L0_ffn_ln_g': _L0_ffn_in['ln_g'], 'L0_ffn_ln_b': _L0_ffn_in['ln_b'], 'L0_ffn_w1': _L0_ffn_in['w1'], 'L0_ffn_b1': _L0_ffn_in['b1'], 'L0_ffn_w2': _L0_ffn_in['w2'], 'L0_ffn_b2': _L0_ffn_in['b2'], 'L1_attn_A': _L1_attn_in['A'], 'L1_attn_Bm': _L1_attn_in['Bm'], 'L1_attn_C': _L1_attn_in['C'], 'L1_attn_D': _L1_attn_in['D'], 'L1_attn_W_in': _L1_attn_in['W_in'], 'L1_attn_b_in': _L1_attn_in['b_in'], 'L1_ffn_router_w': _L1_ffn_in['router_w'], 'L1_ffn_w_gate': _L1_ffn_in['w_gate'], 'L1_ffn_w_up': _L1_ffn_in['w_up'], 'L1_ffn_w_down': _L1_ffn_in['w_down']}
    _x0 = _d['L0_attn_x']
    _d['L0_attn_x'] = jax.random.normal(jax.random.fold_in(jax.random.key(seed), 1), (16, 256, 128), dtype=_x0.dtype)
    del _x0
    return _d

def reference(L0_attn_x, L0_attn_Wq, L0_attn_Wk1, L0_attn_Wk2, L0_attn_Wv, L0_attn_Wo, L0_attn_lambda_logit, L0_ffn_wqkv, L0_ffn_q_scale, L0_ffn_k_scale, L0_ffn_wo, L0_ffn_ln_g, L0_ffn_ln_b, L0_ffn_w1, L0_ffn_b1, L0_ffn_w2, L0_ffn_b2, L1_attn_A, L1_attn_Bm, L1_attn_C, L1_attn_D, L1_attn_W_in, L1_attn_b_in, L1_ffn_router_w, L1_ffn_w_gate, L1_ffn_w_up, L1_ffn_w_down):

    def _L0_attn_ref(x, Wq, Wk1, Wk2, Wv, Wo, lambda_logit):
        import jax, jax.numpy as jnp
        import numpy as np
        D_MODEL = 128
        N_HEADS = 16
        HEAD_DIM = D_MODEL // N_HEADS
        SCALE = HEAD_DIM ** (-0.5)
        MIN_VAL = jnp.finfo(jnp.float32).min

        def _split_heads(y):
            B, T, _ = y.shape
            return y.reshape(B, T, N_HEADS, HEAD_DIM).transpose(0, 2, 1, 3)
        B, T, _ = x.shape
        q = _split_heads(x @ Wq.T)
        k1 = _split_heads(x @ Wk1.T)
        k2 = _split_heads(x @ Wk2.T)
        v = _split_heads(x @ Wv.T)
        s1 = jnp.einsum('bhqd,bhkd->bhqk', q, k1) * SCALE
        s2 = jnp.einsum('bhqd,bhkd->bhqk', q, k2) * SCALE
        causal = jnp.arange(T)[None, :] <= jnp.arange(T)[:, None]
        s1 = jnp.where(causal[None, None], s1, MIN_VAL)
        s2 = jnp.where(causal[None, None], s2, MIN_VAL)
        attn_exp = jax.nn.softmax(s1, axis=-1)
        attn_noise = jax.nn.softmax(s2, axis=-1)
        lam = jax.nn.sigmoid(lambda_logit)[None, :, None, None]
        attn = attn_exp - lam * attn_noise
        denom = jnp.maximum(jnp.sum(jnp.abs(attn), axis=-1, keepdims=True), 1e-06)
        attn = attn / denom
        out = jnp.einsum('bhqk,bhkd->bhqd', attn, v)
        out = out.transpose(0, 2, 1, 3).reshape(B, T, D_MODEL)
        return out @ Wo.T

    def _L0_ffn_ref(x, wqkv, q_scale, k_scale, wo, ln_g, ln_b, w1, b1, w2, b2):
        import jax, jax.numpy as jnp
        import numpy as np
        DIM = 128
        DEPTH = 2
        HEADS = 8
        DIM_HEAD = 64
        WINDOW = 64
        INNER = HEADS * DIM_HEAD
        HID = int(DIM * 4 * 2 / 3)
        B, N = (2, 1024)
        QK_SCALE = 8.0

        def shift_token(t):
            t1, t2 = jnp.split(t, 2, axis=-1)
            t2 = jnp.pad(t2, ((0, 0), (1, 0), (0, 0)))[:, :-1]
            return jnp.concatenate([t1, t2], axis=-1)

        def l2norm(t):
            return t / jnp.clip(jnp.linalg.norm(t, axis=-1, keepdims=True), 1e-12)

        def rotate_half(x):
            x1, x2 = jnp.split(x, 2, axis=-1)
            return jnp.concatenate([-x2, x1], axis=-1)

        def rotary_xpos(q, k):
            n = q.shape[-2]
            half_idx = jnp.arange(0, DIM_HEAD, 2, dtype=jnp.float32)
            inv_freq = 1.0 / 10000.0 ** (half_idx / DIM_HEAD)
            t = jnp.arange(n, dtype=jnp.float32)
            freqs = t[:, None] * inv_freq[None, :]
            freqs = jnp.concatenate([freqs, freqs], axis=-1)
            base = (half_idx + 0.4 * DIM_HEAD) / (1.4 * DIM_HEAD)
            power = (t - n // 2) / float(WINDOW // 2)
            scale = base[None, :] ** power[:, None]
            scale = jnp.concatenate([scale, scale], axis=-1)
            cos, sin = (jnp.cos(freqs), jnp.sin(freqs))
            q = q * cos * scale + rotate_half(q) * sin * scale
            k = k * cos / scale + rotate_half(k) * sin / scale
            return (q, k)

        def local_attention(q, k, v):
            b, h, n, d = q.shape
            w = n // WINDOW
            bq = q.reshape(b, h, w, WINDOW, d) * QK_SCALE
            bk = k.reshape(b, h, w, WINDOW, d)
            bv = v.reshape(b, h, w, WINDOW, d)

            def look_around(t):
                p = jnp.pad(t, ((0, 0), (0, 0), (1, 0), (0, 0), (0, 0)))
                return jnp.concatenate([p[:, :, :w], p[:, :, 1:]], axis=3)
            bk, bv = (look_around(bk), look_around(bv))
            bt = jnp.arange(n).reshape(w, WINDOW)
            btp = jnp.pad(bt, ((1, 0), (0, 0)), constant_values=-1)
            btk = jnp.concatenate([btp[:w], btp[1:]], axis=1)
            sim = jnp.einsum('bhwid,bhwjd->bhwij', bq, bk)
            i = bt[:, :, None]
            j = btk[:, None, :]
            mask = (i < j) | (i > j + WINDOW) | (j == -1)
            sim = jnp.where(mask, -jnp.finfo(sim.dtype).max, sim)
            attn = jax.nn.softmax(sim, axis=-1)
            out = jnp.einsum('bhwij,bhwjd->bhwid', attn, bv)
            return out.reshape(b, h, n, d)

        def _layer(x, wqkv, qs, ksc, wo, lg, lb, w1, b1, w2, b2):
            b, n, _ = x.shape
            h = shift_token(x)
            qkv = h @ wqkv
            q, k, v = jnp.split(qkv, 3, axis=-1)
            to_heads = lambda t: t.reshape(b, n, HEADS, DIM_HEAD).transpose(0, 2, 1, 3)
            q, k, v = (to_heads(q), to_heads(k), to_heads(v))
            q = l2norm(q) * qs
            k = l2norm(k) * ksc
            q, k = rotary_xpos(q, k)
            o = local_attention(q, k, v)
            o = o.transpose(0, 2, 1, 3).reshape(b, n, INNER)
            x = x + o @ wo
            h = shift_token(x)
            mu = h.mean(-1, keepdims=True)
            var = h.var(-1, keepdims=True)
            h = (h - mu) / jnp.sqrt(var + 1e-05) * lg + lb
            h = h @ w1 + b1
            a, g = jnp.split(h, 2, axis=-1)
            h = a * jax.nn.gelu(g, approximate=False)
            x = x + h @ w2 + b2
            return x
        for l in range(DEPTH):
            x = _layer(x, wqkv[l], q_scale[l], k_scale[l], wo[l], ln_g[l], ln_b[l], w1[l], b1[l], w2[l], b2[l])
        return x

    def _L1_attn_ref(x, A, Bm, C, D, W_in, b_in):
        import jax, jax.numpy as jnp
        import numpy as np
        u = jnp.einsum('bsh,nh->bsn', x, W_in) + b_in
        uB = jnp.einsum('bsn,mn->bsm', u, Bm)

        def step(h, uB_t):
            h = h @ A + uB_t
            return (h, h)
        h0 = jnp.zeros((x.shape[0], A.shape[0]), x.dtype)
        _, hs = jax.lax.scan(step, h0, jnp.swapaxes(uB, 0, 1))
        hs = jnp.swapaxes(hs, 0, 1)
        return jnp.einsum('bsn,hn->bsh', hs, C) + D

    def _L1_ffn_ref(x, router_w, w_gate, w_up, w_down):
        import jax, jax.numpy as jnp
        import numpy as np
        TOP_K = 2
        B, S, D = x.shape
        E = router_w.shape[0]
        xt = x.reshape(-1, D)
        logits = xt @ router_w.T
        topk_vals, topk_idx = jax.lax.top_k(logits, TOP_K)
        g = jax.nn.sigmoid(topk_vals)
        g = g / (g.sum(axis=-1, keepdims=True) + 1e-10)
        out = jnp.zeros_like(xt)
        for e in range(E):
            ge = jnp.sum(jnp.where(topk_idx == e, g, jnp.zeros_like(g)), axis=-1)
            h = jax.nn.silu(xt @ w_gate[e]) * (xt @ w_up[e])
            out = out + ge[:, None] * (h @ w_down[e])
        return out.reshape(B, S, D)
    x = L0_attn_x
    x = x + _layernorm(_L0_attn_ref(_layernorm(x, axis=-1), L0_attn_Wq, L0_attn_Wk1, L0_attn_Wk2, L0_attn_Wv, L0_attn_Wo, L0_attn_lambda_logit), axis=-1)
    x = x + _layernorm(_L0_ffn_ref(_layernorm(x, axis=-1), L0_ffn_wqkv, L0_ffn_q_scale, L0_ffn_k_scale, L0_ffn_wo, L0_ffn_ln_g, L0_ffn_ln_b, L0_ffn_w1, L0_ffn_b1, L0_ffn_w2, L0_ffn_b2), axis=-1)
    x = x + _layernorm(_L1_attn_ref(_layernorm(x, axis=-1), L1_attn_A, L1_attn_Bm, L1_attn_C, L1_attn_D, L1_attn_W_in, L1_attn_b_in), axis=-1)
    x = x + _layernorm(_L1_ffn_ref(_layernorm(x, axis=-1), L1_ffn_router_w, L1_ffn_w_gate, L1_ffn_w_up, L1_ffn_w_down), axis=-1)
    return x

_drawn_inputs = setup_inputs


def setup_inputs(seed=0):
    import zlib

    import numpy as np

    out = dict(_drawn_inputs(seed))
    spreads = {'L0_attn_lambda_logit': (0.0, 0.1),
     'L0_ffn_q_scale': (1.0, 0.6),
     'L0_ffn_k_scale': (1.0, 0.6),
     'L0_ffn_ln_g': (1.0, 0.6),
     'L0_ffn_ln_b': (0.0, 0.677),
     'L0_ffn_b1': (0.0, 0.308),
     'L0_ffn_b2': (0.0, 0.1),
     'L1_attn_D': (0.009999999776482582, 0.2),
     'L1_attn_b_in': (0.0, 0.1)}
    factors = {}
    for name, (base, spread) in spreads.items():
        noise = np.random.default_rng([zlib.crc32(name.encode()), seed]).standard_normal(out[name].shape)
        drawn = base * np.exp(spread * noise) if base else spread * noise
        out[name] = jnp.asarray(drawn.astype(out[name].dtype))
    for name, factor in factors.items():
        out[name] = (out[name] * factor).astype(out[name].dtype)
    return out
```

```python
import numpy as np
import concourse.bass as bass
from concourse import mybir
from contextlib import ExitStack

FP32 = mybir.dt.float32
BF16 = mybir.dt.bfloat16
ALU = mybir.AluOpType
ACT = mybir.ActivationFunctionType
AX = mybir.AxisListType

P = 128
D = 128
BATCH = 16
T = 256
QT = T // P
TILES = BATCH * QT
EPS_LN = 1e-5


class Signal:
    opened = []

    def __init__(self, sem, per, base=0):
        self.sem, self.per, self.base = sem, per, base + 1
        self.opened.append(self)

    def early(self, k):
        return k + 1

    def at(self, pair, half, k):
        return pair * (2 * self.per) + (half * self.per + k + self.base)


class Chain(Signal):

    def __init__(self, sem, per, base=0):
        super().__init__(sem, per, base)
        self.k = 0

    def begin(self, eng, pair, half):
        self.eng, self.pair, self.half, self.k = eng, pair, half, 0

    def restart(self, raises):
        self.base = raises + 1

    def mark(self, ins):
        self.k += 1
        ins.then_inc(self.sem, 1)
        return self.k

    def wait(self, k):
        self.eng.wait_ge(self.sem, self.at(self.pair, self.half, k))

    def last(self):
        self.wait(self.k)

    def end(self):
        assert self.k == self.per, f"{self.k} raises a batch, not {self.per}"


def open_signals(eng):
    for signal in Signal.opened:
        eng.sem_inc(signal.sem, 1)
    Signal.opened.clear()


APART = {}


def apart(eng, scratch):
    eng.tensor_tensor(scratch, scratch, scratch, ALU.mult)

CHAIN_A = 62
CHAIN_B = 10
CHAIN_F = 2
CHAIN_M, CHAIN_M_PRE = 13, 10


def differential_attention(nc, X, consts, weights):
    H, HD = 16, 8
    GH = 4
    SCALE = HD ** -0.5
    ident, identb, causal, headrow, neglam = (consts[k] for k in ("ident", "identb", "causal", "headrow", "neglam"))
    wq, wk1, wk2, wv, wo = (weights[k] for k in ("Wq", "Wk1", "Wk2", "Wv", "Wo"))
    minus_half = consts["minus_half"]

    with ExitStack() as ctx:
        sb = lambda name, shape, dt=FP32: ctx.enter_context(nc.sbuf_tensor("a_" + name, shape, dt))
        ps = lambda name, shape: ctx.enter_context(nc.psum_tensor("a_" + name, shape, FP32))
        sem = lambda name: nc.alloc_semaphore("a_" + name)

        qm = sb("qm", [P, 2, H, T])
        qT = sb("qT", [P, T])
        kT = sb("kT", [P, 2, 2, T])
        vp = sb("vp", [P, 2, QT, H, 32])
        xn = sb("xn", [P, QT, D])
        xnT = sb("xnT", [P, T])
        st = sb("st", [P, 2, QT, 6])
        mv = sb("mv", [P, 2, QT, 2])
        rs = sb("rs", [P, 2, QT])
        nm = sb("nm", [P, 2, 2, 2])
        Z = sb("Z", [P, 2, H, 2, 2])
        E = sb("E", [P, 2, 2, 384])
        rz = sb("rz", [P, 2, 2])
        cf = sb("cf", [P, 2, 2])
        d = sb("d", [P, 2, 384])
        ab = sb("ab", [P, 2, H, 3])
        den = sb("den", [P, 2, H])
        floor = sb("floor", [P, 2, H])
        dT = sb("dT", [P, 2, 384])
        OT = sb("OT", [P, H // GH, T])
        On = sb("On", [P, QT, D])
        OnT = sb("OnT", [P, T])
        y = sb("y", [P, QT, D])
        yn = sb("yn", [P, QT, D])

        psS = ps("psS", [P, 2, 2, 512])
        psT = ps("psT", [P, 2, 512])
        psO = ps("psO", [P, T])
        psM = ps("psM", [P, 512])

        E_OT0, E_OT1, E_ONT, E_Y, P_XNT, P_Q, P_K1, P_K2, P_V = range(9)
        USES, PRE = 9, 5
        misc_full = Signal(sem("misc_full"), USES, PRE)
        misc_free = Signal(sem("misc_free"), USES, PRE)
        scored = Signal(sem("scored"), H)
        maxed = Signal(sem("maxed"), H)
        exped = Signal(sem("exped"), H, 2)
        mixed = Signal(sem("mixed"), H, 2)
        turned = Signal(sem("turned"), H, 2)
        evaced = Signal(sem("evaced"), H, 2)
        pved = Signal(sem("pved"), H, 2)
        otmoved = Signal(sem("otmoved"), H // GH, 1)
        qm_ready = Signal(sem("qm_ready"), H)
        xn_ready = Signal(sem("xn_ready"), 1, 1)
        var_ready = Signal(sem("var_ready"), 2, 1)
        rs_ready = Signal(sem("rs_ready"), 2, 1)
        den_ready = Signal(sem("den_ready"), 1)
        added = Signal(sem("added"), 1)
        zeroed = sem("zeroed")
        own = Chain(sem("own"), CHAIN_A, 4)

        block = ctx.enter_context(nc.Block())
        LAST = BATCH // 2

        def x_of(pair, half):
            return X[:, bass.ds((pair * 2 + (half + 1)) * QT, QT), :]

        @block.sync
        def _(sp):
            open_signals(sp)

        @block.gpsimd
        def _(pool):
            for tile in (vp, OT, Z, ab, dT):
                pool.memset(tile[:], 1.0 if tile in (Z, ab) else 0.0).then_inc(zeroed, 1)

            def rstd(which, pair, half, k):
                pool.wait_ge(var_ready.sem, var_ready.at(pair, half, k))
                pool.tensor_tensor(rs[:, which, :], mv[:, which, :, 1], minus_half[:, 0:QT], ALU.pow)\
                    .then_inc(rs_ready.sem, 1)

            def mask_heads(half):
                apart(pool, APART["pool"])
                for h in range(H):
                    pool.tensor_scalar(qm[:, half % 2, h, :], qT[:, :], headrow[:, h:h + 1], 1.0,
                                       ALU.mult, ALU.mult).then_inc(qm_ready.sem, 1)

            rstd(0, 0, 0, 0)
            pool.wait_ge(misc_free.sem, misc_free.early(2))
            mask_heads(0)
            with pool.Fori(0, LAST) as pair:
                for half in range(2):
                    rstd(0, pair, half, 1)
                    rstd(1, pair, half, 2)
                    pool.wait_ge(misc_free.sem, misc_free.at(pair, half, P_Q + 1))
                    pool.wait_ge(scored.sem, scored.at(pair, half, 0))
                    mask_heads(half + 1)
            rstd(1, LAST, 0, 1)

        @block.vector
        def _(dve):
            def maxima(pair, half, h):
                s = h % 2
                dve.wait_ge(scored.sem, scored.at(pair, half, h + 1))
                dve.tensor_reduce(nm[:, s, 0, :], psS[:, s, :, 0:P], axis=AX.X, op=ALU.max, negate=True)
                dve.tensor_reduce(nm[:, s, 1, :], psS[:, s, :, P:384], axis=AX.X, op=ALU.max, negate=True)\
                   .then_inc(maxed.sem, 1)

            def mix(pair, half, h):
                s, p = h % 2, half % 2
                dve.wait_ge(exped.sem, exped.at(pair, half, h + 1))
                own.mark(dve.reciprocal(rz[:, s, :], Z[:, p, h, :, 1]))
                own.last()
                own.mark(dve.scalar_tensor_tensor(out=cf[:, s, :], in0=Z[:, p, h, :, 0], scalar=neglam[:, h:h + 1],
                                                  in1=rz[:, s, :], op0=ALU.mult, op1=ALU.mult))
                dve.wait_ge(turned.sem, turned.at(pair, half, h - 1))
                own.last()
                for t, c0, c1 in ((0, 0, P), (1, P, 384)):
                    ins = dve.scalar_tensor_tensor(out=d[:, s, c0:c1], in0=E[:, s, 1, c0:c1],
                                                   scalar=cf[:, s, t:t + 1], in1=E[:, s, 0, c0:c1],
                                                   op0=ALU.mult, op1=ALU.add)
                ins.then_inc(mixed.sem, 1)
                dve.wait_ge(mixed.sem, mixed.at(pair, half, h + 1))
                own.mark(dve.tensor_reduce(ab[:, p, h, :], d[:, s, :].rearrange("p (c k) -> p c k", c=3),
                                           axis=AX.X, op=ALU.add, apply_absolute_value=True))

            def variance(which, src):
                for t in range(QT):
                    own.mark(dve.bn_stats(st[:, which, t, :], src[:, t, :]))
                own.last()
                apart(dve, APART["dve"])
                for t in range(QT):
                    own.mark(dve.bn_aggr(mv[:, which, t, :], st[:, which, t, :]))
                own.last()
                dve.tensor_scalar(mv[:, which, :, 1], mv[:, which, :, 1], EPS_LN, None, ALU.add)\
                   .then_inc(var_ready.sem, 1)

            def normalise_x(xs):
                for t in range(QT):
                    ins = dve.tensor_scalar(xn[:, t, :], xs[:, t, :], mv[:, 0, t, 0:1], rs[:, 0, t:t + 1],
                                            ALU.subtract, ALU.mult)
                ins.then_inc(xn_ready.sem, 1)

            def denominators(pair, half):
                q = (half - 1) % 2
                own.last()
                own.mark(dve.tensor_copy(den[:, 0, :], ab[:, q, :, 0]))
                own.mark(dve.tensor_tensor(den[:, 1, :], ab[:, q, :, 1], ab[:, q, :, 2], ALU.add))
                own.last()
                for t in range(QT):
                    own.mark(dve.scalar_tensor_tensor(out=floor[:, t, :], in0=Z[:, q, :, t, 0], scalar=1e-6,
                                                      in1=den[:, t, :], op0=ALU.mult, op1=ALU.max))
                own.last()
                dve.reciprocal(den[:, :, :], floor[:, :, :]).then_inc(den_ready.sem, 1)

            def normalise_o(pair, half, t):
                dve.wait_ge(misc_full.sem, misc_full.at(pair, half, E_OT0 + t + 1))
                dve.wait_ge(den_ready.sem, den_ready.at(pair, half, 1))
                dve.tensor_tensor(On[:, t, :].rearrange("p (h e) -> p h e", e=HD),
                                  psM[:, :].rearrange("p (h e) -> p h e", e=32)[:, :, 0:HD],
                                  den[:, t, :].unsqueeze(2).broadcast_to([P, H, HD]), ALU.mult)\
                   .then_inc(misc_free.sem, 1)

            def residual(pair, half, k):
                dve.wait_ge(rs_ready.sem, rs_ready.at(pair, half, k))
                for t in range(QT):
                    own.mark(dve.tensor_scalar(yn[:, t, :], y[:, t, :], mv[:, 1, t, 0:1], rs[:, 1, t:t + 1],
                                               ALU.subtract, ALU.mult))
                own.last()
                xs = x_of(pair, half - 1)
                dve.tensor_tensor(xs, xs, yn[:, :, :], ALU.add).then_inc(added.sem, 1)

            dve.memset(psO[:, :], 0.0).then_inc(zeroed, 1)
            dve.wait_ge(zeroed, 6)
            own.begin(dve, 0, 0)
            own.restart(0)
            variance(0, x_of(0, 0))
            own.restart(own.k)
            assert own.k == 4
            dve.wait_ge(rs_ready.sem, rs_ready.early(1))
            normalise_x(x_of(0, 0))
            maxima(0, 0, 0)
            with dve.Fori(0, LAST) as pair:
                for half in range(2):
                    own.begin(dve, pair, half)
                    for s in range(H):
                        maxima(pair, half + (s + 1) // H, (s + 1) % H)
                        if s == 0:
                            denominators(pair, half)
                        mix(pair, half, s)
                        if s in (2, 4):
                            normalise_o(pair, half, s // 2 - 1)
                        if s == 5:
                            variance(0, x_of(pair, half + 1))
                        if s == 7:
                            dve.wait_ge(rs_ready.sem, rs_ready.at(pair, half, 1))
                            dve.wait_ge(misc_full.sem, misc_full.at(pair, half - 1, P_XNT + 1))
                            normalise_x(x_of(pair, half + 1))
                        if s == 9:
                            dve.wait_ge(misc_free.sem, misc_free.at(pair, half, E_Y + 1))
                            variance(1, y)
                        if s == 12:
                            residual(pair, half, 2)
                    own.end()
            own.begin(dve, LAST, 0)
            denominators(LAST, 0)
            normalise_o(LAST, 0, 0)
            normalise_o(LAST, 0, 1)
            dve.wait_ge(misc_free.sem, misc_free.at(LAST, 0, E_Y + 1))
            variance(1, y)
            residual(LAST, 0, 1)

        @block.scalar
        def _(act):
            def exps(pair, half, h, first=False):
                s, p = h % 2, half % 2
                act.wait_ge(maxed.sem, maxed.at(pair, half, h + 1))
                act.wait_ge(mixed.sem, mixed.at(pair, half, h - 1))
                if h == 0:
                    act.wait_ge(den_ready.sem, den_ready.at(pair, half, 0))
                for t, c0, c1 in ((0, 0, P), (1, P, 384)):
                    for m in range(2):
                        ins = act.activation(E[:, s, m, c0:c1], psS[:, s, m, c0:c1], ACT.Exp,
                                             bias=nm[:, s, t, m:m + 1], accum_out=Z[:, p, h, t, m:m + 1])
                ins.then_inc(exped.sem, 1)

            def evac_d(pair, half, h):
                s = h % 2
                act.wait_ge(turned.sem, turned.at(pair, half, h + 1))
                act.wait_ge(pved.sem, pved.at(pair, half, h - 1))
                act.activation(dT[:, s, :], psT[:, s, 0:384], ACT.Copy).then_inc(evaced.sem, 1)

            def move_ot(pair, half, g):
                act.wait_ge(pved.sem, pved.at(pair, half, GH * (g + 1)))
                if g == 0:
                    act.wait_ge(misc_full.sem, misc_full.at(pair, half, E_OT1 + 1))
                act.activation(OT[:, g, :], psO[:, :], ACT.Copy).then_inc(otmoved.sem, 1)

            def copy(dst, src, full, scale=1.0):
                act.wait_ge(misc_full.sem, full)
                act.activation(dst, src, ACT.Copy, scale=scale).then_inc(misc_free.sem, 1)

            def prepare(use, p, full):
                if use == P_XNT:
                    copy(xnT[:, :], psM[:, 0:T], full)
                elif use == P_Q:
                    copy(qT[:, :], psM[:, T:512], full, SCALE)
                elif use == P_K1:
                    copy(kT[:, p, 0, :], psM[:, 0:T], full)
                elif use == P_K2:
                    copy(kT[:, p, 1, :], psM[:, T:512], full)
                elif use == P_V:
                    copy(vp[:, p, :, :, 0:HD],
                         psM[:, 0:T].rearrange("p (t h e) -> p t h e", t=QT, e=HD), full)

            act.wait_ge(zeroed, 6)
            for signal, n in ((exped, 2), (mixed, 2), (turned, 2), (evaced, 2), (pved, 1)):
                act.sem_inc(signal.sem, n)
            for n, use in enumerate((P_XNT, P_Q, P_K1, P_K2, P_V)):
                prepare(use, 0, misc_full.early(n + 1))
            exps(0, 0, 0)
            with act.Fori(0, LAST) as pair:
                for half in range(2):
                    p = (half + 1) % 2
                    for s in range(H):
                        exps(pair, half + (s + 1) // H, (s + 1) % H)
                        if s == 0:
                            move_ot(pair, half - 1, H // GH - 1)
                        evac_d(pair, half, s)
                        if s in (4, 8, 12):
                            move_ot(pair, half, s // 4 - 1)
                        if s == 6:
                            copy(OnT[:, :], psM[:, 0:T], misc_full.at(pair, half, E_ONT + 1))
                        if s == 8:
                            act.wait_ge(added.sem, added.at(pair, half, 0))
                            copy(y[:, :, :], psM[:, T:512].rearrange("p (t n) -> p t n", t=QT),
                                 misc_full.at(pair, half, E_Y + 1))
                        if 9 <= s <= 13:
                            use = P_XNT + s - 9
                            if use == P_Q:
                                act.wait_ge(qm_ready.sem, qm_ready.at(pair, half + 1, 0))
                            if use == P_K1:
                                act.wait_ge(scored.sem, scored.at(pair, half, 0))
                            if use == P_V:
                                act.wait_ge(pved.sem, pved.at(pair, half, 0))
                            prepare(use, p, misc_full.at(pair, half, use + 1))
            move_ot(LAST, -1, H // GH - 1)
            copy(OnT[:, :], psM[:, 0:T], misc_full.at(LAST, 0, E_ONT + 1))
            act.wait_ge(added.sem, added.at(LAST, 0, 0))
            copy(y[:, :, :], psM[:, T:512].rearrange("p (t n) -> p t n", t=QT), misc_full.at(LAST, 0, E_Y + 1))

        @block.tensor
        def _(pe):
            def scores(pair, half, h):
                s, p = h % 2, half % 2
                pe.wait_ge(exped.sem, exped.at(pair, half, h - 1))
                pe.wait_ge(qm_ready.sem, qm_ready.at(pair, half, h + 1))
                for m in range(2):
                    out = psS[:, s, m, :]
                    pe.matmul(out[:, 0:P], qm[:, p, h, 0:P], kT[:, p, m, 0:P], start=True, stop=False)
                    pe.matmul(out[:, 0:P], identb[:, :], causal[:, :], start=False, stop=True)
                    pe.matmul(out[:, P:384], qm[:, p, h, P:T], kT[:, p, m, 0:T], start=True, stop=False)
                    ins = pe.matmul(out[:, T:384], identb[:, :], causal[:, :], start=False, stop=True)
                ins.then_inc(scored.sem, 1)

            def turn(pair, half, h):
                s = h % 2
                pe.wait_ge(mixed.sem, mixed.at(pair, half, h + 1))
                pe.wait_ge(evaced.sem, evaced.at(pair, half, h - 1))
                for c in range(3):
                    ins = pe.transpose(psT[:, s, c * P:(c + 1) * P], d[:, s, c * P:(c + 1) * P], ident[:, :])
                ins.then_inc(turned.sem, 1)

            def outputs(pair, half, h):
                s, p, g, j = h % 2, half % 2, h // GH, h % GH
                pe.wait_ge(evaced.sem, evaced.at(pair, half, h + 1))
                if j == 0:
                    pe.wait_ge(otmoved.sem, otmoved.at(pair, half, g))
                out = psO[32 * j:32 * j + 32, :]
                pe.matmul(out[:, 0:P], vp[:, p, 0, h, :], dT[:, s, 0:P], start=True, stop=True)
                pe.matmul(out[:, P:T], vp[:, p, 0, h, :], dT[:, s, P:T], start=True, stop=False)
                pe.matmul(out[:, P:T], vp[:, p, 1, h, :], dT[:, s, T:384], start=False, stop=True)\
                  .then_inc(pved.sem, 1)

            def use_misc(use, p, free):
                pe.wait_ge(misc_free.sem, free)
                lo, hi = psM[:, 0:T], psM[:, T:512]
                if use in (E_OT0, E_OT1):
                    t = use - E_OT0
                    for g in range(H // GH):
                        ins = pe.transpose(psM[:, g * P:(g + 1) * P], OT[:, g, t * P:(t + 1) * P], ident[:, :])
                elif use == E_ONT:
                    for t in range(QT):
                        ins = pe.transpose(lo[:, t * P:(t + 1) * P], On[:, t, :], ident[:, :])
                elif use == E_Y:
                    for t in range(QT):
                        ins = pe.matmul(hi[:, t * P:(t + 1) * P], OnT[:, t * P:(t + 1) * P], wo[:, :],
                                        start=True, stop=True)
                elif use == P_XNT:
                    for t in range(QT):
                        ins = pe.transpose(lo[:, t * P:(t + 1) * P], xn[:, t, :], ident[:, :])
                elif use == P_Q:
                    ins = pe.matmul(hi, wq[:, :], xnT[:, :], start=True, stop=True)
                elif use == P_K1:
                    ins = pe.matmul(lo, wk1[:, :], xnT[:, :], start=True, stop=True)
                elif use == P_K2:
                    ins = pe.matmul(hi, wk2[:, :], xnT[:, :], start=True, stop=True)
                else:
                    for t in range(QT):
                        ins = pe.matmul(lo[:, t * P:(t + 1) * P], xnT[:, t * P:(t + 1) * P], wv[:, :],
                                        start=True, stop=True)
                ins.then_inc(misc_full.sem, 1)

            pe.wait_ge(zeroed, 6)
            pe.wait_ge(xn_ready.sem, xn_ready.early(1))
            for n, use in enumerate((P_XNT, P_Q, P_K1, P_K2, P_V)):
                use_misc(use, 0, misc_free.early(n))
            pe.wait_ge(misc_free.sem, misc_free.early(PRE))
            scores(0, 0, 0)
            scores(0, 0, 1)
            SCHEDULE = {1: E_OT0, 3: E_OT1, 5: E_ONT, 7: E_Y, 8: P_XNT, 9: P_Q, 10: P_K1, 11: P_K2, 12: P_V}
            with pe.Fori(0, LAST) as pair:
                for half in range(2):
                    for s in range(H):
                        if s == H - 2:
                            pe.wait_ge(misc_free.sem, misc_free.at(pair, half, USES))
                        scores(pair, half + (s + 2) // H, (s + 2) % H)
                        turn(pair, half, s)
                        outputs(pair, half - 1 if s == 0 else half, (s - 1) % H)
                        if s in SCHEDULE:
                            use = SCHEDULE[s]
                            if use == E_OT0:
                                pe.wait_ge(otmoved.sem, otmoved.at(pair, half, 0))
                            if use == P_XNT:
                                pe.wait_ge(xn_ready.sem, xn_ready.at(pair, half, 1))
                            use_misc(use, half, misc_free.at(pair, half, use))
            outputs(LAST, -1, H - 1)
            pe.wait_ge(otmoved.sem, otmoved.at(LAST, 0, 0))
            for use in (E_OT0, E_OT1, E_ONT, E_Y):
                use_misc(use, 0, misc_free.at(LAST, 0, use))


def normalise_all(nc, name, src, dst, minus_half):
    G = 8
    with ExitStack() as ctx:
        sem = lambda n: nc.alloc_semaphore(name + n)
        st = ctx.enter_context(nc.sbuf_tensor(name + "st", [P, G, 6], FP32))
        mv = ctx.enter_context(nc.sbuf_tensor(name + "mv", [P, G, 2], FP32))
        rs = ctx.enter_context(nc.sbuf_tensor(name + "rs", [P, G], FP32))
        stats, var_ready, rs_ready = sem("stats"), sem("var_ready"), sem("rs_ready")
        block = ctx.enter_context(nc.Block())

        @block.gpsimd
        def _(pool):
            with pool.Fori(0, TILES // G) as g:
                pool.wait_ge(var_ready, g + 1)
                pool.tensor_tensor(rs[:, :], mv[:, :, 1], minus_half[:, 0:G], ALU.pow).then_inc(rs_ready, 1)

        @block.vector
        def _(dve):
            with dve.Fori(0, TILES // G) as g:
                tiles = lambda a, t: a[:, bass.ds(g * G + (QT + t), 1), :]
                for t in range(G):
                    ins = dve.bn_stats(st[:, t, :], tiles(src, t)[:, 0, :])
                ins.then_inc(stats, 1)
                dve.wait_ge(stats, g * 2 + 1)
                apart(dve, APART["dve"])
                for t in range(G):
                    ins = dve.bn_aggr(mv[:, t, :], st[:, t, :])
                ins.then_inc(stats, 1)
                dve.wait_ge(stats, g * 2 + 2)
                dve.tensor_scalar(mv[:, :, 1], mv[:, :, 1], EPS_LN, None, ALU.add).then_inc(var_ready, 1)
                dve.wait_ge(rs_ready, g + 1)
                for t in range(G):
                    dve.tensor_scalar(tiles(dst, t)[:, 0, :], tiles(src, t)[:, 0, :], mv[:, t, 0:1], rs[:, t:t + 1],
                                      ALU.subtract, ALU.mult)


def add_normalised(nc, name, X, src, minus_half):
    G = 8
    with ExitStack() as ctx:
        sem = lambda n: nc.alloc_semaphore(name + n)
        st = ctx.enter_context(nc.sbuf_tensor(name + "st", [P, G, 6], FP32))
        mv = ctx.enter_context(nc.sbuf_tensor(name + "mv", [P, G, 2], FP32))
        rs = ctx.enter_context(nc.sbuf_tensor(name + "rs", [P, G], FP32))
        yn = ctx.enter_context(nc.sbuf_tensor(name + "yn", [P, G, D], FP32))
        stats, var_ready, rs_ready, scaled = sem("stats"), sem("var_ready"), sem("rs_ready"), sem("scaled")
        block = ctx.enter_context(nc.Block())

        @block.gpsimd
        def _(pool):
            with pool.Fori(0, TILES // G) as g:
                pool.wait_ge(var_ready, g + 1)
                pool.tensor_tensor(rs[:, :], mv[:, :, 1], minus_half[:, 0:G], ALU.pow).then_inc(rs_ready, 1)

        @block.vector
        def _(dve):
            with dve.Fori(0, TILES // G) as g:
                for t in range(G):
                    ins = dve.bn_stats(st[:, t, :], src[:, bass.ds(g * G + (QT + t), 1), :][:, 0, :])
                ins.then_inc(stats, 1)
                dve.wait_ge(stats, g * 2 + 1)
                apart(dve, APART["dve"])
                for t in range(G):
                    ins = dve.bn_aggr(mv[:, t, :], st[:, t, :])
                ins.then_inc(stats, 1)
                dve.wait_ge(stats, g * 2 + 2)
                dve.tensor_scalar(mv[:, :, 1], mv[:, :, 1], EPS_LN, None, ALU.add).then_inc(var_ready, 1)
                dve.wait_ge(rs_ready, g + 1)
                for t in range(G):
                    ins = dve.tensor_scalar(yn[:, t, :], src[:, bass.ds(g * G + (QT + t), 1), :][:, 0, :],
                                            mv[:, t, 0:1], rs[:, t:t + 1], ALU.subtract, ALU.mult)
                ins.then_inc(scaled, 1)
                dve.wait_ge(scaled, g + 1)
                xs = X[:, bass.ds(g * G + QT, G), :]
                dve.tensor_tensor(xs, xs, yn[:, :, :], ALU.add)


def window_attention(nc, name, F, consts, w):
    H, HD = 8, 64
    GH = 2
    NP = H // GH
    W = H * HD
    ident, identb, behind = (consts[k] for k in ("ident", "identb", "behind"))
    minus_half = consts["minus_half"]
    wqk, wv, wo = w["wqk"], w["wv"], w["wo"]
    cos, sin = w["cos"], w["sin"]

    with ExitStack() as ctx:
        sb = lambda n, shape, dt=FP32: ctx.enter_context(nc.sbuf_tensor(name + n, shape, dt))
        ps = lambda n, shape: ctx.enter_context(nc.psum_tensor(name + n, shape, FP32))
        sem = lambda n: nc.alloc_semaphore(name + n)

        staged = sb("staged", [P, QT, D])
        hT = sb("hT", [P, T])
        sq = sb("sq", [P, 2 * W])
        ss = sb("ss", [P, QT, 2 * H])
        rn = sb("rn", [P, QT, 2 * H])
        part = sb("part", [P, 2, 2 * W])
        rot = sb("rot", [P, 2 * W])
        qk = sb("qk", [P, QT, 2 * W])
        qm = sb("qm", [P, 2, H, T])
        kT = sb("kT", [P, 2, NP, T])
        v = sb("v", [P, 2, QT, W])
        nm = sb("nm", [P, 2, 2])
        Z = sb("Z", [P, 2, 2])
        rz = sb("rz", [P, 2, 2])
        E = sb("E", [P, 2, 384])
        d = sb("d", [P, 2, 384])
        dT = sb("dT", [P, 2, 384])
        OT = sb("OT", [P, NP, T])

        psQ = ps("psQ", [P, 2 * W])
        psS = ps("psS", [P, 2, 512])
        psT = ps("psT", [P, 2, 512])
        psO = ps("psO", [P, T])
        psM = ps("psM", [P, 512])

        U_HT, U_WO, U_V0, U_V1, U_TQ0, U_TK0, U_TQ1, U_TK1 = range(8)
        USES, PRE = 8, 7
        PEELED = (U_HT, U_V0, U_V1, U_TQ0, U_TK0, U_TQ1, U_TK1)
        misc_full = Signal(sem("misc_full"), USES, PRE)
        misc_free = Signal(sem("misc_free"), USES, PRE)
        qk_full = Signal(sem("qk_full"), QT, QT)
        squared = Signal(sem("squared"), QT, QT)
        ss_ready = Signal(sem("ss_ready"), QT, QT)
        rn_ready = Signal(sem("rn_ready"), QT, QT)
        parts = Signal(sem("parts"), QT, QT)
        summed = Signal(sem("summed"), QT, QT)
        qk_ready = Signal(sem("qk_ready"), QT, QT)
        scored = Signal(sem("scored"), H)
        maxed = Signal(sem("maxed"), H)
        exped = Signal(sem("exped"), H, 2)
        mixed = Signal(sem("mixed"), H, 2)
        turned = Signal(sem("turned"), H, 2)
        evaced = Signal(sem("evaced"), H, 2)
        pved = Signal(sem("pved"), H, 2)
        otmoved = Signal(sem("otmoved"), NP, 1)
        stage_full = Signal(sem("stage_full"), 1, 1)
        zeroed = sem("zeroed")
        own = Chain(sem("own"), CHAIN_B, 2)

        block = ctx.enter_context(nc.Block())
        LAST = BATCH // 2

        def f_of(pair, half):
            return F[:, bass.ds((pair * 2 + (half + 1)) * QT, QT), :]

        @block.sync
        def _(sp):
            open_signals(sp)

        @block.gpsimd
        def _(pool):
            for tile in (qm, OT, dT, hT, v):
                pool.memset(tile[:], 0.0).then_inc(zeroed, 1)

            def norms_and_sum(pair, half, t):
                pool.wait_ge(ss_ready.sem, ss_ready.at(pair, half, t + 1))
                pool.tensor_tensor(rn[:, t, :], ss[:, t, :], minus_half[:, 0:2 * H], ALU.pow).then_inc(rn_ready.sem, 1)
                pool.wait_ge(parts.sem, parts.at(pair, half, t + 1))
                pool.wait_ge(qk_ready.sem, qk_ready.at(pair, half, t))
                pool.tensor_tensor(rot[:, :], part[:, 0, :], part[:, 1, :], ALU.add).then_inc(summed.sem, 1)

            pool.tensor_copy(staged[:, :, :], f_of(0, 0)).then_inc(stage_full.sem, 1)
            for t in range(QT):
                norms_and_sum(0, -1, t)
            with pool.Fori(0, LAST) as pair:
                for half in range(2):
                    pool.wait_ge(misc_full.sem, misc_full.at(pair, half - 1, U_V0 + 1))
                    pool.tensor_copy(staged[:, :, :], f_of(pair, half + 1)).then_inc(stage_full.sem, 1)
                    for t in range(QT):
                        norms_and_sum(pair, half, t)

        @block.vector
        def _(dve):
            def rotate(pair, half, t):
                dve.wait_ge(squared.sem, squared.at(pair, half, t + 1))
                own.mark(dve.tensor_reduce(ss[:, t, :], sq[:, :].rearrange("p (h e) -> p h e", e=HD),
                                           axis=AX.X, op=ALU.add))
                dve.wait_ge(summed.sem, summed.at(pair, half, t))
                src = psQ[:, :].rearrange("p (a h e) -> p a h e", a=2, e=HD)
                out = part[:, :, :].rearrange("p b (a h e) -> p b a h e", a=2, e=HD)
                tab = lambda a, lo, n: a[:, t, :, lo:lo + n].unsqueeze(2).broadcast_to([P, 2, H, n])
                dve.tensor_tensor(out[:, 0], src, tab(cos, 0, HD), ALU.mult)
                own.last()
                dve.tensor_scalar(ss[:, t, :], ss[:, t, :], 1e-24, None, ALU.max).then_inc(ss_ready.sem, 1)
                R = HD // 2
                dve.tensor_tensor(out[:, 1, :, :, 0:R], src[:, :, :, R:HD], tab(sin, 0, R), ALU.mult)
                dve.tensor_tensor(out[:, 1, :, :, R:HD], src[:, :, :, 0:R], tab(sin, R, R), ALU.mult)\
                   .then_inc(parts.sem, 1)

            def scale(pair, half, t, used):
                dve.wait_ge(summed.sem, summed.at(pair, half, t + 1))
                dve.wait_ge(rn_ready.sem, rn_ready.at(pair, half, t + 1))
                if used is not None:
                    dve.wait_ge(misc_full.sem, used)
                dve.tensor_tensor(qk[:, t, :].rearrange("p (h e) -> p h e", e=HD),
                                  rot[:, :].rearrange("p (h e) -> p h e", e=HD),
                                  rn[:, t, :].unsqueeze(2).broadcast_to([P, 2 * H, HD]), ALU.mult)\
                   .then_inc(qk_ready.sem, 1)

            def maxima(pair, half, h):
                s = h % 2
                dve.wait_ge(scored.sem, scored.at(pair, half, h + 1))
                dve.tensor_reduce(nm[:, s, 0:1], psS[:, s, 0:P], axis=AX.X, op=ALU.max, negate=True)
                dve.tensor_reduce(nm[:, s, 1:2], psS[:, s, P:384], axis=AX.X, op=ALU.max, negate=True)\
                   .then_inc(maxed.sem, 1)

            def inverse(pair, half, h):
                s = h % 2
                dve.wait_ge(exped.sem, exped.at(pair, half, h + 1))
                return own.mark(dve.reciprocal(rz[:, s, :], Z[:, s, :]))

            def normalise(pair, half, h, k):
                s = h % 2
                dve.wait_ge(turned.sem, turned.at(pair, half, h - 1))
                own.wait(k)
                dve.tensor_scalar(d[:, s, 0:P], E[:, s, 0:P], rz[:, s, 0:1], None, ALU.mult)
                dve.tensor_scalar(d[:, s, P:384], E[:, s, P:384], rz[:, s, 1:2], None, ALU.mult)\
                   .then_inc(mixed.sem, 1)

            def residual(pair, half, full):
                dve.wait_ge(misc_full.sem, full)
                fs = f_of(pair, half - 1)
                dve.tensor_tensor(fs, psM[:, 0:T].rearrange("p (t n) -> p t n", t=QT), fs, ALU.add)\
                   .then_inc(misc_free.sem, 1)

            dve.memset(psO[:, :], 0.0).then_inc(zeroed, 1)
            dve.wait_ge(zeroed, 6)
            own.begin(dve, 0, 0)
            own.restart(0)
            for t in range(QT):
                rotate(0, -1, t)
                scale(0, -1, t, None)
            assert own.k == 2
            own.restart(own.k)
            maxima(0, 0, 0)
            with dve.Fori(0, LAST) as pair:
                for half in range(2):
                    own.begin(dve, pair, half)
                    for s in range(H):
                        k = inverse(pair, half, s)
                        maxima(pair, half + (s + 1) // H, (s + 1) % H) if s < H - 1 else None
                        normalise(pair, half, s, k)
                        if s == 2:
                            residual(pair, half, misc_full.at(pair, half, U_WO + 1))
                            rotate(pair, half, 0)
                        if s == 3:
                            rotate(pair, half, 1)
                        if s == 4:
                            scale(pair, half, 0, misc_full.at(pair, half - 1, U_TK0 + 1))
                        if s == 6:
                            scale(pair, half, 1, misc_full.at(pair, half - 1, U_TK1 + 1))
                        if s == H - 1:
                            maxima(pair, half + 1, 0)
                    own.end()
            residual(LAST, 0, misc_full.at(LAST, 0, 1))

        @block.scalar
        def _(act):
            def exps(pair, half, h):
                s = h % 2
                act.wait_ge(maxed.sem, maxed.at(pair, half, h + 1))
                act.wait_ge(mixed.sem, mixed.at(pair, half, h - 1))
                act.activation(E[:, s, 0:P], psS[:, s, 0:P], ACT.Exp, bias=nm[:, s, 0:1], accum_out=Z[:, s, 0:1])
                act.activation(E[:, s, P:384], psS[:, s, P:384], ACT.Exp, bias=nm[:, s, 1:2],
                               accum_out=Z[:, s, 1:2]).then_inc(exped.sem, 1)

            def evac_d(pair, half, h):
                s = h % 2
                act.wait_ge(turned.sem, turned.at(pair, half, h + 1))
                act.wait_ge(pved.sem, pved.at(pair, half, h - 1))
                act.activation(dT[:, s, :], psT[:, s, 0:384], ACT.Copy).then_inc(evaced.sem, 1)

            def move_ot(pair, half, g):
                act.wait_ge(pved.sem, pved.at(pair, half, GH * (g + 1)))
                if g == 0:
                    act.wait_ge(misc_full.sem, misc_full.at(pair, half, U_WO + 1))
                act.activation(OT[:, g, :], psO[:, :], ACT.Copy).then_inc(otmoved.sem, 1)

            def square(pair, half, t):
                act.wait_ge(qk_full.sem, qk_full.at(pair, half, t + 1))
                act.wait_ge(ss_ready.sem, ss_ready.at(pair, half, t))
                act.activation(sq[:, :], psQ[:, :], ACT.Square).then_inc(squared.sem, 1)

            def use_copy(use, p, full):
                act.wait_ge(misc_full.sem, full)
                if use == U_HT:
                    act.activation(hT[0:64, :], psM[0:64, 0:T], ACT.Copy)
                    ins = act.activation(hT[64:P, 1:T], psM[64:P, 0:T - 1], ACT.Copy)
                elif use in (U_V0, U_V1):
                    ins = act.activation(v[:, p, use - U_V0, :], psM[:, :], ACT.Copy)
                elif use in (U_TQ0, U_TQ1):
                    c = (use - U_TQ0) // 2 * P
                    src = psM[:, :].rearrange("p (n t) -> p n t", t=P)
                    for r in range(2):
                        rows = slice(64 * r, 64 * r + 64)
                        ins = act.activation(qm[rows, p, r::2, c:c + P], src[rows], ACT.Copy)
                else:
                    c = (use - U_TK0) // 2 * P
                    ins = act.activation(kT[:, p, :, c:c + P], psM[:, :].rearrange("p (n t) -> p n t", t=P), ACT.Copy)
                ins.then_inc(misc_free.sem, 1)

            act.wait_ge(zeroed, 6)
            for signal, n in ((exped, 2), (mixed, 2), (turned, 2), (evaced, 2), (pved, 1)):
                act.sem_inc(signal.sem, n)
            use_copy(U_HT, 0, misc_full.early(1))
            use_copy(U_V0, 0, misc_full.early(2))
            square(0, -1, 0)
            use_copy(U_V1, 0, misc_full.early(3))
            square(0, -1, 1)
            for n in range(4):
                use_copy(U_TQ0 + n, 0, misc_full.early(4 + n))
            exps(0, 0, 0)
            with act.Fori(0, LAST) as pair:
                for half in range(2):
                    p = (half + 1) % 2
                    copy = lambda use: use_copy(use, p, misc_full.at(pair, half, use + 1))
                    for s in range(H):
                        if s < H - 1:
                            exps(pair, half, s + 1)
                        if s == 0:
                            move_ot(pair, half - 1, NP - 1)
                        if s == 6:
                            copy(U_TQ1)
                            copy(U_TK1)
                        evac_d(pair, half, s)
                        if s in (2, 4, 6):
                            move_ot(pair, half, s // 2 - 1)
                        if s == 0:
                            copy(U_HT)
                        if s == 1:
                            square(pair, half, 0)
                        if s == 3:
                            square(pair, half, 1)
                            act.wait_ge(pved.sem, pved.at(pair, half, 0))
                            copy(U_V0)
                        if s == 4:
                            copy(U_V1)
                        if s == 5:
                            act.wait_ge(scored.sem, scored.at(pair, half, 0))
                            copy(U_TQ0)
                            copy(U_TK0)
                        if s == H - 1:
                            exps(pair, half + 1, 0)
            move_ot(LAST, -1, NP - 1)

        @block.tensor
        def _(pe):
            def scores(pair, half, h):
                s, p = h % 2, half % 2
                pe.wait_ge(exped.sem, exped.at(pair, half, h - 1))
                out = psS[:, s, :]
                key = kT[:, p, h // 2, :]
                pe.matmul(out[:, 0:P], qm[:, p, h, 0:P], key[:, 0:P], start=True, stop=False)
                pe.matmul(out[:, 0:P], identb[:, :], behind[:, P:T], start=False, stop=True)
                pe.matmul(out[:, P:384], qm[:, p, h, P:T], key, start=True, stop=False)
                pe.matmul(out[:, P:384], identb[:, :], behind[:, :], start=False, stop=True).then_inc(scored.sem, 1)

            def turn(pair, half, h):
                s = h % 2
                pe.wait_ge(mixed.sem, mixed.at(pair, half, h + 1))
                pe.wait_ge(evaced.sem, evaced.at(pair, half, h - 1))
                for c in range(3):
                    ins = pe.transpose(psT[:, s, c * P:(c + 1) * P], d[:, s, c * P:(c + 1) * P], ident[:, :])
                ins.then_inc(turned.sem, 1)

            def outputs(pair, half, h):
                s, p, j = h % 2, half % 2, h % 2
                pe.wait_ge(evaced.sem, evaced.at(pair, half, h + 1))
                if j == 0:
                    pe.wait_ge(otmoved.sem, otmoved.at(pair, half, h // 2))
                out = psO[64 * j:64 * j + 64, :]
                vh = lambda t: v[:, p, t, h * HD:(h + 1) * HD]
                pe.matmul(out[:, 0:P], vh(0), dT[:, s, 0:P], start=True, stop=True)
                pe.matmul(out[:, P:T], vh(0), dT[:, s, P:T], start=True, stop=False)
                pe.matmul(out[:, P:T], vh(1), dT[:, s, T:384], start=False, stop=True).then_inc(pved.sem, 1)

            def project(pair, half, t):
                pe.wait_ge(parts.sem, parts.at(pair, half, t))
                for n in range(2):
                    ins = pe.matmul(psQ[:, n * W:(n + 1) * W], hT[:, t * P:(t + 1) * P], wqk[:, n * W:(n + 1) * W],
                                    start=True, stop=True)
                ins.then_inc(qk_full.sem, 1)

            def use_misc(use, free, fs=None):
                pe.wait_ge(misc_free.sem, free)
                if use == U_HT:
                    for t in range(QT):
                        ins = pe.transpose(psM[:, t * P:(t + 1) * P], fs[:, t, :], ident[:, :])
                elif use == U_WO:
                    for t in range(QT):
                        for n in range(NP):
                            ins = pe.matmul(psM[:, t * P:(t + 1) * P], OT[:, n, t * P:(t + 1) * P], wo[:, n, :],
                                            start=(n == 0), stop=(n == NP - 1))
                elif use in (U_V0, U_V1):
                    t = use - U_V0
                    ins = pe.matmul(psM[:, :], hT[:, t * P:(t + 1) * P], wv[:, :], start=True, stop=True)
                else:
                    t, a = divmod(use - U_TQ0, 2)
                    for n in range(NP):
                        ins = pe.transpose(psM[:, n * P:(n + 1) * P],
                                           qk[:, t, a * W + n * P:a * W + (n + 1) * P], ident[:, :])
                ins.then_inc(misc_full.sem, 1)
            pe.wait_ge(zeroed, 6)
            pe.wait_ge(stage_full.sem, stage_full.early(1))
            use_misc(U_HT, misc_free.early(0), staged)
            pe.wait_ge(misc_free.sem, misc_free.early(1))
            project(0, -1, 0)
            use_misc(U_V0, misc_free.early(1))
            project(0, -1, 1)
            use_misc(U_V1, misc_free.early(2))
            for n in range(4):
                pe.wait_ge(qk_ready.sem, qk_ready.early(n // 2 + 1))
                use_misc(U_TQ0 + n, misc_free.early(3 + n))
            pe.wait_ge(misc_free.sem, misc_free.early(PRE))
            scores(0, 0, 0)
            scores(0, 0, 1)
            with pe.Fori(0, LAST) as pair:
                for half in range(2):
                    use = lambda u, fs=None: use_misc(u, misc_free.at(pair, half, u), fs)
                    for s in range(H):
                        if s == H - 2:
                            pe.wait_ge(qk_ready.sem, qk_ready.at(pair, half, 2))
                            use(U_TQ1)
                            use(U_TK1)
                            pe.wait_ge(misc_free.sem, misc_free.at(pair, half, USES))
                        scores(pair, half + (s + 2) // H, (s + 2) % H)
                        turn(pair, half, s)
                        outputs(pair, half - 1 if s == 0 else half, (s - 1) % H)
                        if s == 0:
                            pe.wait_ge(stage_full.sem, stage_full.at(pair, half, 1))
                            use(U_HT, staged)
                        if s == 1:
                            pe.wait_ge(otmoved.sem, otmoved.at(pair, half, 0))
                            use(U_WO)
                            project(pair, half, 0)
                        if s == 2:
                            project(pair, half, 1)
                        if s == 3:
                            use(U_V0)
                        if s == 4:
                            use(U_V1)
                        if s == 5:
                            pe.wait_ge(qk_ready.sem, qk_ready.at(pair, half, 1))
                            use(U_TQ0)
                            use(U_TK0)
            outputs(LAST, -1, H - 1)
            pe.wait_ge(otmoved.sem, otmoved.at(LAST, 0, 0))
            use_misc(U_WO, misc_free.at(LAST, 0, 0))


def feed_forward(nc, name, F, consts, w):
    NT = 4
    N = NT * P
    PAIRS = TILES // NT // 2
    HID = 341
    parts = [(j, min(P, HID - P * j)) for j in range((HID + P - 1) // P)]
    J = len(parts)
    ident, minus_half = consts["ident"], consts["minus_half"]
    w1, b1, w2, b2, lg, lb = (w[k] for k in ("w1", "b1", "w2", "b2", "ln_g", "ln_b"))

    with ExitStack() as ctx:
        sb = lambda n, shape, dt=FP32: ctx.enter_context(nc.sbuf_tensor(name + n, shape, dt))
        ps = lambda n, shape: ctx.enter_context(nc.psum_tensor(name + n, shape, FP32))
        sem = lambda n: nc.alloc_semaphore(name + n)
        z = sb("z", [P, 2, NT, D])
        st = sb("st", [P, NT, 6])
        mv = sb("mv", [P, NT, 2])
        rs = sb("rs", [P, NT])
        xn = sb("xn", [P, NT, D])
        hT = sb("hT", [P, N])
        gg = sb("gg", [P, J, N])
        u = sb("u", [P, J, N])
        fb = sb("fb", [P, NT, D])
        psG = ps("psG", [P, J, N])
        psA = ps("psA", [P, J, N])
        psX = ps("psX", [P, N])
        psY = ps("psY", [P, N])

        shifted = [sem("shifted"), sem("shifted_odd")]
        g_full = Signal(sem("g_full"), J)
        a_full = Signal(sem("a_full"), J)
        gelued = Signal(sem("gelued"), J)
        gated = Signal(sem("gated"), J)
        var_ready = Signal(sem("var_ready"), 1, 1)
        rs_ready = Signal(sem("rs_ready"), 1, 1)
        xn_ready = Signal(sem("xn_ready"), 1, 1)
        x_full = Signal(sem("x_full"), 1, 1)
        h_ready = Signal(sem("h_ready"), 1, 1)
        y_full = Signal(sem("y_full"), 1)
        added = Signal(sem("added"), 1)
        fb_ready = Signal(sem("fb_ready"), 1)
        zeroed = sem("zeroed")
        own = Chain(sem("own"), CHAIN_F, 2)
        block = ctx.enter_context(nc.Block())

        def f_of(pair, half):
            return F[:, bass.ds((pair * 2 + half) * NT + QT, NT), :]

        def z_landed(eng, pair, half):
            eng.wait_ge(shifted[half % 2], (pair + half // 2) * 48 + 48)

        @block.sync
        def _(sp):
            open_signals(sp)
            def shift(pair, half):
                done = shifted[half % 2]
                p, fs = half % 2, f_of(pair, half)
                sp.dma_start(z[:, p, :, 0:64], fs[:, :, 0:64]).then_inc(done, 16)
                sp.dma_start(z[1:P, p, :, 64:D], fs[0:P - 1, :, 64:D]).then_inc(done, 16)
                sp.dma_start(z[0:1, p, 1::2, 64:D], fs[P - 1:P, 0::2, 64:D]).then_inc(done, 16)

            sp.wait_ge(zeroed, 1)
            shift(0, 0)
            shift(0, 1)
            with sp.Fori(0, PAIRS - 1) as pair:
                for half in range(2):
                    sp.wait_ge(xn_ready.sem, xn_ready.at(pair, half, 0))
                    shift(pair, half + 2)
            sp.wait_ge(xn_ready.sem, xn_ready.at(PAIRS - 1, 0, 0))
            shift(PAIRS - 1, 2)

        @block.gpsimd
        def _(pool):
            pool.memset(z[0:1, :, 0::2, 64:D], 0.0).then_inc(zeroed, 1)

            def rstd(pair, half, k):
                pool.wait_ge(var_ready.sem, var_ready.at(pair, half, k))
                pool.tensor_tensor(rs[:, :], mv[:, :, 1], minus_half[:, 0:NT], ALU.pow).then_inc(rs_ready.sem, 1)

            rstd(0, 0, 0)
            with pool.Fori(0, PAIRS) as pair:
                for half in range(2):
                    rstd(pair, half, 1)
                    pool.wait_ge(added.sem, added.at(pair, half, 0))
                    pool.tensor_tensor(fb[:, :, :], f_of(pair, half), b2[:, :].unsqueeze(1).broadcast_to([P, NT, D]),
                                       ALU.add).then_inc(fb_ready.sem, 1)

        @block.vector
        def _(dve):
            def variance(pair, half):
                z_landed(dve, pair, half)
                for t in range(NT):
                    ins = dve.bn_stats(st[:, t, :], z[:, half % 2, t, :])
                own.mark(ins)
                own.last()
                apart(dve, APART["dve"])
                for t in range(NT):
                    ins = dve.bn_aggr(mv[:, t, :], st[:, t, :])
                own.mark(ins)
                own.last()
                dve.tensor_scalar(mv[:, :, 1], mv[:, :, 1], EPS_LN, None, ALU.add).then_inc(var_ready.sem, 1)

            def normalise(pair, half, k):
                dve.wait_ge(rs_ready.sem, rs_ready.at(pair, half, k))
                if k:
                    dve.wait_ge(x_full.sem, x_full.at(pair, half, 0))
                for t in range(NT):
                    ins = dve.tensor_scalar(xn[:, t, :], z[:, (half + k) % 2, t, :], mv[:, t, 0:1], rs[:, t:t + 1],
                                            ALU.subtract, ALU.mult)
                ins.then_inc(xn_ready.sem, 1)

            own.begin(dve, 0, 0)
            own.restart(0)
            variance(0, 0)
            own.restart(own.k)
            normalise(0, 0, 0)
            with dve.Fori(0, PAIRS) as pair:
                for half in range(2):
                    own.begin(dve, pair, half)
                    variance(pair, half + 1)
                    for j, m in parts:
                        dve.wait_ge(gelued.sem, gelued.at(pair, half, j + 1))
                        dve.wait_ge(a_full.sem, a_full.at(pair, half, j + 1))
                        dve.wait_ge(y_full.sem, y_full.at(pair, half, 0))
                        dve.scalar_tensor_tensor(out=u[0:m, j, :], in0=psA[0:m, j, :], scalar=b1[0:m, j:j + 1],
                                                 in1=gg[0:m, j, :], op0=ALU.add, op1=ALU.mult).then_inc(gated.sem, 1)
                        if j == 0:
                            normalise(pair, half, 1)
                    dve.wait_ge(y_full.sem, y_full.at(pair, half, 1))
                    dve.wait_ge(fb_ready.sem, fb_ready.at(pair, half, 1))
                    dve.tensor_tensor(f_of(pair, half), psY[:, :].rearrange("p (t n) -> p t n", t=NT), fb[:, :, :],
                                      ALU.add).then_inc(added.sem, 1)
                    own.end()

        @block.scalar
        def _(act):
            def take_x(full):
                act.wait_ge(x_full.sem, full)
                act.activation(hT[:, :], psX[:, :], ACT.Identity, scale=lg[:, 0:1], bias=lb[:, 0:1])\
                   .then_inc(h_ready.sem, 1)

            take_x(x_full.early(1))
            with act.Fori(0, PAIRS) as pair:
                for half in range(2):
                    for j, m in parts:
                        act.wait_ge(g_full.sem, g_full.at(pair, half, j + 1))
                        act.wait_ge(gated.sem, gated.at(pair, half, 0))
                        act.activation(gg[0:m, j, :], psG[0:m, j, :], ACT.Gelu, bias=b1[0:m, J + j:J + j + 1])\
                           .then_inc(gelued.sem, 1)
                    take_x(x_full.at(pair, half, 1))

        @block.tensor
        def _(pe):
            def turn_x(full):
                pe.wait_ge(xn_ready.sem, full)
                for t in range(NT):
                    ins = pe.transpose(psX[:, t * P:(t + 1) * P], xn[:, t, :], ident[:, :])
                ins.then_inc(x_full.sem, 1)

            turn_x(xn_ready.early(1))
            with pe.Fori(0, PAIRS) as pair:
                for half in range(2):
                    pe.wait_ge(h_ready.sem, h_ready.at(pair, half, 0))
                    for j, m in parts:
                        pe.wait_ge(gelued.sem, gelued.at(pair, half, 0))
                        pe.matmul(psG[0:m, j, :], w1[:, HID + j * P:HID + j * P + m], hT[:, :], start=True, stop=True)\
                          .then_inc(g_full.sem, 1)
                        pe.wait_ge(gated.sem, gated.at(pair, half, 0))
                        pe.matmul(psA[0:m, j, :], w1[:, j * P:j * P + m], hT[:, :], start=True, stop=True)\
                          .then_inc(a_full.sem, 1)
                    turn_x(xn_ready.at(pair, half, 1))
                    pe.wait_ge(gated.sem, gated.at(pair, half, J))
                    pe.wait_ge(added.sem, added.at(pair, half, 0))
                    for t in range(NT):
                        for j, m in parts:
                            ins = pe.matmul(psY[:, t * P:(t + 1) * P], u[0:m, j, t * P:(t + 1) * P], w2[0:m, j, :],
                                            start=(j == 0), stop=(j == J - 1))
                    ins.then_inc(y_full.sem, 1)


def state_space(nc, X, F, consts, w):
    NS, GROUPS = 32, 4
    SEQ = BATCH // GROUPS
    N = SEQ * T
    LEVELS = T.bit_length() - 1
    ident, minus_half = consts["ident"], consts["minus_half"]
    win, bin_, bm, am, amT, cT, dv = (w[k] for k in ("W_in", "b_in", "Bm", "A", "AT", "C", "D"))

    with ExitStack() as ctx:
        sb = lambda n, shape, dt=FP32: ctx.enter_context(nc.sbuf_tensor("s_" + n, shape, dt))
        ps = lambda n, shape: ctx.enter_context(nc.psum_tensor("s_" + n, shape, FP32))
        sem = lambda n: nc.alloc_semaphore("s_" + n)
        xT = sb("xT", [P, 2, T])
        U = sb("U", [P, N])
        Hs = sb("H", [P, SEQ, T])
        pw = sb("pw", [P, 2, 2, P])
        y = sb("y", [P, QT, D])
        yn = sb("yn", [P, QT, D])
        st = sb("st", [P, QT, 6])
        mv = sb("mv", [P, QT, 2])
        rs = sb("rs", [P, QT])
        psX = ps("psX", [P, 2, 512])
        psU = ps("psU", [P, 2, 512])
        psH = ps("psH", [P, 2, 512])
        psP = ps("psP", [P, 512])
        psY = ps("psY", [P, 512])

        x_full, xT_ready, u_full, u_ready = (
            sem(n) for n in ("x_full", "xT_ready", "u_full", "u_ready"))
        b_full, h_ready, level_full, p_full, p_ready = (
            sem(n) for n in ("b_full", "h_ready", "level_full", "p_full", "p_ready"))
        y_full, y_ready, var_ready, rs_ready = (sem(n) for n in ("y_full", "y_ready", "var_ready", "rs_ready"))
        own = sem("own")
        block = ctx.enter_context(nc.Block())

        def f_of(b):
            return F[:, QT + b * QT:QT + (b + 1) * QT, :]

        @block.gpsimd
        def _(pool):
            for b in range(BATCH):
                pool.wait_ge(var_ready, b + 1)
                pool.tensor_tensor(rs[:, :], mv[:, :, 1], minus_half[:, 0:QT], ALU.pow).then_inc(rs_ready, 1)

        @block.scalar
        def _(act):
            for b in range(BATCH):
                act.wait_ge(x_full, b + 1)
                if b >= 2:
                    act.wait_ge(u_full, b - 1)
                act.activation(xT[:, b % 2, :], psX[:, b % 2, 0:T], ACT.Copy).then_inc(xT_ready, 1)
            for c in range(2):
                act.wait_ge(u_full, BATCH)
                act.activation(U[:, c * 512:(c + 1) * 512], psU[:, c, :], ACT.Identity, bias=bin_[:, 0:1])\
                   .then_inc(u_ready, 1)
            for l in range(LEVELS - 1):
                act.wait_ge(p_full, l + 1)
                if l >= 1:
                    act.wait_ge(level_full, 2 * l)
                act.activation(pw[:, (l + 1) % 2, :, :], psP[:, 0:T].rearrange("p (a n) -> p a n", a=2), ACT.Copy)\
                   .then_inc(p_ready, 1)

        @block.vector
        def _(dve):
            dve.tensor_copy(pw[:, 0, 0, :], am[:, :]).then_inc(p_ready, 1)
            dve.tensor_copy(pw[:, 0, 1, :], amT[:, :]).then_inc(p_ready, 1)
            for c in range(2):
                dve.wait_ge(b_full, c + 1)
                dve.tensor_copy(Hs[:, 2 * c:2 * c + 2, :], psH[:, c, :].rearrange("p (a t) -> p a t", a=2))\
                   .then_inc(h_ready, 1)
            for l in range(LEVELS):
                k = 2 ** l
                for c in range(2):
                    dve.wait_ge(level_full, 2 * l + c + 1)
                    dve.wait_ge(h_ready, 2 * l + c + 1)
                    hs = Hs[:, 2 * c:2 * c + 2, k:T]
                    dve.tensor_tensor(hs, psH[:, c, 0:2 * (T - k)].rearrange("p (a t) -> p a t", a=2), hs, ALU.add)\
                       .then_inc(h_ready, 1)
            marks = 0
            for b in range(BATCH):
                dve.wait_ge(y_full, b + 1)
                for t in range(QT):
                    ins = dve.tensor_tensor(y[:, t, :], psY[:, t * P:(t + 1) * P], dv[:, :], ALU.add)
                ins.then_inc(y_ready, 1)
                dve.wait_ge(y_ready, b + 1)
                for t in range(QT):
                    ins = dve.bn_stats(st[:, t, :], y[:, t, :])
                ins.then_inc(own, 1)
                dve.wait_ge(own, marks + 1)
                for t in range(QT):
                    ins = dve.bn_aggr(mv[:, t, :], st[:, t, :])
                ins.then_inc(own, 1)
                dve.wait_ge(own, marks + 2)
                dve.tensor_scalar(mv[:, :, 1], mv[:, :, 1], EPS_LN, None, ALU.add).then_inc(var_ready, 1)
                dve.wait_ge(rs_ready, b + 1)
                for t in range(QT):
                    ins = dve.tensor_scalar(yn[:, t, :], y[:, t, :], mv[:, t, 0:1], rs[:, t:t + 1],
                                            ALU.subtract, ALU.mult)
                ins.then_inc(own, 1)
                dve.wait_ge(own, marks + 3)
                xs = X[:, QT + b * QT:QT + (b + 1) * QT, :]
                dve.tensor_tensor(xs, xs, yn[:, :, :], ALU.add)
                marks += 3

        @block.tensor
        def _(pe):
            def inputs(b):
                g, j = divmod(b, SEQ)
                pe.wait_ge(xT_ready, b + 1)
                pe.matmul(psU[NS * g:NS * g + NS, j // 2, (j % 2) * T:(j % 2) * T + T], win[:, :], xT[:, b % 2, :],
                          start=True, stop=True).then_inc(u_full, 1)

            for b in range(BATCH):
                if b >= 2:
                    pe.wait_ge(xT_ready, b - 1)
                for t in range(QT):
                    ins = pe.transpose(psX[:, b % 2, t * P:(t + 1) * P], f_of(b)[:, t, :], ident[:, :])
                ins.then_inc(x_full, 1)
                if b >= 1:
                    inputs(b - 1)
            inputs(BATCH - 1)
            for c in range(2):
                pe.wait_ge(u_ready, c + 1)
                pe.matmul(psH[:, c, :], bm[:, :], U[:, c * 512:(c + 1) * 512], start=True, stop=True).then_inc(b_full, 1)
            pe.wait_ge(p_ready, 2)
            for l in range(LEVELS):
                k = 2 ** l
                if l:
                    pe.wait_ge(p_ready, 2 + l)
                a, aT = pw[:, l % 2, 0, :], pw[:, l % 2, 1, :]
                for c in range(2):
                    pe.wait_ge(h_ready, 2 * l + c + 1)
                    pe.matmul(psH[:, c, 0:2 * (T - k)], a, Hs[:, 2 * c:2 * c + 2, 0:T - k], start=True, stop=True)\
                      .then_inc(level_full, 1)
                    if c == 0 and l < LEVELS - 1:
                        pe.matmul(psP[:, 0:P], aT, a, start=True, stop=True)
                        pe.matmul(psP[:, P:T], a, aT, start=True, stop=True).then_inc(p_full, 1)
            pe.wait_ge(h_ready, 2 * LEVELS + 2)
            for b in range(BATCH):
                g, j = divmod(b, SEQ)
                if b:
                    pe.wait_ge(y_ready, b)
                for t in range(QT):
                    rows = slice(NS * g, NS * g + NS)
                    ins = pe.matmul(psY[:, t * P:(t + 1) * P], Hs[rows, j, t * P:(t + 1) * P], cT[rows, :],
                                    start=True, stop=True)
                ins.then_inc(y_full, 1)


def mixture_of_experts(nc, X, F, out, consts, w):
    NT = 4
    N = NT * P
    PAIRS = TILES // NT // 2
    NE, HID = 8, 256
    J = HID // P
    ident, minus_half, eid = consts["ident"], consts["minus_half"], consts["expert_id"]
    wr, wg, wu, wd = w["router"], w["gate"], w["up"], w["down"]

    with ExitStack() as ctx:
        sb = lambda n, shape, dt=FP32: ctx.enter_context(nc.sbuf_tensor("mx_" + n, shape, dt))
        ps = lambda n, shape: ctx.enter_context(nc.psum_tensor("mx_" + n, shape, FP32))
        sem = lambda n: nc.alloc_semaphore("mx_" + n)
        staged = sb("staged", [P, NT, D])
        hT = sb("hT", [P, 2, N])
        lo = sb("lo", [P, NT, NE])
        top = sb("top", [P, NT, 8])
        idx = sb("idx", [P, NT, 8], mybir.dt.uint32)
        idf = sb("idf", [P, NT, 2])
        sg = sb("sg", [P, NT, 2])
        gs = sb("gs", [P, NT])
        gate = sb("gate", [P, 2, NT, NE])
        pick = sb("pick", [P, NT, NE])
        sl = sb("sl", [P, 2, J, N])
        h = sb("h", [P, 2, J, N])
        Y = sb("Y", [P, NT, D])
        yn = sb("yn", [P, NT, D])
        res = sb("res", [P, 2, NT, D])
        st = sb("st", [P, NT, 6])
        mv = sb("mv", [P, NT, 2])
        rs = sb("rs", [P, NT])
        psG = ps("psG", [P, J, N])
        psU = ps("psU", [P, J, N])
        psY = ps("psY", [P, 2, N])
        psX = ps("psX", [P, N])
        psR = ps("psR", [P, 512])

        stage_full = Signal(sem("stage_full"), 1, 1)
        x_full = Signal(sem("x_full"), 1, 1)
        h_ready = Signal(sem("h_ready"), 1, 1)
        r_full = Signal(sem("r_full"), 1, 1)
        picked = Signal(sem("picked"), 1, 1)
        expd = Signal(sem("expd"), 1, 1)
        gated = Signal(sem("gated"), 1, 1)
        g_full = Signal(sem("g_full"), NE * J)
        u_full = Signal(sem("u_full"), NE * J)
        silued = Signal(sem("silued"), NE * J)
        h_full = Signal(sem("h_full"), NE * J)
        y_full = Signal(sem("y_full"), NE)
        y_used = Signal(sem("y_used"), NE)
        var_ready = Signal(sem("var_ready"), 1)
        rs_ready = Signal(sem("rs_ready"), 1)
        res_ready = Signal(sem("res_ready"), 1)
        stored = [sem("stored_even"), sem("stored_odd")]
        own = Chain(sem("own"), CHAIN_M, CHAIN_M_PRE)
        block = ctx.enter_context(nc.Block())

        def tiles(a, pair, half):
            return a[:, bass.ds((pair * 2 + half) * NT + QT, NT), :]

        @block.sync
        def _(sp):
            open_signals(sp)
            o = out.rearrange("b (t p) d -> p (b t) d", p=P)
            for s in stored:
                sp.sem_inc(s, 1)
            with sp.Fori(0, PAIRS) as pair:
                for half in range(2):
                    sp.wait_ge(res_ready.sem, res_ready.at(pair, half, 1))
                    sp.dma_start(o[:, bass.ds((pair * 2 + half) * NT, NT), :], res[:, half, :, :])\
                      .then_inc(stored[half], 16)
            for s in stored:
                sp.wait_ge(s, 16 * PAIRS + 1)

        @block.gpsimd
        def _(pool):
            pool.tensor_copy(staged[:, :, :], tiles(F, 0, 0)).then_inc(stage_full.sem, 1)
            with pool.Fori(0, PAIRS) as pair:
                for half in range(2):
                    pool.wait_ge(x_full.sem, x_full.at(pair, half, 0))
                    pool.tensor_copy(staged[:, :, :], tiles(F, pair, half + 1)).then_inc(stage_full.sem, 1)
                    pool.wait_ge(var_ready.sem, var_ready.at(pair, half, 1))
                    pool.tensor_tensor(rs[:, :], mv[:, :, 1], minus_half[:, 0:NT], ALU.pow).then_inc(rs_ready.sem, 1)

        @block.scalar
        def _(act):
            def prepare(pair, half):
                act.wait_ge(x_full.sem, x_full.at(pair, half, 0))
                act.activation(hT[:, half % 2, :], psX[:, :], ACT.Copy).then_inc(h_ready.sem, 1)

            def sigmoid_of(pair, half):
                act.wait_ge(picked.sem, picked.at(pair, half, 0))
                act.activation(sg[:, :, :], top[:, :, 0:2], ACT.Exp, scale=-1.0).then_inc(expd.sem, 1)

            prepare(0, 0)
            sigmoid_of(0, 0)
            with act.Fori(0, PAIRS) as pair:
                for half in range(2):
                    for e in range(NE):
                        for j in range(J):
                            k = e * J + j
                            act.wait_ge(g_full.sem, g_full.at(pair, half, k + 1))
                            act.wait_ge(h_full.sem, h_full.at(pair, half, max(k + 1 - 2 * J, 0)))
                            act.activation(sl[:, e % 2, j, :], psG[:, j, :], ACT.Silu).then_inc(silued.sem, 1)
                        if e == 1:
                            prepare(pair, half + 1)
                        if e == 6:
                            sigmoid_of(pair, half + 1)

        @block.vector
        def _(dve):
            def choose(pair, half):
                dve.wait_ge(r_full.sem, r_full.at(pair, half, 0))
                own.mark(dve.tensor_copy(lo[:, :, :], psR[:, 0:NT * NE].rearrange("p (t e) -> p t e", t=NT)))
                own.last()
                apart(dve, APART["dve"])
                for t in range(NT):
                    ins = dve.max(top[:, t, :], lo[:, t, :])
                ins.then_inc(picked.sem, 1)
                dve.wait_ge(picked.sem, picked.at(pair, half, 0))
                apart(dve, APART["dve"])
                for t in range(NT):
                    ins = dve.max_index(idx[:, t, :], top[:, t, :], lo[:, t, :])
                own.mark(ins)
                own.last()
                own.mark(dve.tensor_copy(idf[:, :, :], idx[:, :, 0:2]))

            def gates(pair, half):
                p = half % 2
                dve.wait_ge(expd.sem, expd.at(pair, half, 0))
                own.mark(dve.tensor_scalar(sg[:, :, :], sg[:, :, :], 1.0, None, ALU.add))
                own.last()
                own.mark(dve.reciprocal(sg[:, :, :], sg[:, :, :]))
                own.last()
                own.mark(dve.tensor_tensor(gs[:, :], sg[:, :, 0], sg[:, :, 1], ALU.add))
                own.last()
                own.mark(dve.tensor_scalar(gs[:, :], gs[:, :], 1e-10, None, ALU.add))
                own.last()
                own.mark(dve.reciprocal(gs[:, :], gs[:, :]))
                own.last()
                own.mark(dve.tensor_tensor(sg[:, :, :], sg[:, :, :], gs[:, :].unsqueeze(2).broadcast_to([P, NT, 2]),
                                           ALU.mult))
                own.last()
                for t in range(NT):
                    dve.tensor_scalar(gate[:, p, t, :], eid[:, :], idf[:, t, 0:1], sg[:, t, 0:1],
                                      ALU.is_equal, ALU.mult)
                    ins = dve.tensor_scalar(pick[:, t, :], eid[:, :], idf[:, t, 1:2], sg[:, t, 1:2],
                                            ALU.is_equal, ALU.mult)
                own.mark(ins)
                own.last()
                dve.tensor_tensor(gate[:, p, :, :], gate[:, p, :, :], pick[:, :, :], ALU.add).then_inc(gated.sem, 1)

            def accumulate(pair, half, e):
                p = half % 2
                dve.wait_ge(y_full.sem, y_full.at(pair, half, e + 1))
                if e == 0:
                    dve.wait_ge(gated.sem, gated.at(pair, half, 0))
                else:
                    own.last()
                for t in range(NT):
                    src, g = psY[:, e % 2, t * P:(t + 1) * P], gate[:, p, t, e:e + 1]
                    if e == 0:
                        ins = dve.tensor_scalar(Y[:, t, :], src, g, None, ALU.mult)
                    else:
                        ins = dve.scalar_tensor_tensor(out=Y[:, t, :], in0=src, scalar=g, in1=Y[:, t, :],
                                                       op0=ALU.mult, op1=ALU.add)
                ins.then_inc(y_used.sem, 1)
                dve.wait_ge(y_used.sem, y_used.at(pair, half, e + 1))

            def finish(pair, half):
                for t in range(NT):
                    ins = dve.bn_stats(st[:, t, :], Y[:, t, :])
                own.mark(ins)
                own.last()
                apart(dve, APART["dve"])
                for t in range(NT):
                    ins = dve.bn_aggr(mv[:, t, :], st[:, t, :])
                own.mark(ins)
                own.last()
                dve.tensor_scalar(mv[:, :, 1], mv[:, :, 1], EPS_LN, None, ALU.add).then_inc(var_ready.sem, 1)
                dve.wait_ge(rs_ready.sem, rs_ready.at(pair, half, 1))
                for t in range(NT):
                    ins = dve.tensor_scalar(yn[:, t, :], Y[:, t, :], mv[:, t, 0:1], rs[:, t:t + 1],
                                            ALU.subtract, ALU.mult)
                own.mark(ins)
                own.last()
                dve.wait_ge(stored[half % 2], pair * 16 + 1)
                dve.tensor_tensor(res[:, half % 2, :, :], yn[:, :, :], tiles(X, pair, half), ALU.add)\
                   .then_inc(res_ready.sem, 1)

            own.begin(dve, 0, 0)
            own.restart(0)
            choose(0, 0)
            gates(0, 0)
            own.restart(own.k)
            assert own.k == CHAIN_M_PRE, own.k
            with dve.Fori(0, PAIRS) as pair:
                for half in range(2):
                    own.begin(dve, pair, half)
                    for e in range(NE):
                        for j in range(J):
                            k = e * J + j
                            dve.wait_ge(silued.sem, silued.at(pair, half, k + 1))
                            dve.wait_ge(u_full.sem, u_full.at(pair, half, k + 1))
                            dve.wait_ge(y_full.sem, y_full.at(pair, half, max(e - 1, 0)))
                            dve.tensor_tensor(h[:, e % 2, j, :], psU[:, j, :], sl[:, e % 2, j, :], ALU.mult)\
                               .then_inc(h_full.sem, 1)
                        if e >= 1:
                            accumulate(pair, half, e - 1)
                        if e == 5:
                            choose(pair, half + 1)
                        if e == 7:
                            gates(pair, half + 1)
                    accumulate(pair, half, NE - 1)
                    finish(pair, half)
                    own.end()

        @block.tensor
        def _(pe):
            def prepare(pair, half):
                pe.wait_ge(stage_full.sem, stage_full.at(pair, half, 0))
                for t in range(NT):
                    ins = pe.transpose(psX[:, t * P:(t + 1) * P], staged[:, t, :], ident[:, :])
                ins.then_inc(x_full.sem, 1)

            def route(pair, half):
                pe.wait_ge(h_ready.sem, h_ready.at(pair, half, 0))
                for t in range(NT):
                    ins = pe.matmul(psR[:, t * NE:(t + 1) * NE], hT[:, half % 2, t * P:(t + 1) * P], wr[:, :],
                                    start=True, stop=True)
                ins.then_inc(r_full.sem, 1)

            def down(pair, half, e):
                pe.wait_ge(h_full.sem, h_full.at(pair, half, (e + 1) * J))
                pe.wait_ge(y_used.sem, y_used.at(pair, half, max(e - 1, 0)))
                for t in range(NT):
                    for j in range(J):
                        ins = pe.matmul(psY[:, e % 2, t * P:(t + 1) * P], h[:, e % 2, j, t * P:(t + 1) * P],
                                        wd[:, e, j, :], start=(j == 0), stop=(j == J - 1))
                ins.then_inc(y_full.sem, 1)

            prepare(0, 0)
            route(0, 0)
            with pe.Fori(0, PAIRS) as pair:
                for half in range(2):
                    x = hT[:, half % 2, :]
                    for e in range(NE):
                        for j in range(J):
                            k = e * J + j
                            cols = slice(j * P, (j + 1) * P)
                            pe.wait_ge(silued.sem, silued.at(pair, half, max(k + 1 - J, 0)))
                            pe.matmul(psG[:, j, :], wg[:, e, cols], x, start=True, stop=True).then_inc(g_full.sem, 1)
                            pe.wait_ge(h_full.sem, h_full.at(pair, half, max(k + 1 - J, 0)))
                            pe.matmul(psU[:, j, :], wu[:, e, cols], x, start=True, stop=True).then_inc(u_full.sem, 1)
                        if e >= 1:
                            down(pair, half, e - 1)
                        if e == 1:
                            prepare(pair, half + 1)
                        if e == 4:
                            pe.wait_ge(picked.sem, picked.at(pair, half, 0))
                            route(pair, half + 1)
                    down(pair, half, NE - 1)


def build(nc, ins, consts_in, out, stop=None):
    with ExitStack() as ctx:
        sb = lambda name, shape, dt=FP32: ctx.enter_context(nc.sbuf_tensor(name, shape, dt))
        sem = lambda name: nc.alloc_semaphore(name)
        APART["dve"], APART["pool"] = sb("apart_dve", [P, 1])[:, :], sb("apart_pool", [P, 1])[:, :]
        X = sb("X", [P, TILES + 2 * QT, D])
        F = sb("F", [P, QT + TILES + 4, D])

        first, later = [], []
        first.append((X[:, QT:QT + TILES, :], ins["x"].rearrange("b (t p) d -> p (b t) d", p=P)))
        wA = {}
        for k in ("Wq", "Wk1", "Wk2", "Wv", "Wo"):
            wA[k] = sb(k, [P, D])
            first.append((wA[k][:, :], ins[k]))
        consts = {}
        for k, shape, group in (("ident", [P, P], first), ("headrow", [P, 16], first), ("expert_id", [P, 8], later)):
            consts[k] = sb(k, shape)
            group.append((consts[k][:, :], consts_in[k]))
        casts = []
        for k, n, src, at in (("identb", P, "ident", 0), ("causal", P, "causal", 1), ("behind", T, "behind", 2)):
            consts[k] = sb(k, [P, n], BF16)
            wide = F[:, QT + at:QT + at + n // P, :]
            first.append((wide, consts_in[src].rearrange("p (a n) -> p a n", n=P)))
            casts.append((consts[k][:, :].rearrange("p (a n) -> p a n", n=P), wide))
        neglam = consts["neglam"] = sb("neglam", [P, 16])
        first.append((neglam[:, :], ins["lambda_logit"].unsqueeze(0).broadcast_to([P, 16])))
        minus_half = consts["minus_half"] = sb("minus_half", [P, TILES])

        row = lambda a: a.unsqueeze(0).broadcast_to([P, a.shape[0]])
        wB, wF = [], []
        for l in range(2):
            n = str(l)
            w = {"wqk": sb("wqk" + n, [P, 1024]), "wv": sb("wv" + n, [P, 512]), "wo": sb("wo" + n, [P, 4, D]),
                 "cos": sb("cos" + n, [P, QT, 2, 64]), "sin": sb("sin" + n, [P, QT, 2, 64]),
                 "scale": sb("scale" + n, [P, 2, 64]), "scaler": sb("scaler" + n, [P, 2, 64])}
            later += [(w["wqk"][:, :], ins["wqkv"][l, :, 0:1024]), (w["wv"][:, :], ins["wqkv"][l, :, 1024:1536]),
                      (w["wo"][:, :, :], ins["wo"][l].rearrange("(n p) d -> p n d", p=P)),
                      (w["cos"][:, :, :, :], consts_in["cos"]), (w["sin"][:, :, :, :], consts_in["sin"])]
            for a, k in enumerate(("q_scale", "k_scale")):
                s = ins[k][l, :]
                later += [(w["scale"][:, a, :], row(s)), (w["scaler"][:, a, 0:32], row(s[32:64])),
                          (w["scaler"][:, a, 32:64], row(s[0:32]))]
            wB.append(w)
            w = {"w1": sb("w1" + n, [P, 682]), "b1": sb("b1" + n, [P, 6]), "w2": sb("w2" + n, [P, 3, D]),
                 "b2": sb("b2" + n, [P, D]), "ln_g": sb("lng" + n, [P, 1]), "ln_b": sb("lnb" + n, [P, 1])}
            later += [(w["w1"][:, :], ins["w1"][l]), (w["b1"][:, :], ins["b1"][l]), (w["w2"][:, :, :], ins["w2"][l]),
                      (w["b2"][:, :], row(ins["b2"][l, :])), (w["ln_g"][:, :], ins["ln_g"][l, :].unsqueeze(1)),
                      (w["ln_b"][:, :], ins["ln_b"][l, :].unsqueeze(1))]
            wF.append(w)
        wS = {}
        for k, shape in (("W_in", [P, 32]), ("b_in", [P, 1]), ("Bm", [P, P]), ("A", [P, P]), ("AT", [P, P]),
                         ("C", [P, D])):
            wS[k] = sb("s_w" + k, shape)
            later.append((wS[k][:, :], ins["s_" + k]))
        wS["D"] = sb("s_wD", [P, D])
        later.append((wS["D"][:, :], row(ins["s_D"])))
        wM = {"router": sb("m_router", [P, 8]), "gate": sb("m_gate", [P, 8, 256]), "up": sb("m_up", [P, 8, 256]),
              "down": sb("m_down", [P, 8, 2, D])}
        later += [(wM["router"][:, :], ins["router"]), (wM["gate"][:, :, :], ins["w_gate"].rearrange("e d h -> d e h")),
                  (wM["up"][:, :, :], ins["w_up"].rearrange("e d h -> d e h")),
                  (wM["down"][:, :, :, :], ins["w_down"].rearrange("e (j p) d -> p e j d", p=P))]

        loaded, loaded_later, ready = sem("loaded"), sem("loaded_later"), sem("ready")
        with nc.Block() as block:
            @block.sync
            def _(sp):
                for dst, src in first:
                    sp.dma_start(dst, src).then_inc(loaded, 16)
                for dst, src in later:
                    sp.dma_start(dst, src).then_inc(loaded_later, 16)
                sp.wait_ge(loaded, 16 * len(first))

            @block.gpsimd
            def _(pool):
                pool.memset(minus_half[:, :], -0.5)
                pool.memset(APART["dve"], 0.0)
                pool.memset(APART["pool"], 0.0)
                pool.memset(X[:, 0:QT, :], 0.0)
                pool.memset(X[:, QT + TILES:TILES + 2 * QT, :], 0.0)
                pool.memset(F[:, 0:QT, :], 0.0)
                pool.memset(F[:, QT + TILES:, :], 0.0).then_inc(ready, 1)

            @block.scalar
            def _(act):
                act.wait_ge(loaded, 16 * len(first))
                act.activation(neglam[:, :], neglam[:, :], ACT.Exp, scale=-1.0).then_inc(ready, 1)

            @block.vector
            def _(dve):
                dve.wait_ge(ready, 2)
                dve.tensor_scalar(neglam[:, :], neglam[:, :], -1.0, -1.0, ALU.mult, ALU.add).then_inc(ready, 1)
                for narrow, wide in casts:
                    dve.tensor_copy(narrow, wide)
                dve.wait_ge(ready, 3)
                dve.reciprocal(neglam[:, :], neglam[:, :]).then_inc(ready, 1)

        differential_attention(nc, X, consts, wA)

        if stop != "A":
            with nc.Block() as block:
                @block.vector
                def _(dve):
                    dve.wait_ge(loaded_later, 16 * len(later))
                    for w in wB:
                        for tab, s in (("cos", "scale"), ("sin", "scaler")):
                            for t in range(QT):
                                dve.tensor_tensor(w[tab][:, t], w[tab][:, t], w[s][:, :, :], ALU.mult)
            normalise_all(nc, "n0", X, F, minus_half)
            for l in range(2):
                window_attention(nc, f"b{l}", F, consts, wB[l])
                if stop == "B0":
                    break
                feed_forward(nc, f"f{l}", F, consts, wF[l])
                if stop == "F0":
                    break
            if stop in ("B0", "F0"):
                X = F
            else:
                add_normalised(nc, "n1", X, F, minus_half)
        if stop in (None, "S"):
            normalise_all(nc, "n2", X, F, minus_half)
            state_space(nc, X, F, consts, wS)
        if stop is None:
            normalise_all(nc, "n3", X, F, minus_half)
            mixture_of_experts(nc, X, F, out, consts, wM)
            return

        stored = nc.alloc_semaphore("stored")
        with nc.Block() as block:
            @block.sync
            def _(sp):
                sp.dma_start(out.rearrange("b (t p) d -> p (b t) d", p=P), X[:, QT:QT + TILES, :]).then_inc(stored, 16)
                sp.wait_ge(stored, 16)


def constants():
    r = np.arange(128)
    c = {
        "ident": np.eye(128, dtype=np.float32),
        "causal": np.where(r[None, :] <= r[:, None], 0.0, -1e37).astype(np.float32),
        "headrow": (r[:, None] // 8 == np.arange(16)[None, :]).astype(np.float32),
    }
    i, j = 128 + r[:, None], np.arange(256)[None, :]
    c["behind"] = np.where((j <= i) & (i <= j + 64), 0.0, -1e37).astype(np.float32)
    c["expert_id"] = np.tile(np.arange(8, dtype=np.float32), (128, 1))
    f = np.float32
    half = np.arange(0, 64, 2).astype(f)
    inv = f(1) / f(10000) ** (half / f(64))
    t = np.arange(256).astype(f)
    freqs = np.concatenate([t[:, None] * inv[None]] * 2, -1)
    base = (half + f(25.6)) / f(89.6)
    scale = base[None] ** ((t - f(128)) / f(32))[:, None]
    scale = np.concatenate([scale] * 2, -1)
    sign = np.where(np.arange(64) < 32, -1, 1).astype(f)
    both = lambda a: np.stack([f(8) * a * scale, a / scale], 1)
    tiles = lambda a: np.ascontiguousarray(both(a).reshape(2, 128, 2, 64).transpose(1, 0, 2, 3)).astype(f)
    c["cos"] = tiles(np.cos(freqs))
    c["sin"] = tiles(np.sin(freqs) * sign)
    return c


def layout(inputs):
    a = {k: np.asarray(v) for k, v in inputs.items()}
    c = np.ascontiguousarray
    b1 = np.zeros((2, 2, 384), np.float32)
    b1[:, :, :341] = a["L0_ffn_b1"].reshape(2, 2, 341)
    b1 = c(b1.reshape(2, 6, 128).transpose(0, 2, 1))
    w2 = np.zeros((2, 384, 128), np.float32)
    w2[:, :341] = a["L0_ffn_w2"]
    w2 = c(w2.reshape(2, 3, 128, 128).transpose(0, 2, 1, 3))

    def diagonal(m):
        big = np.zeros((128, 128), np.float32)
        for g in range(4):
            big[32 * g:32 * g + 32, 32 * g:32 * g + 32] = m
        return big

    return {
        "x": c(a["L0_attn_x"]),
        **{k: c(a["L0_attn_" + k].T) for k in ("Wq", "Wk1", "Wk2", "Wv", "Wo")},
        "lambda_logit": c(a["L0_attn_lambda_logit"]),
        **{k: c(a["L0_ffn_" + k]) for k in ("wqkv", "q_scale", "k_scale", "wo", "w1", "b2", "ln_g", "ln_b")},
        "b1": b1,
        "w2": w2,
        "s_W_in": c(a["L1_attn_W_in"].T),
        "s_b_in": c(np.tile(a["L1_attn_b_in"], 4)[:, None]),
        "s_Bm": diagonal(a["L1_attn_Bm"].T),
        "s_A": diagonal(a["L1_attn_A"]),
        "s_AT": diagonal(a["L1_attn_A"].T),
        "s_C": c(np.tile(a["L1_attn_C"].T, (4, 1))),
        "s_D": c(a["L1_attn_D"]),
        "router": c(a["L1_ffn_router_w"].T),
        **{k: c(a["L1_ffn_" + k]) for k in ("w_gate", "w_up", "w_down")},
    }


def kernel(**inputs):
    import concourse.bacc as bacc
    from concourse.bass_utils import run_bass_kernel_spmd as run

    nc = bacc.Bacc("TRN2", target_bir_lowering=False, num_devices=1)
    arrays, ins, consts = {}, {}, {}
    for group, into in ((layout(inputs), ins), (constants(), consts)):
        for name, a in group.items():
            full = f"in_{name}_dram"
            arrays[full] = a
            into[name] = nc.dram_tensor(full, a.shape, mybir.dt.from_np(a.dtype), kind="ExternalInput").ap()
    out = nc.dram_tensor("out_0_dram", (16, 256, 128), FP32, kind="ExternalOutput").ap()
    build(nc, ins, consts, out)
    r = run(nc, [arrays], core_ids=[0])
    return r.results[0]["out_0_dram"]
```

```python
import numpy as np
import concourse.bass as bass
from concourse import mybir
from contextlib import ExitStack

FP32 = mybir.dt.float32
BF16 = mybir.dt.bfloat16
ALU = mybir.AluOpType
ACT = mybir.ActivationFunctionType
AX = mybir.AxisListType

P = 128
D = 128
BATCH = 16
T = 256
QT = T // P
TILES = BATCH * QT
EPS_LN = 1e-5


class Signal:
    opened = []

    def __init__(self, sem, per, base=0):
        self.sem, self.per, self.base = sem, per, base + 1
        self.opened.append(self)

    def early(self, k):
        return k + 1

    def at(self, pair, half, k):
        return pair * (2 * self.per) + (half * self.per + k + self.base)


class Chain(Signal):

    def __init__(self, sem, per, base=0):
        super().__init__(sem, per, base)
        self.k = 0

    def begin(self, eng, pair, half):
        self.eng, self.pair, self.half, self.k = eng, pair, half, 0

    def restart(self, raises):
        self.base = raises + 1

    def mark(self, ins):
        self.k += 1
        ins.then_inc(self.sem, 1)
        return self.k

    def wait(self, k):
        self.eng.wait_ge(self.sem, self.at(self.pair, self.half, k))

    def last(self):
        self.wait(self.k)

    def end(self):
        assert self.k == self.per, f"{self.k} raises a batch, not {self.per}"


def open_signals(eng):
    for signal in Signal.opened:
        eng.sem_inc(signal.sem, 1)
    Signal.opened.clear()


APART = {}


def apart(eng, scratch):
    eng.tensor_tensor(scratch, scratch, scratch, ALU.mult)

CHAIN_A = 62
CHAIN_B = 6
CHAIN_F = 2
CHAIN_M, CHAIN_M_PRE = 13, 10


def differential_attention(nc, X, consts, weights):
    H, HD = 16, 8
    GH = 4
    SCALE = HD ** -0.5
    ident, identb, causal, headrow, neglam = (consts[k] for k in ("ident", "identb", "causal", "headrow", "neglam"))
    wq, wk1, wk2, wv, wo = (weights[k] for k in ("Wq", "Wk1", "Wk2", "Wv", "Wo"))
    minus_half = consts["minus_half"]

    with ExitStack() as ctx:
        sb = lambda name, shape, dt=FP32: ctx.enter_context(nc.sbuf_tensor("a_" + name, shape, dt))
        ps = lambda name, shape: ctx.enter_context(nc.psum_tensor("a_" + name, shape, FP32))
        sem = lambda name: nc.alloc_semaphore("a_" + name)

        qm = sb("qm", [P, 2, H, T])
        qT = sb("qT", [P, T])
        kT = sb("kT", [P, 2, 2, T])
        vp = sb("vp", [P, 2, QT, H, 32])
        xn = sb("xn", [P, QT, D])
        xnT = sb("xnT", [P, T])
        st = sb("st", [P, 2, QT, 6])
        mv = sb("mv", [P, 2, QT, 2])
        rs = sb("rs", [P, 2, QT])
        nm = sb("nm", [P, 2, 2, 2])
        Z = sb("Z", [P, 2, H, 2, 2])
        E = sb("E", [P, 2, 2, 384])
        rz = sb("rz", [P, 2, 2])
        cf = sb("cf", [P, 2, 2])
        d = sb("d", [P, 2, 384])
        ab = sb("ab", [P, 2, H, 3])
        den = sb("den", [P, 2, H])
        floor = sb("floor", [P, 2, H])
        dT = sb("dT", [P, 2, 384])
        OT = sb("OT", [P, H // GH, T])
        On = sb("On", [P, QT, D])
        OnT = sb("OnT", [P, T])
        y = sb("y", [P, QT, D])
        yn = sb("yn", [P, QT, D])

        psS = ps("psS", [P, 2, 2, 512])
        psT = ps("psT", [P, 2, 512])
        psO = ps("psO", [P, T])
        psM = ps("psM", [P, 512])

        E_OT0, E_OT1, E_ONT, E_Y, P_XNT, P_Q, P_K1, P_K2, P_V = range(9)
        USES, PRE = 9, 5
        misc_full = Signal(sem("misc_full"), USES, PRE)
        misc_free = Signal(sem("misc_free"), USES, PRE)
        scored = Signal(sem("scored"), H)
        maxed = Signal(sem("maxed"), H)
        exped = Signal(sem("exped"), H, 2)
        mixed = Signal(sem("mixed"), H, 2)
        turned = Signal(sem("turned"), H, 2)
        evaced = Signal(sem("evaced"), H, 2)
        pved = Signal(sem("pved"), H, 2)
        otmoved = Signal(sem("otmoved"), H // GH, 1)
        qm_ready = Signal(sem("qm_ready"), H)
        xn_ready = Signal(sem("xn_ready"), 1, 1)
        var_ready = Signal(sem("var_ready"), 2, 1)
        rs_ready = Signal(sem("rs_ready"), 2, 1)
        den_ready = Signal(sem("den_ready"), 1)
        added = Signal(sem("added"), 1)
        zeroed = sem("zeroed")
        own = Chain(sem("own"), CHAIN_A, 4)

        block = ctx.enter_context(nc.Block())
        LAST = BATCH // 2

        def x_of(pair, half):
            return X[:, bass.ds((pair * 2 + (half + 1)) * QT, QT), :]

        @block.sync
        def _(sp):
            open_signals(sp)

        @block.gpsimd
        def _(pool):
            for tile in (vp, OT, Z, ab, dT):
                pool.memset(tile[:], 1.0 if tile in (Z, ab) else 0.0).then_inc(zeroed, 1)

            def rstd(which, pair, half, k):
                pool.wait_ge(var_ready.sem, var_ready.at(pair, half, k))
                pool.tensor_tensor(rs[:, which, :], mv[:, which, :, 1], minus_half[:, 0:QT], ALU.pow)\
                    .then_inc(rs_ready.sem, 1)

            def mask_heads(half):
                apart(pool, APART["pool"])
                for h in range(H):
                    pool.tensor_scalar(qm[:, half % 2, h, :], qT[:, :], headrow[:, h:h + 1], 1.0,
                                       ALU.mult, ALU.mult).then_inc(qm_ready.sem, 1)

            rstd(0, 0, 0, 0)
            pool.wait_ge(misc_free.sem, misc_free.early(2))
            mask_heads(0)
            with pool.Fori(0, LAST) as pair:
                for half in range(2):
                    rstd(0, pair, half, 1)
                    rstd(1, pair, half, 2)
                    pool.wait_ge(misc_free.sem, misc_free.at(pair, half, P_Q + 1))
                    pool.wait_ge(scored.sem, scored.at(pair, half, 0))
                    mask_heads(half + 1)
            rstd(1, LAST, 0, 1)

        @block.vector
        def _(dve):
            def maxima(pair, half, h):
                s = h % 2
                dve.wait_ge(scored.sem, scored.at(pair, half, h + 1))
                dve.tensor_reduce(nm[:, s, 0, :], psS[:, s, :, 0:P], axis=AX.X, op=ALU.max, negate=True)
                dve.tensor_reduce(nm[:, s, 1, :], psS[:, s, :, P:384], axis=AX.X, op=ALU.max, negate=True)\
                   .then_inc(maxed.sem, 1)

            def mix(pair, half, h):
                s, p = h % 2, half % 2
                dve.wait_ge(exped.sem, exped.at(pair, half, h + 1))
                own.mark(dve.reciprocal(rz[:, s, :], Z[:, p, h, :, 1]))
                own.last()
                own.mark(dve.scalar_tensor_tensor(out=cf[:, s, :], in0=Z[:, p, h, :, 0], scalar=neglam[:, h:h + 1],
                                                  in1=rz[:, s, :], op0=ALU.mult, op1=ALU.mult))
                dve.wait_ge(turned.sem, turned.at(pair, half, h - 1))
                own.last()
                for t, c0, c1 in ((0, 0, P), (1, P, 384)):
                    ins = dve.scalar_tensor_tensor(out=d[:, s, c0:c1], in0=E[:, s, 1, c0:c1],
                                                   scalar=cf[:, s, t:t + 1], in1=E[:, s, 0, c0:c1],
                                                   op0=ALU.mult, op1=ALU.add)
                ins.then_inc(mixed.sem, 1)
                dve.wait_ge(mixed.sem, mixed.at(pair, half, h + 1))
                own.mark(dve.tensor_reduce(ab[:, p, h, :], d[:, s, :].rearrange("p (c k) -> p c k", c=3),
                                           axis=AX.X, op=ALU.add, apply_absolute_value=True))

            def variance(which, src):
                for t in range(QT):
                    own.mark(dve.bn_stats(st[:, which, t, :], src[:, t, :]))
                own.last()
                apart(dve, APART["dve"])
                for t in range(QT):
                    own.mark(dve.bn_aggr(mv[:, which, t, :], st[:, which, t, :]))
                own.last()
                dve.tensor_scalar(mv[:, which, :, 1], mv[:, which, :, 1], EPS_LN, None, ALU.add)\
                   .then_inc(var_ready.sem, 1)

            def normalise_x(xs):
                for t in range(QT):
                    ins = dve.tensor_scalar(xn[:, t, :], xs[:, t, :], mv[:, 0, t, 0:1], rs[:, 0, t:t + 1],
                                            ALU.subtract, ALU.mult)
                ins.then_inc(xn_ready.sem, 1)

            def denominators(pair, half):
                q = (half - 1) % 2
                own.last()
                own.mark(dve.tensor_copy(den[:, 0, :], ab[:, q, :, 0]))
                own.mark(dve.tensor_tensor(den[:, 1, :], ab[:, q, :, 1], ab[:, q, :, 2], ALU.add))
                own.last()
                for t in range(QT):
                    own.mark(dve.scalar_tensor_tensor(out=floor[:, t, :], in0=Z[:, q, :, t, 0], scalar=1e-6,
                                                      in1=den[:, t, :], op0=ALU.mult, op1=ALU.max))
                own.last()
                dve.reciprocal(den[:, :, :], floor[:, :, :]).then_inc(den_ready.sem, 1)

            def normalise_o(pair, half, t):
                dve.wait_ge(misc_full.sem, misc_full.at(pair, half, E_OT0 + t + 1))
                dve.wait_ge(den_ready.sem, den_ready.at(pair, half, 1))
                dve.tensor_tensor(On[:, t, :].rearrange("p (h e) -> p h e", e=HD),
                                  psM[:, :].rearrange("p (h e) -> p h e", e=32)[:, :, 0:HD],
                                  den[:, t, :].unsqueeze(2).broadcast_to([P, H, HD]), ALU.mult)\
                   .then_inc(misc_free.sem, 1)

            def residual(pair, half, k):
                dve.wait_ge(rs_ready.sem, rs_ready.at(pair, half, k))
                for t in range(QT):
                    own.mark(dve.tensor_scalar(yn[:, t, :], y[:, t, :], mv[:, 1, t, 0:1], rs[:, 1, t:t + 1],
                                               ALU.subtract, ALU.mult))
                own.last()
                xs = x_of(pair, half - 1)
                dve.tensor_tensor(xs, xs, yn[:, :, :], ALU.add).then_inc(added.sem, 1)

            dve.memset(psO[:, :], 0.0).then_inc(zeroed, 1)
            dve.wait_ge(zeroed, 6)
            own.begin(dve, 0, 0)
            own.restart(0)
            variance(0, x_of(0, 0))
            own.restart(own.k)
            assert own.k == 4
            dve.wait_ge(rs_ready.sem, rs_ready.early(1))
            normalise_x(x_of(0, 0))
            maxima(0, 0, 0)
            with dve.Fori(0, LAST) as pair:
                for half in range(2):
                    own.begin(dve, pair, half)
                    for s in range(H):
                        maxima(pair, half + (s + 1) // H, (s + 1) % H)
                        if s == 0:
                            denominators(pair, half)
                        mix(pair, half, s)
                        if s in (2, 4):
                            normalise_o(pair, half, s // 2 - 1)
                        if s == 5:
                            variance(0, x_of(pair, half + 1))
                        if s == 7:
                            dve.wait_ge(rs_ready.sem, rs_ready.at(pair, half, 1))
                            dve.wait_ge(misc_full.sem, misc_full.at(pair, half - 1, P_XNT + 1))
                            normalise_x(x_of(pair, half + 1))
                        if s == 9:
                            dve.wait_ge(misc_free.sem, misc_free.at(pair, half, E_Y + 1))
                            variance(1, y)
                        if s == 12:
                            residual(pair, half, 2)
                    own.end()
            own.begin(dve, LAST, 0)
            denominators(LAST, 0)
            normalise_o(LAST, 0, 0)
            normalise_o(LAST, 0, 1)
            dve.wait_ge(misc_free.sem, misc_free.at(LAST, 0, E_Y + 1))
            variance(1, y)
            residual(LAST, 0, 1)

        @block.scalar
        def _(act):
            def exps(pair, half, h, first=False):
                s, p = h % 2, half % 2
                act.wait_ge(maxed.sem, maxed.at(pair, half, h + 1))
                act.wait_ge(mixed.sem, mixed.at(pair, half, h - 1))
                if h == 0:
                    act.wait_ge(den_ready.sem, den_ready.at(pair, half, 0))
                for t, c0, c1 in ((0, 0, P), (1, P, 384)):
                    for m in range(2):
                        ins = act.activation(E[:, s, m, c0:c1], psS[:, s, m, c0:c1], ACT.Exp,
                                             bias=nm[:, s, t, m:m + 1], accum_out=Z[:, p, h, t, m:m + 1])
                ins.then_inc(exped.sem, 1)

            def evac_d(pair, half, h):
                s = h % 2
                act.wait_ge(turned.sem, turned.at(pair, half, h + 1))
                act.wait_ge(pved.sem, pved.at(pair, half, h - 1))
                act.activation(dT[:, s, :], psT[:, s, 0:384], ACT.Copy).then_inc(evaced.sem, 1)

            def move_ot(pair, half, g):
                act.wait_ge(pved.sem, pved.at(pair, half, GH * (g + 1)))
                if g == 0:
                    act.wait_ge(misc_full.sem, misc_full.at(pair, half, E_OT1 + 1))
                act.activation(OT[:, g, :], psO[:, :], ACT.Copy).then_inc(otmoved.sem, 1)

            def copy(dst, src, full, scale=1.0):
                act.wait_ge(misc_full.sem, full)
                act.activation(dst, src, ACT.Copy, scale=scale).then_inc(misc_free.sem, 1)

            def prepare(use, p, full):
                if use == P_XNT:
                    copy(xnT[:, :], psM[:, 0:T], full)
                elif use == P_Q:
                    copy(qT[:, :], psM[:, T:512], full, SCALE)
                elif use == P_K1:
                    copy(kT[:, p, 0, :], psM[:, 0:T], full)
                elif use == P_K2:
                    copy(kT[:, p, 1, :], psM[:, T:512], full)
                elif use == P_V:
                    copy(vp[:, p, :, :, 0:HD],
                         psM[:, 0:T].rearrange("p (t h e) -> p t h e", t=QT, e=HD), full)

            act.wait_ge(zeroed, 6)
            for signal, n in ((exped, 2), (mixed, 2), (turned, 2), (evaced, 2), (pved, 1)):
                act.sem_inc(signal.sem, n)
            for n, use in enumerate((P_XNT, P_Q, P_K1, P_K2, P_V)):
                prepare(use, 0, misc_full.early(n + 1))
            exps(0, 0, 0)
            with act.Fori(0, LAST) as pair:
                for half in range(2):
                    p = (half + 1) % 2
                    for s in range(H):
                        exps(pair, half + (s + 1) // H, (s + 1) % H)
                        if s == 0:
                            move_ot(pair, half - 1, H // GH - 1)
                        evac_d(pair, half, s)
                        if s in (4, 8, 12):
                            move_ot(pair, half, s // 4 - 1)
                        if s == 6:
                            copy(OnT[:, :], psM[:, 0:T], misc_full.at(pair, half, E_ONT + 1))
                        if s == 8:
                            act.wait_ge(added.sem, added.at(pair, half, 0))
                            copy(y[:, :, :], psM[:, T:512].rearrange("p (t n) -> p t n", t=QT),
                                 misc_full.at(pair, half, E_Y + 1))
                        if 9 <= s <= 13:
                            use = P_XNT + s - 9
                            if use == P_Q:
                                act.wait_ge(qm_ready.sem, qm_ready.at(pair, half + 1, 0))
                            if use == P_K1:
                                act.wait_ge(scored.sem, scored.at(pair, half, 0))
                            if use == P_V:
                                act.wait_ge(pved.sem, pved.at(pair, half, 0))
                            prepare(use, p, misc_full.at(pair, half, use + 1))
            move_ot(LAST, -1, H // GH - 1)
            copy(OnT[:, :], psM[:, 0:T], misc_full.at(LAST, 0, E_ONT + 1))
            act.wait_ge(added.sem, added.at(LAST, 0, 0))
            copy(y[:, :, :], psM[:, T:512].rearrange("p (t n) -> p t n", t=QT), misc_full.at(LAST, 0, E_Y + 1))

        @block.tensor
        def _(pe):
            def scores(pair, half, h):
                s, p = h % 2, half % 2
                pe.wait_ge(exped.sem, exped.at(pair, half, h - 1))
                pe.wait_ge(qm_ready.sem, qm_ready.at(pair, half, h + 1))
                for m in range(2):
                    out = psS[:, s, m, :]
                    pe.matmul(out[:, 0:P], qm[:, p, h, 0:P], kT[:, p, m, 0:P], start=True, stop=False)
                    pe.matmul(out[:, 0:P], identb[:, :], causal[:, :], start=False, stop=True)
                    pe.matmul(out[:, P:384], qm[:, p, h, P:T], kT[:, p, m, 0:T], start=True, stop=False)
                    ins = pe.matmul(out[:, T:384], identb[:, :], causal[:, :], start=False, stop=True)
                ins.then_inc(scored.sem, 1)

            def turn(pair, half, h):
                s = h % 2
                pe.wait_ge(mixed.sem, mixed.at(pair, half, h + 1))
                pe.wait_ge(evaced.sem, evaced.at(pair, half, h - 1))
                for c in range(3):
                    ins = pe.transpose(psT[:, s, c * P:(c + 1) * P], d[:, s, c * P:(c + 1) * P], ident[:, :])
                ins.then_inc(turned.sem, 1)

            def outputs(pair, half, h):
                s, p, g, j = h % 2, half % 2, h // GH, h % GH
                pe.wait_ge(evaced.sem, evaced.at(pair, half, h + 1))
                if j == 0:
                    pe.wait_ge(otmoved.sem, otmoved.at(pair, half, g))
                out = psO[32 * j:32 * j + 32, :]
                pe.matmul(out[:, 0:P], vp[:, p, 0, h, :], dT[:, s, 0:P], start=True, stop=True)
                pe.matmul(out[:, P:T], vp[:, p, 0, h, :], dT[:, s, P:T], start=True, stop=False)
                pe.matmul(out[:, P:T], vp[:, p, 1, h, :], dT[:, s, T:384], start=False, stop=True)\
                  .then_inc(pved.sem, 1)

            def use_misc(use, p, free):
                pe.wait_ge(misc_free.sem, free)
                lo, hi = psM[:, 0:T], psM[:, T:512]
                if use in (E_OT0, E_OT1):
                    t = use - E_OT0
                    for g in range(H // GH):
                        ins = pe.transpose(psM[:, g * P:(g + 1) * P], OT[:, g, t * P:(t + 1) * P], ident[:, :])
                elif use == E_ONT:
                    for t in range(QT):
                        ins = pe.transpose(lo[:, t * P:(t + 1) * P], On[:, t, :], ident[:, :])
                elif use == E_Y:
                    for t in range(QT):
                        ins = pe.matmul(hi[:, t * P:(t + 1) * P], OnT[:, t * P:(t + 1) * P], wo[:, :],
                                        start=True, stop=True)
                elif use == P_XNT:
                    for t in range(QT):
                        ins = pe.transpose(lo[:, t * P:(t + 1) * P], xn[:, t, :], ident[:, :])
                elif use == P_Q:
                    ins = pe.matmul(hi, wq[:, :], xnT[:, :], start=True, stop=True)
                elif use == P_K1:
                    ins = pe.matmul(lo, wk1[:, :], xnT[:, :], start=True, stop=True)
                elif use == P_K2:
                    ins = pe.matmul(hi, wk2[:, :], xnT[:, :], start=True, stop=True)
                else:
                    for t in range(QT):
                        ins = pe.matmul(lo[:, t * P:(t + 1) * P], xnT[:, t * P:(t + 1) * P], wv[:, :],
                                        start=True, stop=True)
                ins.then_inc(misc_full.sem, 1)

            pe.wait_ge(zeroed, 6)
            pe.wait_ge(xn_ready.sem, xn_ready.early(1))
            for n, use in enumerate((P_XNT, P_Q, P_K1, P_K2, P_V)):
                use_misc(use, 0, misc_free.early(n))
            pe.wait_ge(misc_free.sem, misc_free.early(PRE))
            scores(0, 0, 0)
            scores(0, 0, 1)
            SCHEDULE = {1: E_OT0, 3: E_OT1, 5: E_ONT, 7: E_Y, 8: P_XNT, 9: P_Q, 10: P_K1, 11: P_K2, 12: P_V}
            with pe.Fori(0, LAST) as pair:
                for half in range(2):
                    for s in range(H):
                        if s == H - 2:
                            pe.wait_ge(misc_free.sem, misc_free.at(pair, half, USES))
                        scores(pair, half + (s + 2) // H, (s + 2) % H)
                        turn(pair, half, s)
                        outputs(pair, half - 1 if s == 0 else half, (s - 1) % H)
                        if s in SCHEDULE:
                            use = SCHEDULE[s]
                            if use == E_OT0:
                                pe.wait_ge(otmoved.sem, otmoved.at(pair, half, 0))
                            if use == P_XNT:
                                pe.wait_ge(xn_ready.sem, xn_ready.at(pair, half, 1))
                            use_misc(use, half, misc_free.at(pair, half, use))
            outputs(LAST, -1, H - 1)
            pe.wait_ge(otmoved.sem, otmoved.at(LAST, 0, 0))
            for use in (E_OT0, E_OT1, E_ONT, E_Y):
                use_misc(use, 0, misc_free.at(LAST, 0, use))


def normalise_all(nc, name, src, dst, minus_half):
    G = 8
    with ExitStack() as ctx:
        sem = lambda n: nc.alloc_semaphore(name + n)
        st = ctx.enter_context(nc.sbuf_tensor(name + "st", [P, G, 6], FP32))
        mv = ctx.enter_context(nc.sbuf_tensor(name + "mv", [P, G, 2], FP32))
        rs = ctx.enter_context(nc.sbuf_tensor(name + "rs", [P, G], FP32))
        stats, var_ready, rs_ready = sem("stats"), sem("var_ready"), sem("rs_ready")
        block = ctx.enter_context(nc.Block())

        @block.gpsimd
        def _(pool):
            with pool.Fori(0, TILES // G) as g:
                pool.wait_ge(var_ready, g + 1)
                pool.tensor_tensor(rs[:, :], mv[:, :, 1], minus_half[:, 0:G], ALU.pow).then_inc(rs_ready, 1)

        @block.vector
        def _(dve):
            with dve.Fori(0, TILES // G) as g:
                tiles = lambda a, t: a[:, bass.ds(g * G + (QT + t), 1), :]
                for t in range(G):
                    ins = dve.bn_stats(st[:, t, :], tiles(src, t)[:, 0, :])
                ins.then_inc(stats, 1)
                dve.wait_ge(stats, g * 2 + 1)
                apart(dve, APART["dve"])
                for t in range(G):
                    ins = dve.bn_aggr(mv[:, t, :], st[:, t, :])
                ins.then_inc(stats, 1)
                dve.wait_ge(stats, g * 2 + 2)
                dve.tensor_scalar(mv[:, :, 1], mv[:, :, 1], EPS_LN, None, ALU.add).then_inc(var_ready, 1)
                dve.wait_ge(rs_ready, g + 1)
                for t in range(G):
                    dve.tensor_scalar(tiles(dst, t)[:, 0, :], tiles(src, t)[:, 0, :], mv[:, t, 0:1], rs[:, t:t + 1],
                                      ALU.subtract, ALU.mult)


def add_normalised(nc, name, X, src, minus_half):
    G = 8
    with ExitStack() as ctx:
        sem = lambda n: nc.alloc_semaphore(name + n)
        st = ctx.enter_context(nc.sbuf_tensor(name + "st", [P, G, 6], FP32))
        mv = ctx.enter_context(nc.sbuf_tensor(name + "mv", [P, G, 2], FP32))
        rs = ctx.enter_context(nc.sbuf_tensor(name + "rs", [P, G], FP32))
        yn = ctx.enter_context(nc.sbuf_tensor(name + "yn", [P, G, D], FP32))
        stats, var_ready, rs_ready, scaled = sem("stats"), sem("var_ready"), sem("rs_ready"), sem("scaled")
        block = ctx.enter_context(nc.Block())

        @block.gpsimd
        def _(pool):
            with pool.Fori(0, TILES // G) as g:
                pool.wait_ge(var_ready, g + 1)
                pool.tensor_tensor(rs[:, :], mv[:, :, 1], minus_half[:, 0:G], ALU.pow).then_inc(rs_ready, 1)

        @block.vector
        def _(dve):
            with dve.Fori(0, TILES // G) as g:
                for t in range(G):
                    ins = dve.bn_stats(st[:, t, :], src[:, bass.ds(g * G + (QT + t), 1), :][:, 0, :])
                ins.then_inc(stats, 1)
                dve.wait_ge(stats, g * 2 + 1)
                apart(dve, APART["dve"])
                for t in range(G):
                    ins = dve.bn_aggr(mv[:, t, :], st[:, t, :])
                ins.then_inc(stats, 1)
                dve.wait_ge(stats, g * 2 + 2)
                dve.tensor_scalar(mv[:, :, 1], mv[:, :, 1], EPS_LN, None, ALU.add).then_inc(var_ready, 1)
                dve.wait_ge(rs_ready, g + 1)
                for t in range(G):
                    ins = dve.tensor_scalar(yn[:, t, :], src[:, bass.ds(g * G + (QT + t), 1), :][:, 0, :],
                                            mv[:, t, 0:1], rs[:, t:t + 1], ALU.subtract, ALU.mult)
                ins.then_inc(scaled, 1)
                dve.wait_ge(scaled, g + 1)
                xs = X[:, bass.ds(g * G + QT, G), :]
                dve.tensor_tensor(xs, xs, yn[:, :, :], ALU.add)


def window_attention(nc, name, F, consts, w):
    H, HD = 8, 64
    NP = H // 2
    W = H * HD
    NW = T // 64
    KEYS = (0, 0, 64, 128)
    ident, identb, behind = (consts[k] for k in ("ident", "identb", "behind"))
    minus_half = consts["minus_half"]
    wqk, wv, wo = w["wqk"], w["wv"], w["wo"]
    cos, sin = w["cos"], w["sin"]

    with ExitStack() as ctx:
        sb = lambda n, shape, dt=FP32: ctx.enter_context(nc.sbuf_tensor(name + n, shape, dt))
        ps = lambda n, shape: ctx.enter_context(nc.psum_tensor(name + n, shape, FP32))
        sem = lambda n: nc.alloc_semaphore(name + n)

        staged = sb("staged", [P, QT, D])
        hT = sb("hT", [P, 2, T])
        sq = sb("sq", [P, 2 * W])
        ss = sb("ss", [P, QT, 2 * H])
        rn = sb("rn", [P, QT, 2 * H])
        part = sb("part", [P, 2, 2 * W])
        rot = sb("rot", [P, 2 * W])
        qk = sb("qk", [P, QT, 2 * W])
        qm = sb("qm", [P, 2, NP, NW, 2, 64])
        kT = sb("kT", [P, 2, NP, T])
        v = sb("v", [P, 2, 3, W])
        nm = sb("nm", [P, 2, NW])
        Z = sb("Z", [P, 2, NW])
        rz = sb("rz", [P, 2, NW])
        E = sb("E", [P, 2, NW, P])
        d = sb("d", [P, 2, NW, P])
        dT = sb("dT", [P, 2, NW, 2, 64])
        OT = sb("OT", [P, 2, NP, T])

        psQ = ps("psQ", [P, 2 * W])
        psS = ps("psS", [P, 2, 512])
        psT = ps("psT", [P, 512])
        psO = ps("psO", [P, T])
        psM = ps("psM", [P, 2, 512])

        U_TQ0, U_TK0, U_V0, U_TQ1, U_TK1, U_V1, U_WO, U_V2, U_HT = range(9)
        USES, PRE = 9, 10
        PEELED = ((U_HT, 0), (U_V0, 0), (U_V1, 0), (U_V2, 0), (U_HT, 1), (U_TQ0, 0), (U_TK0, 0), (U_TQ1, 0),
                  (U_TK1, 0), (U_HT, 2))
        bank = lambda use, half: (use + half) % 2
        misc_full = Signal(sem("misc_full"), USES, PRE)
        misc_free = Signal(sem("misc_free"), USES, PRE)
        qk_full = Signal(sem("qk_full"), QT, 2 * QT)
        squared = Signal(sem("squared"), QT, 2 * QT)
        ss_ready = Signal(sem("ss_ready"), QT, 2 * QT)
        rn_ready = Signal(sem("rn_ready"), QT, 2 * QT)
        parts = Signal(sem("parts"), QT, 2 * QT)
        summed = Signal(sem("summed"), QT, 2 * QT)
        qk_ready = Signal(sem("qk_ready"), QT, 2 * QT)
        scored = Signal(sem("scored"), NP)
        maxed = Signal(sem("maxed"), NP)
        exped = Signal(sem("exped"), NP, 2)
        mixed = Signal(sem("mixed"), NP, 2)
        turned = Signal(sem("turned"), NP, 2)
        evaced = Signal(sem("evaced"), NP, 2)
        pved = Signal(sem("pved"), NP, 2)
        otmoved = Signal(sem("otmoved"), NP, 1)
        stage_full = Signal(sem("stage_full"), 1, 3)
        zeroed = sem("zeroed")
        own = Chain(sem("own"), CHAIN_B, 4)

        block = ctx.enter_context(nc.Block())
        LAST = BATCH // 2

        def f_of(pair, half):
            return F[:, bass.ds((pair * 2 + (half + 1)) * QT, QT), :]

        @block.sync
        def _(sp):
            open_signals(sp)

        @block.gpsimd
        def _(pool):
            def stage(pair, half):
                pool.tensor_copy(staged[:, :, :], f_of(pair, half)).then_inc(stage_full.sem, 1)

            def norms_and_sum(pair, half, t):
                pool.wait_ge(ss_ready.sem, ss_ready.at(pair, half, t + 1))
                pool.tensor_tensor(rn[:, t, :], ss[:, t, :], minus_half[:, 0:2 * H], ALU.pow).then_inc(rn_ready.sem, 1)
                pool.wait_ge(parts.sem, parts.at(pair, half, t + 1))
                pool.wait_ge(qk_ready.sem, qk_ready.at(pair, half, t))
                pool.tensor_tensor(rot[:, :], part[:, 0, :], part[:, 1, :], ALU.add).then_inc(summed.sem, 1)

            stage(0, 0)
            for tile in (hT, qm, OT, dT, v):
                pool.memset(tile[:], 0.0).then_inc(zeroed, 1)
            pool.wait_ge(misc_full.sem, misc_full.early(1))
            stage(0, 1)
            for t in range(QT):
                norms_and_sum(0, -2, t)
            pool.wait_ge(misc_full.sem, misc_full.early(5))
            stage(0, 2)
            for t in range(QT):
                norms_and_sum(0, -1, t)
            with pool.Fori(0, LAST) as pair:
                for half in range(2):
                    pool.wait_ge(misc_full.sem, misc_full.at(pair, half - 1, U_HT + 1))
                    stage(pair, half + 3)
                    for t in range(QT):
                        norms_and_sum(pair, half, t)

        @block.vector
        def _(dve):
            src = psQ[:, :].rearrange("p (a h e) -> p a h e", a=2, e=HD)
            out = part[:, :, :].rearrange("p b (a h e) -> p b a h e", a=2, e=HD)
            tab = lambda a, t, lo, n: a[:, t, :, lo:lo + n].unsqueeze(2).broadcast_to([P, 2, H, n])

            def norms(pair, half, t):
                dve.wait_ge(squared.sem, squared.at(pair, half, t + 1))
                dve.wait_ge(rn_ready.sem, rn_ready.at(pair, half, t - 1))
                own.mark(dve.tensor_reduce(ss[:, t, :], sq[:, :].rearrange("p (h e) -> p h e", e=HD),
                                           axis=AX.X, op=ALU.add))
                own.last()
                dve.tensor_scalar(ss[:, t, :], ss[:, t, :], 1e-24, None, ALU.max).then_inc(ss_ready.sem, 1)

            def rotate(pair, half, t):
                dve.wait_ge(summed.sem, summed.at(pair, half, t))
                dve.tensor_tensor(out[:, 0], src, tab(cos, t, 0, HD), ALU.mult)
                R = HD // 2
                dve.tensor_tensor(out[:, 1, :, :, 0:R], src[:, :, :, R:HD], tab(sin, t, 0, R), ALU.mult)
                dve.tensor_tensor(out[:, 1, :, :, R:HD], src[:, :, :, 0:R], tab(sin, t, R, R), ALU.mult)\
                   .then_inc(parts.sem, 1)

            def scale(pair, half, t, used=None):
                dve.wait_ge(summed.sem, summed.at(pair, half, t + 1))
                dve.wait_ge(rn_ready.sem, rn_ready.at(pair, half, t + 1))
                if used is not None:
                    dve.wait_ge(misc_full.sem, used)
                dve.tensor_tensor(qk[:, t, :].rearrange("p (h e) -> p h e", e=HD),
                                  rot[:, :].rearrange("p (h e) -> p h e", e=HD),
                                  rn[:, t, :].unsqueeze(2).broadcast_to([P, 2 * H, HD]), ALU.mult)\
                   .then_inc(qk_ready.sem, 1)

            def maxima(pair, half, g):
                s = g % 2
                dve.wait_ge(scored.sem, scored.at(pair, half, g + 1))
                dve.tensor_reduce(nm[:, s, :], psS[:, s, :].rearrange("p (w k) -> p w k", k=P), axis=AX.X,
                                  op=ALU.max, negate=True).then_inc(maxed.sem, 1)

            def inverse(pair, half, g):
                s = g % 2
                dve.wait_ge(exped.sem, exped.at(pair, half, g + 1))
                return own.mark(dve.reciprocal(rz[:, s, :], Z[:, s, :]))

            def normalise(pair, half, g, k):
                s = g % 2
                dve.wait_ge(turned.sem, turned.at(pair, half, g - 1))
                own.wait(k)
                dve.tensor_tensor(d[:, s], E[:, s], rz[:, s, :].unsqueeze(2).broadcast_to([P, NW, P]), ALU.mult)\
                   .then_inc(mixed.sem, 1)

            def residual(pair, half, full, m):
                dve.wait_ge(misc_full.sem, full)
                fs = f_of(pair, half - 1)
                dve.tensor_tensor(fs, psM[:, m, 0:T].rearrange("p (t n) -> p t n", t=QT), fs, ALU.add)\
                   .then_inc(misc_free.sem, 1)

            dve.memset(psO[:, :], 0.0).then_inc(zeroed, 1)
            dve.wait_ge(zeroed, 6)
            own.begin(dve, 0, 0)
            own.restart(0)
            for t in range(QT):
                norms(0, -2, t)
                rotate(0, -2, t)
                scale(0, -2, t)
            maxima(0, 0, 0)
            for t in range(QT):
                norms(0, -1, t)
                rotate(0, -1, t)
                if t == 0:
                    scale(0, -1, t, misc_full.early(PRE))
            assert own.k == 4
            own.restart(own.k)
            with dve.Fori(0, LAST) as pair:
                for half in range(2):
                    own.begin(dve, pair, half)
                    for s in range(NP):
                        k = inverse(pair, half, s)
                        maxima(pair, half + (s + 1) // NP, (s + 1) % NP)
                        normalise(pair, half, s, k)
                        if s == 0:
                            scale(pair, half - 1, 1, misc_full.at(pair, half, 0))
                            norms(pair, half, 0)
                        if s == 1:
                            rotate(pair, half, 0)
                        if s == 2:
                            scale(pair, half, 0, misc_full.at(pair, half, U_TK0 + 1))
                            norms(pair, half, 1)
                        if s == 3:
                            residual(pair, half, misc_full.at(pair, half, U_WO + 1), bank(U_WO, half))
                            rotate(pair, half, 1)
                    own.end()
            residual(LAST, 0, misc_full.at(LAST, 0, 1), 0)

        @block.scalar
        def _(act):
            def exps(pair, half, g):
                s = g % 2
                act.wait_ge(maxed.sem, maxed.at(pair, half, g + 1))
                act.wait_ge(mixed.sem, mixed.at(pair, half, g - 1))
                for n in range(NW):
                    ins = act.activation(E[:, s, n, :], psS[:, s, n * P:(n + 1) * P], ACT.Exp, bias=nm[:, s, n:n + 1],
                                         accum_out=Z[:, s, n:n + 1])
                ins.then_inc(exped.sem, 1)

            def evac_d(pair, half, g):
                s = g % 2
                act.wait_ge(turned.sem, turned.at(pair, half, g + 1))
                act.wait_ge(pved.sem, pved.at(pair, half, g - 1))
                act.activation(dT[:, s].rearrange("p w j q -> p (w j q)"), psT[:, :], ACT.Copy)\
                   .then_inc(evaced.sem, 1)

            def move_ot(pair, half, g, p):
                act.wait_ge(pved.sem, pved.at(pair, half, g + 1))
                if g == 0:
                    act.wait_ge(misc_full.sem, misc_full.at(pair, half - 1, U_WO + 1))
                act.activation(OT[:, p, g, :], psO[:, :], ACT.Copy).then_inc(otmoved.sem, 1)

            def square(pair, half, t):
                act.wait_ge(qk_full.sem, qk_full.at(pair, half, t + 1))
                act.wait_ge(ss_ready.sem, ss_ready.at(pair, half, t))
                act.activation(sq[:, :], psQ[:, :], ACT.Square).then_inc(squared.sem, 1)

            def use_copy(use, p, full, m):
                act.wait_ge(misc_full.sem, full)
                if use == U_HT:
                    act.activation(hT[0:64, p, :], psM[0:64, m, 0:T], ACT.Copy)
                    ins = act.activation(hT[64:P, p, 1:T], psM[64:P, m, 0:T - 1], ACT.Copy)
                elif use in (U_V0, U_V1, U_V2):
                    ins = act.activation(v[:, p, (U_V0, U_V1, U_V2).index(use), :], psM[:, m, :], ACT.Copy)
                elif use in (U_TQ0, U_TQ1):
                    n = 2 * (use == U_TQ1)
                    for j in range(2):
                        rows = slice(64 * j, 64 * j + 64)
                        ins = act.activation(qm[rows, p, :, n:n + 2, j, :],
                                             psM[rows, m, :].rearrange("p (g w q) -> p g w q", w=2, q=64), ACT.Copy)
                else:
                    c = P * (use == U_TK1)
                    ins = act.activation(kT[:, p, :, c:c + P], psM[:, m, :].rearrange("p (n t) -> p n t", t=P), ACT.Copy)
                ins.then_inc(misc_free.sem, 1)

            act.wait_ge(zeroed, 6)
            for signal, n in ((exped, 2), (mixed, 2), (turned, 2), (evaced, 2), (pved, 1)):
                act.sem_inc(signal.sem, n)
            for n, (use, batch) in enumerate(PEELED):
                use_copy(use, batch % 2, misc_full.early(n + 1), n % 2)
                if n < 2:
                    square(0, -2, n)
            exps(0, 0, 0)
            for t in range(QT):
                square(0, -1, t)
            with act.Fori(0, LAST) as pair:
                for half in range(2):
                    copy = lambda use: use_copy(use, 1 - half, misc_full.at(pair, half, use + 1), bank(use, half))
                    for s in range(NP):
                        exps(pair, half + (s + 1) // NP, (s + 1) % NP)
                        if s in (0, 2):
                            square(pair, half, s // 2)
                        copy((U_TQ0, U_TQ1, U_V1, U_V2)[s])
                        evac_d(pair, half, s)
                        if s < 2:
                            copy((U_TK0, U_TK1)[s])
                        if s == 3:
                            copy(U_HT)
                        move_ot(pair, half - (s == 0), (s - 1) % NP, 1 - half if s == 0 else half)
                        if s == 0:
                            act.wait_ge(pved.sem, pved.at(pair, half, 0))
                            copy(U_V0)
            move_ot(LAST, -1, NP - 1, 1)

        @block.tensor
        def _(pe):
            def scores(pair, half, g):
                s, p = g % 2, half % 2
                pe.wait_ge(exped.sem, exped.at(pair, half, g - 1))
                pe.matmul(psS[:, s, :], identb[:, :], behind[:, :], start=True, stop=False)
                for n in range(NW):
                    ins = pe.matmul(psS[:, s, n * P:(n + 1) * P], qm[:, p, g, n].rearrange("p j q -> p (j q)"),
                                    kT[:, p, g, KEYS[n]:KEYS[n] + P], start=False, stop=(n == NW - 1))
                ins.then_inc(scored.sem, 1)

            def turn(pair, half, g):
                s = g % 2
                pe.wait_ge(mixed.sem, mixed.at(pair, half, g + 1))
                pe.wait_ge(evaced.sem, evaced.at(pair, half, g))
                for n in range(NW):
                    ins = pe.transpose(psT[:, n * P:(n + 1) * P], d[:, s, n, :], ident[:, :])
                ins.then_inc(turned.sem, 1)

            def outputs(pair, half, g):
                s, p = g % 2, half % 2
                pe.wait_ge(evaced.sem, evaced.at(pair, half, g + 1))
                pe.wait_ge(otmoved.sem, otmoved.at(pair, half, g))
                for j in range(2):
                    h = 2 * g + j
                    out = psO[64 * j:64 * j + 64, :]
                    vh = lambda t: v[:, p, t, h * HD:(h + 1) * HD]
                    pe.matmul(out[:, 0:P], vh(0), dT[:, s, 0:2, j, :], start=True, stop=True)
                    pe.matmul(out[:, P:192], vh(1), dT[:, s, 2, j, :], start=True, stop=True)
                    ins = pe.matmul(out[:, 192:T], vh(2), dT[:, s, 3, j, :], start=True, stop=True)
                ins.then_inc(pved.sem, 1)

            def project(pair, half, t):
                p = half % 2
                pe.wait_ge(parts.sem, parts.at(pair, half, t))
                for n in range(2):
                    ins = pe.matmul(psQ[:, n * W:(n + 1) * W], hT[:, p, t * P:(t + 1) * P],
                                    wqk[:, n * W:(n + 1) * W], start=True, stop=True)
                ins.then_inc(qk_full.sem, 1)

            def use_misc(use, free, p, m):
                out = psM[:, m, :]
                pe.wait_ge(misc_free.sem, free)
                if use == U_HT:
                    for t in range(QT):
                        ins = pe.transpose(out[:, t * P:(t + 1) * P], staged[:, t, :], ident[:, :])
                elif use == U_WO:
                    for t in range(QT):
                        for n in range(NP):
                            ins = pe.matmul(out[:, t * P:(t + 1) * P], OT[:, p, n, t * P:(t + 1) * P], wo[:, n, :],
                                            start=(n == 0), stop=(n == NP - 1))
                elif use in (U_V0, U_V1, U_V2):
                    t = (U_V0, U_V1, U_V2).index(use) * 64
                    ins = pe.matmul(out, hT[:, p, t:t + P], wv[:, :], start=True, stop=True)
                else:
                    t, a = int(use in (U_TQ1, U_TK1)), int(use in (U_TK0, U_TK1))
                    for n in range(NP):
                        ins = pe.transpose(out[:, n * P:(n + 1) * P],
                                           qk[:, t, a * W + n * P:a * W + (n + 1) * P], ident[:, :])
                ins.then_inc(misc_full.sem, 1)

            pe.wait_ge(zeroed, 6)
            for n, (use, batch) in enumerate(PEELED):
                if n == 1:
                    pe.wait_ge(misc_free.sem, misc_free.early(1))
                    project(0, -2, 0)
                if n == 2:
                    project(0, -2, 1)
                if use == U_HT:
                    pe.wait_ge(stage_full.sem, stage_full.early(1 + batch))
                if use in (U_TQ0, U_TQ1):
                    pe.wait_ge(qk_ready.sem, qk_ready.early(1 + (use == U_TQ1)))
                if n < 2:
                    use_misc(use, misc_free.early(0), 0, n)
                else:
                    use_misc(use, misc_free.early(n - 1), 0, n % 2)
            pe.wait_ge(misc_free.sem, misc_free.early(PRE))
            scores(0, 0, 0)
            scores(0, 0, 1)
            for t in range(QT):
                project(0, -1, t)
            project(0, 0, 0)
            with pe.Fori(0, LAST) as pair:
                for half in range(2):
                    use = lambda u: use_misc(u, misc_free.at(pair, half, u - 1 + (u in (U_V2, U_HT))), 1 - half,
                                             bank(u, half))
                    for s in range(NP):
                        if s == 2:
                            pe.wait_ge(misc_free.sem, misc_free.at(pair, half, U_TK1 + 1))
                        scores(pair, half + (s + 2) // NP, (s + 2) % NP)
                        if s < 2:
                            pe.wait_ge(qk_ready.sem, qk_ready.at(pair, half - 1, s + 1))
                        use((U_TQ0, U_TQ1, U_V1, U_V2)[s])
                        turn(pair, half, s)
                        if s == 2:
                            pe.wait_ge(otmoved.sem, otmoved.at(pair, half, 0))
                        if s == 3:
                            pe.wait_ge(stage_full.sem, stage_full.at(pair, half, 1))
                        use((U_TK0, U_TK1, U_WO, U_HT)[s])
                        outputs(pair, half - 1 if s == 0 else half, (s - 1) % NP)
                        if s == 0:
                            use(U_V0)
                        if s == 1:
                            project(pair, half, 1)
                        if s == 3:
                            pe.wait_ge(misc_free.sem, misc_free.at(pair, half, U_HT + 1))
                            project(pair, half + 1, 0)
            outputs(LAST, -1, NP - 1)
            pe.wait_ge(otmoved.sem, otmoved.at(LAST, 0, 0))
            use_misc(U_WO, misc_free.at(LAST, 0, 0), 1, 0)


def feed_forward(nc, name, F, consts, w):
    NT = 4
    N = NT * P
    PAIRS = TILES // NT // 2
    HID = 341
    parts = [(j, min(P, HID - P * j)) for j in range((HID + P - 1) // P)]
    J = len(parts)
    ident, minus_half = consts["ident"], consts["minus_half"]
    w1, b1, w2, b2, lg, lb = (w[k] for k in ("w1", "b1", "w2", "b2", "ln_g", "ln_b"))

    with ExitStack() as ctx:
        sb = lambda n, shape, dt=FP32: ctx.enter_context(nc.sbuf_tensor(name + n, shape, dt))
        ps = lambda n, shape: ctx.enter_context(nc.psum_tensor(name + n, shape, FP32))
        sem = lambda n: nc.alloc_semaphore(name + n)
        z = sb("z", [P, 2, NT, D])
        st = sb("st", [P, NT, 6])
        mv = sb("mv", [P, NT, 2])
        rs = sb("rs", [P, NT])
        xn = sb("xn", [P, NT, D])
        hT = sb("hT", [P, N])
        gg = sb("gg", [P, J, N])
        u = sb("u", [P, J, N])
        fb = sb("fb", [P, NT, D])
        psG = ps("psG", [P, J, N])
        psA = ps("psA", [P, J, N])
        psX = ps("psX", [P, N])
        psY = ps("psY", [P, N])

        shifted = [sem("shifted"), sem("shifted_odd")]
        g_full = Signal(sem("g_full"), J)
        a_full = Signal(sem("a_full"), J)
        gelued = Signal(sem("gelued"), J)
        gated = Signal(sem("gated"), J)
        var_ready = Signal(sem("var_ready"), 1, 1)
        rs_ready = Signal(sem("rs_ready"), 1, 1)
        xn_ready = Signal(sem("xn_ready"), 1, 1)
        x_full = Signal(sem("x_full"), 1, 1)
        h_ready = Signal(sem("h_ready"), 1, 1)
        y_full = Signal(sem("y_full"), 1)
        added = Signal(sem("added"), 1)
        fb_ready = Signal(sem("fb_ready"), 1)
        zeroed = sem("zeroed")
        own = Chain(sem("own"), CHAIN_F, 2)
        block = ctx.enter_context(nc.Block())

        def f_of(pair, half):
            return F[:, bass.ds((pair * 2 + half) * NT + QT, NT), :]

        def z_landed(eng, pair, half):
            eng.wait_ge(shifted[half % 2], (pair + half // 2) * 48 + 48)

        @block.sync
        def _(sp):
            open_signals(sp)
            def shift(pair, half):
                done = shifted[half % 2]
                p, fs = half % 2, f_of(pair, half)
                sp.dma_start(z[:, p, :, 0:64], fs[:, :, 0:64]).then_inc(done, 16)
                sp.dma_start(z[1:P, p, :, 64:D], fs[0:P - 1, :, 64:D]).then_inc(done, 16)
                sp.dma_start(z[0:1, p, 1::2, 64:D], fs[P - 1:P, 0::2, 64:D]).then_inc(done, 16)

            sp.wait_ge(zeroed, 1)
            shift(0, 0)
            shift(0, 1)
            with sp.Fori(0, PAIRS - 1) as pair:
                for half in range(2):
                    sp.wait_ge(xn_ready.sem, xn_ready.at(pair, half, 0))
                    shift(pair, half + 2)
            sp.wait_ge(xn_ready.sem, xn_ready.at(PAIRS - 1, 0, 0))
            shift(PAIRS - 1, 2)

        @block.gpsimd
        def _(pool):
            pool.memset(z[0:1, :, 0::2, 64:D], 0.0).then_inc(zeroed, 1)

            def rstd(pair, half, k):
                pool.wait_ge(var_ready.sem, var_ready.at(pair, half, k))
                pool.tensor_tensor(rs[:, :], mv[:, :, 1], minus_half[:, 0:NT], ALU.pow).then_inc(rs_ready.sem, 1)

            rstd(0, 0, 0)
            with pool.Fori(0, PAIRS) as pair:
                for half in range(2):
                    rstd(pair, half, 1)
                    pool.wait_ge(added.sem, added.at(pair, half, 0))
                    pool.tensor_tensor(fb[:, :, :], f_of(pair, half), b2[:, :].unsqueeze(1).broadcast_to([P, NT, D]),
                                       ALU.add).then_inc(fb_ready.sem, 1)

        @block.vector
        def _(dve):
            def variance(pair, half):
                z_landed(dve, pair, half)
                for t in range(NT):
                    ins = dve.bn_stats(st[:, t, :], z[:, half % 2, t, :])
                own.mark(ins)
                own.last()
                apart(dve, APART["dve"])
                for t in range(NT):
                    ins = dve.bn_aggr(mv[:, t, :], st[:, t, :])
                own.mark(ins)
                own.last()
                dve.tensor_scalar(mv[:, :, 1], mv[:, :, 1], EPS_LN, None, ALU.add).then_inc(var_ready.sem, 1)

            def normalise(pair, half, k):
                dve.wait_ge(rs_ready.sem, rs_ready.at(pair, half, k))
                if k:
                    dve.wait_ge(x_full.sem, x_full.at(pair, half, 0))
                for t in range(NT):
                    ins = dve.tensor_scalar(xn[:, t, :], z[:, (half + k) % 2, t, :], mv[:, t, 0:1], rs[:, t:t + 1],
                                            ALU.subtract, ALU.mult)
                ins.then_inc(xn_ready.sem, 1)

            own.begin(dve, 0, 0)
            own.restart(0)
            variance(0, 0)
            own.restart(own.k)
            normalise(0, 0, 0)
            with dve.Fori(0, PAIRS) as pair:
                for half in range(2):
                    own.begin(dve, pair, half)
                    variance(pair, half + 1)
                    for j, m in parts:
                        dve.wait_ge(gelued.sem, gelued.at(pair, half, j + 1))
                        dve.wait_ge(a_full.sem, a_full.at(pair, half, j + 1))
                        dve.wait_ge(y_full.sem, y_full.at(pair, half, 0))
                        dve.scalar_tensor_tensor(out=u[0:m, j, :], in0=psA[0:m, j, :], scalar=b1[0:m, j:j + 1],
                                                 in1=gg[0:m, j, :], op0=ALU.add, op1=ALU.mult).then_inc(gated.sem, 1)
                        if j == 0:
                            normalise(pair, half, 1)
                    dve.wait_ge(y_full.sem, y_full.at(pair, half, 1))
                    dve.wait_ge(fb_ready.sem, fb_ready.at(pair, half, 1))
                    dve.tensor_tensor(f_of(pair, half), psY[:, :].rearrange("p (t n) -> p t n", t=NT), fb[:, :, :],
                                      ALU.add).then_inc(added.sem, 1)
                    own.end()

        @block.scalar
        def _(act):
            def take_x(full):
                act.wait_ge(x_full.sem, full)
                act.activation(hT[:, :], psX[:, :], ACT.Identity, scale=lg[:, 0:1], bias=lb[:, 0:1])\
                   .then_inc(h_ready.sem, 1)

            take_x(x_full.early(1))
            with act.Fori(0, PAIRS) as pair:
                for half in range(2):
                    for j, m in parts:
                        act.wait_ge(g_full.sem, g_full.at(pair, half, j + 1))
                        act.wait_ge(gated.sem, gated.at(pair, half, 0))
                        act.activation(gg[0:m, j, :], psG[0:m, j, :], ACT.Gelu, bias=b1[0:m, J + j:J + j + 1])\
                           .then_inc(gelued.sem, 1)
                    take_x(x_full.at(pair, half, 1))

        @block.tensor
        def _(pe):
            def turn_x(full):
                pe.wait_ge(xn_ready.sem, full)
                for t in range(NT):
                    ins = pe.transpose(psX[:, t * P:(t + 1) * P], xn[:, t, :], ident[:, :])
                ins.then_inc(x_full.sem, 1)

            turn_x(xn_ready.early(1))
            with pe.Fori(0, PAIRS) as pair:
                for half in range(2):
                    pe.wait_ge(h_ready.sem, h_ready.at(pair, half, 0))
                    for j, m in parts:
                        pe.wait_ge(gelued.sem, gelued.at(pair, half, 0))
                        pe.matmul(psG[0:m, j, :], w1[:, HID + j * P:HID + j * P + m], hT[:, :], start=True, stop=True)\
                          .then_inc(g_full.sem, 1)
                        pe.wait_ge(gated.sem, gated.at(pair, half, 0))
                        pe.matmul(psA[0:m, j, :], w1[:, j * P:j * P + m], hT[:, :], start=True, stop=True)\
                          .then_inc(a_full.sem, 1)
                    turn_x(xn_ready.at(pair, half, 1))
                    pe.wait_ge(gated.sem, gated.at(pair, half, J))
                    pe.wait_ge(added.sem, added.at(pair, half, 0))
                    for t in range(NT):
                        for j, m in parts:
                            ins = pe.matmul(psY[:, t * P:(t + 1) * P], u[0:m, j, t * P:(t + 1) * P], w2[0:m, j, :],
                                            start=(j == 0), stop=(j == J - 1))
                    ins.then_inc(y_full.sem, 1)


def state_space(nc, X, F, consts, w):
    NS, GROUPS = 32, 4
    SEQ = BATCH // GROUPS
    N = SEQ * T
    LEVELS = T.bit_length() - 1
    ident, minus_half = consts["ident"], consts["minus_half"]
    win, bin_, bm, am, amT, cT, dv = (w[k] for k in ("W_in", "b_in", "Bm", "A", "AT", "C", "D"))

    with ExitStack() as ctx:
        sb = lambda n, shape, dt=FP32: ctx.enter_context(nc.sbuf_tensor("s_" + n, shape, dt))
        ps = lambda n, shape: ctx.enter_context(nc.psum_tensor("s_" + n, shape, FP32))
        sem = lambda n: nc.alloc_semaphore("s_" + n)
        xT = sb("xT", [P, 2, T])
        U = sb("U", [P, N])
        Hs = sb("H", [P, SEQ, T])
        pw = sb("pw", [P, 2, 2, P])
        y = sb("y", [P, QT, D])
        yn = sb("yn", [P, QT, D])
        st = sb("st", [P, QT, 6])
        mv = sb("mv", [P, QT, 2])
        rs = sb("rs", [P, QT])
        psX = ps("psX", [P, 2, 512])
        psU = ps("psU", [P, 2, 512])
        psH = ps("psH", [P, 2, 512])
        psP = ps("psP", [P, 512])
        psY = ps("psY", [P, 512])

        x_full, xT_ready, u_full, u_ready = (
            sem(n) for n in ("x_full", "xT_ready", "u_full", "u_ready"))
        b_full, h_ready, level_full, p_full, p_ready = (
            sem(n) for n in ("b_full", "h_ready", "level_full", "p_full", "p_ready"))
        y_full, y_ready, var_ready, rs_ready = (sem(n) for n in ("y_full", "y_ready", "var_ready", "rs_ready"))
        own = sem("own")
        block = ctx.enter_context(nc.Block())

        def f_of(b):
            return F[:, QT + b * QT:QT + (b + 1) * QT, :]

        @block.gpsimd
        def _(pool):
            for b in range(BATCH):
                pool.wait_ge(var_ready, b + 1)
                pool.tensor_tensor(rs[:, :], mv[:, :, 1], minus_half[:, 0:QT], ALU.pow).then_inc(rs_ready, 1)

        @block.scalar
        def _(act):
            for b in range(BATCH):
                act.wait_ge(x_full, b + 1)
                if b >= 2:
                    act.wait_ge(u_full, b - 1)
                act.activation(xT[:, b % 2, :], psX[:, b % 2, 0:T], ACT.Copy).then_inc(xT_ready, 1)
            for c in range(2):
                act.wait_ge(u_full, BATCH)
                act.activation(U[:, c * 512:(c + 1) * 512], psU[:, c, :], ACT.Identity, bias=bin_[:, 0:1])\
                   .then_inc(u_ready, 1)
            for l in range(LEVELS - 1):
                act.wait_ge(p_full, l + 1)
                if l >= 1:
                    act.wait_ge(level_full, 2 * l)
                act.activation(pw[:, (l + 1) % 2, :, :], psP[:, 0:T].rearrange("p (a n) -> p a n", a=2), ACT.Copy)\
                   .then_inc(p_ready, 1)

        @block.vector
        def _(dve):
            dve.tensor_copy(pw[:, 0, 0, :], am[:, :]).then_inc(p_ready, 1)
            dve.tensor_copy(pw[:, 0, 1, :], amT[:, :]).then_inc(p_ready, 1)
            for c in range(2):
                dve.wait_ge(b_full, c + 1)
                dve.tensor_copy(Hs[:, 2 * c:2 * c + 2, :], psH[:, c, :].rearrange("p (a t) -> p a t", a=2))\
                   .then_inc(h_ready, 1)
            for l in range(LEVELS):
                k = 2 ** l
                for c in range(2):
                    dve.wait_ge(level_full, 2 * l + c + 1)
                    dve.wait_ge(h_ready, 2 * l + c + 1)
                    hs = Hs[:, 2 * c:2 * c + 2, k:T]
                    dve.tensor_tensor(hs, psH[:, c, 0:2 * (T - k)].rearrange("p (a t) -> p a t", a=2), hs, ALU.add)\
                       .then_inc(h_ready, 1)
            marks = 0
            for b in range(BATCH):
                dve.wait_ge(y_full, b + 1)
                for t in range(QT):
                    ins = dve.tensor_tensor(y[:, t, :], psY[:, t * P:(t + 1) * P], dv[:, :], ALU.add)
                ins.then_inc(y_ready, 1)
                dve.wait_ge(y_ready, b + 1)
                for t in range(QT):
                    ins = dve.bn_stats(st[:, t, :], y[:, t, :])
                ins.then_inc(own, 1)
                dve.wait_ge(own, marks + 1)
                for t in range(QT):
                    ins = dve.bn_aggr(mv[:, t, :], st[:, t, :])
                ins.then_inc(own, 1)
                dve.wait_ge(own, marks + 2)
                dve.tensor_scalar(mv[:, :, 1], mv[:, :, 1], EPS_LN, None, ALU.add).then_inc(var_ready, 1)
                dve.wait_ge(rs_ready, b + 1)
                for t in range(QT):
                    ins = dve.tensor_scalar(yn[:, t, :], y[:, t, :], mv[:, t, 0:1], rs[:, t:t + 1],
                                            ALU.subtract, ALU.mult)
                ins.then_inc(own, 1)
                dve.wait_ge(own, marks + 3)
                xs = X[:, QT + b * QT:QT + (b + 1) * QT, :]
                dve.tensor_tensor(xs, xs, yn[:, :, :], ALU.add)
                marks += 3

        @block.tensor
        def _(pe):
            def inputs(b):
                g, j = divmod(b, SEQ)
                pe.wait_ge(xT_ready, b + 1)
                pe.matmul(psU[NS * g:NS * g + NS, j // 2, (j % 2) * T:(j % 2) * T + T], win[:, :], xT[:, b % 2, :],
                          start=True, stop=True).then_inc(u_full, 1)

            for b in range(BATCH):
                if b >= 2:
                    pe.wait_ge(xT_ready, b - 1)
                for t in range(QT):
                    ins = pe.transpose(psX[:, b % 2, t * P:(t + 1) * P], f_of(b)[:, t, :], ident[:, :])
                ins.then_inc(x_full, 1)
                if b >= 1:
                    inputs(b - 1)
            inputs(BATCH - 1)
            for c in range(2):
                pe.wait_ge(u_ready, c + 1)
                pe.matmul(psH[:, c, :], bm[:, :], U[:, c * 512:(c + 1) * 512], start=True, stop=True).then_inc(b_full, 1)
            pe.wait_ge(p_ready, 2)
            for l in range(LEVELS):
                k = 2 ** l
                if l:
                    pe.wait_ge(p_ready, 2 + l)
                a, aT = pw[:, l % 2, 0, :], pw[:, l % 2, 1, :]
                for c in range(2):
                    pe.wait_ge(h_ready, 2 * l + c + 1)
                    pe.matmul(psH[:, c, 0:2 * (T - k)], a, Hs[:, 2 * c:2 * c + 2, 0:T - k], start=True, stop=True)\
                      .then_inc(level_full, 1)
                    if c == 0 and l < LEVELS - 1:
                        pe.matmul(psP[:, 0:P], aT, a, start=True, stop=True)
                        pe.matmul(psP[:, P:T], a, aT, start=True, stop=True).then_inc(p_full, 1)
            pe.wait_ge(h_ready, 2 * LEVELS + 2)
            for b in range(BATCH):
                g, j = divmod(b, SEQ)
                if b:
                    pe.wait_ge(y_ready, b)
                for t in range(QT):
                    rows = slice(NS * g, NS * g + NS)
                    ins = pe.matmul(psY[:, t * P:(t + 1) * P], Hs[rows, j, t * P:(t + 1) * P], cT[rows, :],
                                    start=True, stop=True)
                ins.then_inc(y_full, 1)


def mixture_of_experts(nc, X, F, out, consts, w):
    NT = 4
    N = NT * P
    PAIRS = TILES // NT // 2
    NE, HID = 8, 256
    J = HID // P
    ident, minus_half, eid = consts["ident"], consts["minus_half"], consts["expert_id"]
    wr, wg, wu, wd = w["router"], w["gate"], w["up"], w["down"]

    with ExitStack() as ctx:
        sb = lambda n, shape, dt=FP32: ctx.enter_context(nc.sbuf_tensor("mx_" + n, shape, dt))
        ps = lambda n, shape: ctx.enter_context(nc.psum_tensor("mx_" + n, shape, FP32))
        sem = lambda n: nc.alloc_semaphore("mx_" + n)
        staged = sb("staged", [P, NT, D])
        hT = sb("hT", [P, 2, N])
        lo = sb("lo", [P, NT, NE])
        top = sb("top", [P, NT, 8])
        idx = sb("idx", [P, NT, 8], mybir.dt.uint32)
        idf = sb("idf", [P, NT, 2])
        sg = sb("sg", [P, NT, 2])
        gs = sb("gs", [P, NT])
        gate = sb("gate", [P, 2, NT, NE])
        pick = sb("pick", [P, NT, NE])
        sl = sb("sl", [P, 2, J, N])
        h = sb("h", [P, 2, J, N])
        Y = sb("Y", [P, NT, D])
        yn = sb("yn", [P, NT, D])
        res = sb("res", [P, 2, NT, D])
        st = sb("st", [P, NT, 6])
        mv = sb("mv", [P, NT, 2])
        rs = sb("rs", [P, NT])
        psG = ps("psG", [P, J, N])
        psU = ps("psU", [P, J, N])
        psY = ps("psY", [P, 2, N])
        psX = ps("psX", [P, N])
        psR = ps("psR", [P, 512])

        stage_full = Signal(sem("stage_full"), 1, 1)
        x_full = Signal(sem("x_full"), 1, 1)
        h_ready = Signal(sem("h_ready"), 1, 1)
        r_full = Signal(sem("r_full"), 1, 1)
        picked = Signal(sem("picked"), 1, 1)
        expd = Signal(sem("expd"), 1, 1)
        gated = Signal(sem("gated"), 1, 1)
        g_full = Signal(sem("g_full"), NE * J)
        u_full = Signal(sem("u_full"), NE * J)
        silued = Signal(sem("silued"), NE * J)
        h_full = Signal(sem("h_full"), NE * J)
        y_full = Signal(sem("y_full"), NE)
        y_used = Signal(sem("y_used"), NE)
        var_ready = Signal(sem("var_ready"), 1)
        rs_ready = Signal(sem("rs_ready"), 1)
        res_ready = Signal(sem("res_ready"), 1)
        stored = [sem("stored_even"), sem("stored_odd")]
        own = Chain(sem("own"), CHAIN_M, CHAIN_M_PRE)
        block = ctx.enter_context(nc.Block())

        def tiles(a, pair, half):
            return a[:, bass.ds((pair * 2 + half) * NT + QT, NT), :]

        @block.sync
        def _(sp):
            open_signals(sp)
            o = out.rearrange("b (t p) d -> p (b t) d", p=P)
            for s in stored:
                sp.sem_inc(s, 1)
            with sp.Fori(0, PAIRS) as pair:
                for half in range(2):
                    sp.wait_ge(res_ready.sem, res_ready.at(pair, half, 1))
                    sp.dma_start(o[:, bass.ds((pair * 2 + half) * NT, NT), :], res[:, half, :, :])\
                      .then_inc(stored[half], 16)
            for s in stored:
                sp.wait_ge(s, 16 * PAIRS + 1)

        @block.gpsimd
        def _(pool):
            pool.tensor_copy(staged[:, :, :], tiles(F, 0, 0)).then_inc(stage_full.sem, 1)
            with pool.Fori(0, PAIRS) as pair:
                for half in range(2):
                    pool.wait_ge(x_full.sem, x_full.at(pair, half, 0))
                    pool.tensor_copy(staged[:, :, :], tiles(F, pair, half + 1)).then_inc(stage_full.sem, 1)
                    pool.wait_ge(var_ready.sem, var_ready.at(pair, half, 1))
                    pool.tensor_tensor(rs[:, :], mv[:, :, 1], minus_half[:, 0:NT], ALU.pow).then_inc(rs_ready.sem, 1)

        @block.scalar
        def _(act):
            def prepare(pair, half):
                act.wait_ge(x_full.sem, x_full.at(pair, half, 0))
                act.activation(hT[:, half % 2, :], psX[:, :], ACT.Copy).then_inc(h_ready.sem, 1)

            def sigmoid_of(pair, half):
                act.wait_ge(picked.sem, picked.at(pair, half, 0))
                act.activation(sg[:, :, :], top[:, :, 0:2], ACT.Exp, scale=-1.0).then_inc(expd.sem, 1)

            prepare(0, 0)
            sigmoid_of(0, 0)
            with act.Fori(0, PAIRS) as pair:
                for half in range(2):
                    for e in range(NE):
                        for j in range(J):
                            k = e * J + j
                            act.wait_ge(g_full.sem, g_full.at(pair, half, k + 1))
                            act.wait_ge(h_full.sem, h_full.at(pair, half, max(k + 1 - 2 * J, 0)))
                            act.activation(sl[:, e % 2, j, :], psG[:, j, :], ACT.Silu).then_inc(silued.sem, 1)
                        if e == 1:
                            prepare(pair, half + 1)
                        if e == 6:
                            sigmoid_of(pair, half + 1)

        @block.vector
        def _(dve):
            def choose(pair, half):
                dve.wait_ge(r_full.sem, r_full.at(pair, half, 0))
                own.mark(dve.tensor_copy(lo[:, :, :], psR[:, 0:NT * NE].rearrange("p (t e) -> p t e", t=NT)))
                own.last()
                apart(dve, APART["dve"])
                for t in range(NT):
                    ins = dve.max(top[:, t, :], lo[:, t, :])
                ins.then_inc(picked.sem, 1)
                dve.wait_ge(picked.sem, picked.at(pair, half, 0))
                apart(dve, APART["dve"])
                for t in range(NT):
                    ins = dve.max_index(idx[:, t, :], top[:, t, :], lo[:, t, :])
                own.mark(ins)
                own.last()
                own.mark(dve.tensor_copy(idf[:, :, :], idx[:, :, 0:2]))

            def gates(pair, half):
                p = half % 2
                dve.wait_ge(expd.sem, expd.at(pair, half, 0))
                own.mark(dve.tensor_scalar(sg[:, :, :], sg[:, :, :], 1.0, None, ALU.add))
                own.last()
                own.mark(dve.reciprocal(sg[:, :, :], sg[:, :, :]))
                own.last()
                own.mark(dve.tensor_tensor(gs[:, :], sg[:, :, 0], sg[:, :, 1], ALU.add))
                own.last()
                own.mark(dve.tensor_scalar(gs[:, :], gs[:, :], 1e-10, None, ALU.add))
                own.last()
                own.mark(dve.reciprocal(gs[:, :], gs[:, :]))
                own.last()
                own.mark(dve.tensor_tensor(sg[:, :, :], sg[:, :, :], gs[:, :].unsqueeze(2).broadcast_to([P, NT, 2]),
                                           ALU.mult))
                own.last()
                for t in range(NT):
                    dve.tensor_scalar(gate[:, p, t, :], eid[:, :], idf[:, t, 0:1], sg[:, t, 0:1],
                                      ALU.is_equal, ALU.mult)
                    ins = dve.tensor_scalar(pick[:, t, :], eid[:, :], idf[:, t, 1:2], sg[:, t, 1:2],
                                            ALU.is_equal, ALU.mult)
                own.mark(ins)
                own.last()
                dve.tensor_tensor(gate[:, p, :, :], gate[:, p, :, :], pick[:, :, :], ALU.add).then_inc(gated.sem, 1)

            def accumulate(pair, half, e):
                p = half % 2
                dve.wait_ge(y_full.sem, y_full.at(pair, half, e + 1))
                if e == 0:
                    dve.wait_ge(gated.sem, gated.at(pair, half, 0))
                else:
                    own.last()
                for t in range(NT):
                    src, g = psY[:, e % 2, t * P:(t + 1) * P], gate[:, p, t, e:e + 1]
                    if e == 0:
                        ins = dve.tensor_scalar(Y[:, t, :], src, g, None, ALU.mult)
                    else:
                        ins = dve.scalar_tensor_tensor(out=Y[:, t, :], in0=src, scalar=g, in1=Y[:, t, :],
                                                       op0=ALU.mult, op1=ALU.add)
                ins.then_inc(y_used.sem, 1)
                dve.wait_ge(y_used.sem, y_used.at(pair, half, e + 1))

            def finish(pair, half):
                for t in range(NT):
                    ins = dve.bn_stats(st[:, t, :], Y[:, t, :])
                own.mark(ins)
                own.last()
                apart(dve, APART["dve"])
                for t in range(NT):
                    ins = dve.bn_aggr(mv[:, t, :], st[:, t, :])
                own.mark(ins)
                own.last()
                dve.tensor_scalar(mv[:, :, 1], mv[:, :, 1], EPS_LN, None, ALU.add).then_inc(var_ready.sem, 1)
                dve.wait_ge(rs_ready.sem, rs_ready.at(pair, half, 1))
                for t in range(NT):
                    ins = dve.tensor_scalar(yn[:, t, :], Y[:, t, :], mv[:, t, 0:1], rs[:, t:t + 1],
                                            ALU.subtract, ALU.mult)
                own.mark(ins)
                own.last()
                dve.wait_ge(stored[half % 2], pair * 16 + 1)
                dve.tensor_tensor(res[:, half % 2, :, :], yn[:, :, :], tiles(X, pair, half), ALU.add)\
                   .then_inc(res_ready.sem, 1)

            own.begin(dve, 0, 0)
            own.restart(0)
            choose(0, 0)
            gates(0, 0)
            own.restart(own.k)
            assert own.k == CHAIN_M_PRE, own.k
            with dve.Fori(0, PAIRS) as pair:
                for half in range(2):
                    own.begin(dve, pair, half)
                    for e in range(NE):
                        for j in range(J):
                            k = e * J + j
                            dve.wait_ge(silued.sem, silued.at(pair, half, k + 1))
                            dve.wait_ge(u_full.sem, u_full.at(pair, half, k + 1))
                            dve.wait_ge(y_full.sem, y_full.at(pair, half, max(e - 1, 0)))
                            dve.tensor_tensor(h[:, e % 2, j, :], psU[:, j, :], sl[:, e % 2, j, :], ALU.mult)\
                               .then_inc(h_full.sem, 1)
                        if e >= 1:
                            accumulate(pair, half, e - 1)
                        if e == 5:
                            choose(pair, half + 1)
                        if e == 7:
                            gates(pair, half + 1)
                    accumulate(pair, half, NE - 1)
                    finish(pair, half)
                    own.end()

        @block.tensor
        def _(pe):
            def prepare(pair, half):
                pe.wait_ge(stage_full.sem, stage_full.at(pair, half, 0))
                for t in range(NT):
                    ins = pe.transpose(psX[:, t * P:(t + 1) * P], staged[:, t, :], ident[:, :])
                ins.then_inc(x_full.sem, 1)

            def route(pair, half):
                pe.wait_ge(h_ready.sem, h_ready.at(pair, half, 0))
                for t in range(NT):
                    ins = pe.matmul(psR[:, t * NE:(t + 1) * NE], hT[:, half % 2, t * P:(t + 1) * P], wr[:, :],
                                    start=True, stop=True)
                ins.then_inc(r_full.sem, 1)

            def down(pair, half, e):
                pe.wait_ge(h_full.sem, h_full.at(pair, half, (e + 1) * J))
                pe.wait_ge(y_used.sem, y_used.at(pair, half, max(e - 1, 0)))
                for t in range(NT):
                    for j in range(J):
                        ins = pe.matmul(psY[:, e % 2, t * P:(t + 1) * P], h[:, e % 2, j, t * P:(t + 1) * P],
                                        wd[:, e, j, :], start=(j == 0), stop=(j == J - 1))
                ins.then_inc(y_full.sem, 1)

            prepare(0, 0)
            route(0, 0)
            with pe.Fori(0, PAIRS) as pair:
                for half in range(2):
                    x = hT[:, half % 2, :]
                    for e in range(NE):
                        for j in range(J):
                            k = e * J + j
                            cols = slice(j * P, (j + 1) * P)
                            pe.wait_ge(silued.sem, silued.at(pair, half, max(k + 1 - J, 0)))
                            pe.matmul(psG[:, j, :], wg[:, e, cols], x, start=True, stop=True).then_inc(g_full.sem, 1)
                            pe.wait_ge(h_full.sem, h_full.at(pair, half, max(k + 1 - J, 0)))
                            pe.matmul(psU[:, j, :], wu[:, e, cols], x, start=True, stop=True).then_inc(u_full.sem, 1)
                        if e >= 1:
                            down(pair, half, e - 1)
                        if e == 1:
                            prepare(pair, half + 1)
                        if e == 4:
                            pe.wait_ge(picked.sem, picked.at(pair, half, 0))
                            route(pair, half + 1)
                    down(pair, half, NE - 1)


def build(nc, ins, consts_in, out, stop=None):
    with ExitStack() as ctx:
        sb = lambda name, shape, dt=FP32: ctx.enter_context(nc.sbuf_tensor(name, shape, dt))
        sem = lambda name: nc.alloc_semaphore(name)
        APART["dve"], APART["pool"] = sb("apart_dve", [P, 1])[:, :], sb("apart_pool", [P, 1])[:, :]
        X = sb("X", [P, TILES + 2 * QT, D])
        F = sb("F", [P, QT + TILES + 4 * QT, D])

        first, later = [], []
        first.append((X[:, QT:QT + TILES, :], ins["x"].rearrange("b (t p) d -> p (b t) d", p=P)))
        wA = {}
        for k in ("Wq", "Wk1", "Wk2", "Wv", "Wo"):
            wA[k] = sb(k, [P, D])
            first.append((wA[k][:, :], ins[k]))
        consts = {}
        for k, shape, group in (("ident", [P, P], first), ("headrow", [P, 16], first), ("expert_id", [P, 8], later)):
            consts[k] = sb(k, shape)
            group.append((consts[k][:, :], consts_in[k]))
        casts = []
        for k, n, src, at in (("identb", P, "ident", 0), ("causal", P, "causal", 1), ("behind", 4 * P, "behind", 2)):
            consts[k] = sb(k, [P, n], BF16)
            wide = F[:, QT + at:QT + at + n // P, :]
            first.append((wide, consts_in[src].rearrange("p (a n) -> p a n", n=P)))
            casts.append((consts[k][:, :].rearrange("p (a n) -> p a n", n=P), wide))
        neglam = consts["neglam"] = sb("neglam", [P, 16])
        first.append((neglam[:, :], ins["lambda_logit"].unsqueeze(0).broadcast_to([P, 16])))
        minus_half = consts["minus_half"] = sb("minus_half", [P, TILES])

        row = lambda a: a.unsqueeze(0).broadcast_to([P, a.shape[0]])
        wB, wF = [], []
        for l in range(2):
            n = str(l)
            w = {"wqk": sb("wqk" + n, [P, 1024]), "wv": sb("wv" + n, [P, 512]), "wo": sb("wo" + n, [P, 4, D]),
                 "cos": sb("cos" + n, [P, QT, 2, 64]), "sin": sb("sin" + n, [P, QT, 2, 64]),
                 "scale": sb("scale" + n, [P, 2, 64]), "scaler": sb("scaler" + n, [P, 2, 64])}
            later += [(w["wqk"][:, :], ins["wqkv"][l, :, 0:1024]), (w["wv"][:, :], ins["wqkv"][l, :, 1024:1536]),
                      (w["wo"][:, :, :], ins["wo"][l].rearrange("(n p) d -> p n d", p=P)),
                      (w["cos"][:, :, :, :], consts_in["cos"]), (w["sin"][:, :, :, :], consts_in["sin"])]
            for a, k in enumerate(("q_scale", "k_scale")):
                s = ins[k][l, :]
                later += [(w["scale"][:, a, :], row(s)), (w["scaler"][:, a, 0:32], row(s[32:64])),
                          (w["scaler"][:, a, 32:64], row(s[0:32]))]
            wB.append(w)
            w = {"w1": sb("w1" + n, [P, 682]), "b1": sb("b1" + n, [P, 6]), "w2": sb("w2" + n, [P, 3, D]),
                 "b2": sb("b2" + n, [P, D]), "ln_g": sb("lng" + n, [P, 1]), "ln_b": sb("lnb" + n, [P, 1])}
            later += [(w["w1"][:, :], ins["w1"][l]), (w["b1"][:, :], ins["b1"][l]), (w["w2"][:, :, :], ins["w2"][l]),
                      (w["b2"][:, :], row(ins["b2"][l, :])), (w["ln_g"][:, :], ins["ln_g"][l, :].unsqueeze(1)),
                      (w["ln_b"][:, :], ins["ln_b"][l, :].unsqueeze(1))]
            wF.append(w)
        wS = {}
        for k, shape in (("W_in", [P, 32]), ("b_in", [P, 1]), ("Bm", [P, P]), ("A", [P, P]), ("AT", [P, P]),
                         ("C", [P, D])):
            wS[k] = sb("s_w" + k, shape)
            later.append((wS[k][:, :], ins["s_" + k]))
        wS["D"] = sb("s_wD", [P, D])
        later.append((wS["D"][:, :], row(ins["s_D"])))
        wM = {"router": sb("m_router", [P, 8]), "gate": sb("m_gate", [P, 8, 256]), "up": sb("m_up", [P, 8, 256]),
              "down": sb("m_down", [P, 8, 2, D])}
        later += [(wM["router"][:, :], ins["router"]), (wM["gate"][:, :, :], ins["w_gate"].rearrange("e d h -> d e h")),
                  (wM["up"][:, :, :], ins["w_up"].rearrange("e d h -> d e h")),
                  (wM["down"][:, :, :, :], ins["w_down"].rearrange("e (j p) d -> p e j d", p=P))]

        loaded, loaded_later, ready = sem("loaded"), sem("loaded_later"), sem("ready")
        with nc.Block() as block:
            @block.sync
            def _(sp):
                for dst, src in first:
                    sp.dma_start(dst, src).then_inc(loaded, 16)
                for dst, src in later:
                    sp.dma_start(dst, src).then_inc(loaded_later, 16)
                sp.wait_ge(loaded, 16 * len(first))

            @block.gpsimd
            def _(pool):
                pool.memset(minus_half[:, :], -0.5)
                pool.memset(APART["dve"], 0.0)
                pool.memset(APART["pool"], 0.0)
                pool.memset(X[:, 0:QT, :], 0.0)
                pool.memset(X[:, QT + TILES:TILES + 2 * QT, :], 0.0)
                pool.memset(F[:, 0:QT, :], 0.0)
                pool.memset(F[:, QT + TILES:, :], 0.0).then_inc(ready, 1)

            @block.scalar
            def _(act):
                act.wait_ge(loaded, 16 * len(first))
                act.activation(neglam[:, :], neglam[:, :], ACT.Exp, scale=-1.0).then_inc(ready, 1)

            @block.vector
            def _(dve):
                dve.wait_ge(ready, 2)
                dve.tensor_scalar(neglam[:, :], neglam[:, :], -1.0, -1.0, ALU.mult, ALU.add).then_inc(ready, 1)
                for narrow, wide in casts:
                    dve.tensor_copy(narrow, wide)
                dve.wait_ge(ready, 3)
                dve.reciprocal(neglam[:, :], neglam[:, :]).then_inc(ready, 1)

        differential_attention(nc, X, consts, wA)

        if stop != "A":
            with nc.Block() as block:
                @block.vector
                def _(dve):
                    dve.wait_ge(loaded_later, 16 * len(later))
                    for w in wB:
                        for tab, s in (("cos", "scale"), ("sin", "scaler")):
                            for t in range(QT):
                                dve.tensor_tensor(w[tab][:, t], w[tab][:, t], w[s][:, :, :], ALU.mult)
            normalise_all(nc, "n0", X, F, minus_half)
            for l in range(2):
                window_attention(nc, f"b{l}", F, consts, wB[l])
                if stop == "B0":
                    break
                feed_forward(nc, f"f{l}", F, consts, wF[l])
                if stop == "F0":
                    break
            if stop in ("B0", "F0"):
                X = F
            else:
                add_normalised(nc, "n1", X, F, minus_half)
        if stop in (None, "S"):
            normalise_all(nc, "n2", X, F, minus_half)
            state_space(nc, X, F, consts, wS)
        if stop is None:
            normalise_all(nc, "n3", X, F, minus_half)
            mixture_of_experts(nc, X, F, out, consts, wM)
            return

        stored = nc.alloc_semaphore("stored")
        with nc.Block() as block:
            @block.sync
            def _(sp):
                sp.dma_start(out.rearrange("b (t p) d -> p (b t) d", p=P), X[:, QT:QT + TILES, :]).then_inc(stored, 16)
                sp.wait_ge(stored, 16)


def constants():
    r = np.arange(128)
    c = {
        "ident": np.eye(128, dtype=np.float32),
        "causal": np.where(r[None, :] <= r[:, None], 0.0, -1e37).astype(np.float32),
        "headrow": (r[:, None] // 8 == np.arange(16)[None, :]).astype(np.float32),
    }
    keys = []
    for n, first in enumerate((0, 0, 64, 128)):
        i, j = n * 64 + r[:, None] % 64, first + r[None, :]
        keys.append(np.where((j <= i) & (i <= j + 64), 0.0, -1e37))
    c["behind"] = np.concatenate(keys, 1).astype(np.float32)
    c["expert_id"] = np.tile(np.arange(8, dtype=np.float32), (128, 1))
    f = np.float32
    half = np.arange(0, 64, 2).astype(f)
    inv = f(1) / f(10000) ** (half / f(64))
    t = np.arange(256).astype(f)
    freqs = np.concatenate([t[:, None] * inv[None]] * 2, -1)
    base = (half + f(25.6)) / f(89.6)
    scale = base[None] ** ((t - f(128)) / f(32))[:, None]
    scale = np.concatenate([scale] * 2, -1)
    sign = np.where(np.arange(64) < 32, -1, 1).astype(f)
    both = lambda a: np.stack([f(8) * a * scale, a / scale], 1)
    tiles = lambda a: np.ascontiguousarray(both(a).reshape(2, 128, 2, 64).transpose(1, 0, 2, 3)).astype(f)
    c["cos"] = tiles(np.cos(freqs))
    c["sin"] = tiles(np.sin(freqs) * sign)
    return c


def layout(inputs):
    a = {k: np.asarray(v) for k, v in inputs.items()}
    c = np.ascontiguousarray
    b1 = np.zeros((2, 2, 384), np.float32)
    b1[:, :, :341] = a["L0_ffn_b1"].reshape(2, 2, 341)
    b1 = c(b1.reshape(2, 6, 128).transpose(0, 2, 1))
    w2 = np.zeros((2, 384, 128), np.float32)
    w2[:, :341] = a["L0_ffn_w2"]
    w2 = c(w2.reshape(2, 3, 128, 128).transpose(0, 2, 1, 3))

    def diagonal(m):
        big = np.zeros((128, 128), np.float32)
        for g in range(4):
            big[32 * g:32 * g + 32, 32 * g:32 * g + 32] = m
        return big

    return {
        "x": c(a["L0_attn_x"]),
        **{k: c(a["L0_attn_" + k].T) for k in ("Wq", "Wk1", "Wk2", "Wv", "Wo")},
        "lambda_logit": c(a["L0_attn_lambda_logit"]),
        **{k: c(a["L0_ffn_" + k]) for k in ("wqkv", "q_scale", "k_scale", "wo", "w1", "b2", "ln_g", "ln_b")},
        "b1": b1,
        "w2": w2,
        "s_W_in": c(a["L1_attn_W_in"].T),
        "s_b_in": c(np.tile(a["L1_attn_b_in"], 4)[:, None]),
        "s_Bm": diagonal(a["L1_attn_Bm"].T),
        "s_A": diagonal(a["L1_attn_A"]),
        "s_AT": diagonal(a["L1_attn_A"].T),
        "s_C": c(np.tile(a["L1_attn_C"].T, (4, 1))),
        "s_D": c(a["L1_attn_D"]),
        "router": c(a["L1_ffn_router_w"].T),
        **{k: c(a["L1_ffn_" + k]) for k in ("w_gate", "w_up", "w_down")},
    }


def kernel(**inputs):
    import concourse.bacc as bacc
    from concourse.bass_utils import run_bass_kernel_spmd as run

    nc = bacc.Bacc("TRN2", target_bir_lowering=False, num_devices=1)
    arrays, ins, consts = {}, {}, {}
    for group, into in ((layout(inputs), ins), (constants(), consts)):
        for name, a in group.items():
            full = f"in_{name}_dram"
            arrays[full] = a
            into[name] = nc.dram_tensor(full, a.shape, mybir.dt.from_np(a.dtype), kind="ExternalInput").ap()
    out = nc.dram_tensor("out_0_dram", (16, 256, 128), FP32, kind="ExternalOutput").ap()
    build(nc, ins, consts, out)
    r = run(nc, [arrays], core_ids=[0])
    return r.results[0]["out_0_dram"]
```

```python
import numpy as np
import concourse.bass as bass
from concourse import mybir
from contextlib import ExitStack

FP32 = mybir.dt.float32
BF16 = mybir.dt.bfloat16
ALU = mybir.AluOpType
ACT = mybir.ActivationFunctionType
AX = mybir.AxisListType

P = 128
D = 128
BATCH = 16
T = 256
QT = T // P
TILES = BATCH * QT
EPS_LN = 1e-5


class Signal:
    opened = []

    def __init__(self, sem, per, base=0):
        self.sem, self.per, self.base = sem, per, base + 1
        self.opened.append(self)

    def early(self, k):
        return k + 1

    def at(self, pair, half, k):
        return pair * (2 * self.per) + (half * self.per + k + self.base)


class Chain(Signal):

    def __init__(self, sem, per, base=0):
        super().__init__(sem, per, base)
        self.k = 0

    def begin(self, eng, pair, half):
        self.eng, self.pair, self.half, self.k = eng, pair, half, 0

    def restart(self, raises):
        self.base = raises + 1

    def mark(self, ins):
        self.k += 1
        ins.then_inc(self.sem, 1)
        return self.k

    def wait(self, k):
        self.eng.wait_ge(self.sem, self.at(self.pair, self.half, k))

    def last(self):
        self.wait(self.k)

    def end(self):
        assert self.k == self.per, f"{self.k} raises a batch, not {self.per}"


def open_signals(eng):
    for signal in Signal.opened:
        eng.sem_inc(signal.sem, 1)
    Signal.opened.clear()


APART = {}


def apart(eng, scratch):
    eng.tensor_tensor(scratch, scratch, scratch, ALU.mult)

CHAIN_A = 62
CHAIN_B = 6
CHAIN_F = 2
CHAIN_M, CHAIN_M_PRE = 13, 10


def differential_attention(nc, X, consts, weights, load_later):
    H, HD = 16, 8
    GH = 4
    SCALE = HD ** -0.5
    ident, identb, causal, headrow, neglam = (consts[k] for k in ("ident", "identb", "causal", "headrow", "neglam"))
    wq, wk1, wk2, wv, wo = (weights[k] for k in ("Wq", "Wk1", "Wk2", "Wv", "Wo"))
    minus_half = consts["minus_half"]

    with ExitStack() as ctx:
        sb = lambda name, shape, dt=FP32: ctx.enter_context(nc.sbuf_tensor("a_" + name, shape, dt))
        ps = lambda name, shape: ctx.enter_context(nc.psum_tensor("a_" + name, shape, FP32))
        sem = lambda name: nc.alloc_semaphore("a_" + name)

        qm = sb("qm", [P, 2, H, T])
        qT = sb("qT", [P, T])
        kT = sb("kT", [P, 2, 2, T])
        vp = sb("vp", [P, 2, QT, H, 32])
        xn = sb("xn", [P, QT, D])
        xnT = sb("xnT", [P, T])
        st = sb("st", [P, 2, QT, 6])
        mv = sb("mv", [P, 2, QT, 2])
        rs = sb("rs", [P, 2, QT])
        nm = sb("nm", [P, 2, 2, 2])
        Z = sb("Z", [P, 2, H, 2, 2])
        E = sb("E", [P, 2, 2, 384])
        rz = sb("rz", [P, 2, 2])
        cf = sb("cf", [P, 2, 2])
        d = sb("d", [P, 2, 384])
        ab = sb("ab", [P, 2, H, 3])
        den = sb("den", [P, 2, H])
        floor = sb("floor", [P, 2, H])
        dT = sb("dT", [P, 2, 384])
        OT = sb("OT", [P, H // GH, T])
        On = sb("On", [P, QT, D])
        OnT = sb("OnT", [P, T])
        y = sb("y", [P, QT, D])
        yn = sb("yn", [P, QT, D])

        psS = ps("psS", [P, 2, 2, 512])
        psT = ps("psT", [P, 2, 512])
        psO = ps("psO", [P, T])
        psM = ps("psM", [P, 512])

        E_OT0, E_OT1, E_ONT, E_Y, P_XNT, P_Q, P_K1, P_K2, P_V = range(9)
        USES, PRE = 9, 5
        misc_full = Signal(sem("misc_full"), USES, PRE)
        misc_free = Signal(sem("misc_free"), USES, PRE)
        scored = Signal(sem("scored"), H)
        maxed = Signal(sem("maxed"), H)
        exped = Signal(sem("exped"), H, 2)
        mixed = Signal(sem("mixed"), H, 2)
        turned = Signal(sem("turned"), H, 2)
        evaced = Signal(sem("evaced"), H, 2)
        pved = Signal(sem("pved"), H, 2)
        otmoved = Signal(sem("otmoved"), H // GH, 1)
        qm_ready = Signal(sem("qm_ready"), H)
        xn_ready = Signal(sem("xn_ready"), 1, 1)
        var_ready = Signal(sem("var_ready"), 2, 1)
        rs_ready = Signal(sem("rs_ready"), 2, 1)
        den_ready = Signal(sem("den_ready"), 1)
        added = Signal(sem("added"), 1)
        zeroed = sem("zeroed")
        own = Chain(sem("own"), CHAIN_A, 4)

        block = ctx.enter_context(nc.Block())
        LAST = BATCH // 2

        def x_of(pair, half):
            return X[:, bass.ds((pair * 2 + (half + 1)) * QT, QT), :]

        @block.sync
        def _(sp):
            open_signals(sp)
            load_later(sp)

        @block.gpsimd
        def _(pool):
            for tile in (vp, OT, Z, ab, dT, d):
                pool.memset(tile[:], 1.0 if tile in (Z, ab) else 0.0).then_inc(zeroed, 1)

            def rstd(which, pair, half, k):
                pool.wait_ge(var_ready.sem, var_ready.at(pair, half, k))
                pool.tensor_tensor(rs[:, which, :], mv[:, which, :, 1], minus_half[:, 0:QT], ALU.pow)\
                    .then_inc(rs_ready.sem, 1)

            def mask_heads(half):
                apart(pool, APART["pool"])
                for h in range(H):
                    pool.tensor_scalar(qm[:, half % 2, h, :], qT[:, :], headrow[:, h:h + 1], 1.0,
                                       ALU.mult, ALU.mult).then_inc(qm_ready.sem, 1)

            rstd(0, 0, 0, 0)
            pool.wait_ge(misc_free.sem, misc_free.early(2))
            mask_heads(0)
            with pool.Fori(0, LAST) as pair:
                for half in range(2):
                    rstd(0, pair, half, 1)
                    rstd(1, pair, half, 2)
                    pool.wait_ge(misc_free.sem, misc_free.at(pair, half, P_Q + 1))
                    pool.wait_ge(scored.sem, scored.at(pair, half, 0))
                    mask_heads(half + 1)
            rstd(1, LAST, 0, 1)

        @block.vector
        def _(dve):
            def maxima(pair, half, h, t):
                s = h % 2
                if t == 0:
                    dve.wait_ge(scored.sem, scored.at(pair, half, h + 1))
                ins = dve.tensor_reduce(nm[:, s, t, :], psS[:, s, :, (0, P)[t]:(P, 384)[t]], axis=AX.X,
                                        op=ALU.max, negate=True)
                if t == 1:
                    ins.then_inc(maxed.sem, 1)

            def inverse(pair, half, h):
                s, p = h % 2, half % 2
                dve.wait_ge(exped.sem, exped.at(pair, half, h + 1))
                return own.mark(dve.reciprocal(rz[:, s, :], Z[:, p, h, :, 1]))

            def coefficient(pair, half, h, k):
                s, p = h % 2, half % 2
                own.wait(k)
                return own.mark(dve.scalar_tensor_tensor(out=cf[:, s, :], in0=Z[:, p, h, :, 0],
                                                         scalar=neglam[:, h:h + 1], in1=rz[:, s, :],
                                                         op0=ALU.mult, op1=ALU.mult))

            def mix(pair, half, h, k):
                s = h % 2
                dve.wait_ge(turned.sem, turned.at(pair, half, h - 1))
                own.wait(k)
                for t, c0, c1 in ((0, 0, P), (1, P, 384)):
                    ins = dve.scalar_tensor_tensor(out=d[:, s, c0:c1], in0=E[:, s, 1, c0:c1],
                                                   scalar=cf[:, s, t:t + 1], in1=E[:, s, 0, c0:c1],
                                                   op0=ALU.mult, op1=ALU.add)
                ins.then_inc(mixed.sem, 1)

            def absolute(pair, half, h):
                s, p = h % 2, half % 2
                dve.wait_ge(mixed.sem, mixed.at(pair, half, h % H + 1 if h >= 0 else 0))
                own.mark(dve.tensor_reduce(ab[:, p if h >= 0 else 1 - p, h % H, :],
                                           d[:, s, :].rearrange("p (c k) -> p c k", c=3),
                                           axis=AX.X, op=ALU.add, apply_absolute_value=True))

            def statistics(which, src):
                for t in range(QT):
                    own.mark(dve.bn_stats(st[:, which, t, :], src[:, t, :]))

            def aggregate(which):
                own.last()
                apart(dve, APART["dve"])
                for t in range(QT):
                    own.mark(dve.bn_aggr(mv[:, which, t, :], st[:, which, t, :]))

            def guard(which):
                own.last()
                dve.tensor_scalar(mv[:, which, :, 1], mv[:, which, :, 1], EPS_LN, None, ALU.add)\
                   .then_inc(var_ready.sem, 1)

            def normalise_x(xs):
                for t in range(QT):
                    ins = dve.tensor_scalar(xn[:, t, :], xs[:, t, :], mv[:, 0, t, 0:1], rs[:, 0, t:t + 1],
                                            ALU.subtract, ALU.mult)
                ins.then_inc(xn_ready.sem, 1)

            def sum_absolute(half):
                q = (half - 1) % 2
                own.last()
                own.mark(dve.tensor_copy(den[:, 0, :], ab[:, q, :, 0]))
                return own.mark(dve.tensor_tensor(den[:, 1, :], ab[:, q, :, 1], ab[:, q, :, 2], ALU.add))

            def guard_sums(half, k):
                q = (half - 1) % 2
                own.wait(k)
                for t in range(QT):
                    k = own.mark(dve.scalar_tensor_tensor(out=floor[:, t, :], in0=Z[:, q, :, t, 0], scalar=1e-6,
                                                          in1=den[:, t, :], op0=ALU.mult, op1=ALU.max))
                return k

            def denominators(k):
                own.wait(k)
                dve.reciprocal(den[:, :, :], floor[:, :, :]).then_inc(den_ready.sem, 1)

            def normalise_o(pair, half, t):
                dve.wait_ge(misc_full.sem, misc_full.at(pair, half, E_OT0 + t + 1))
                dve.wait_ge(den_ready.sem, den_ready.at(pair, half, 1))
                dve.tensor_tensor(On[:, t, :].rearrange("p (h e) -> p h e", e=HD),
                                  psM[:, :].rearrange("p (h e) -> p h e", e=32)[:, :, 0:HD],
                                  den[:, t, :].unsqueeze(2).broadcast_to([P, H, HD]), ALU.mult)\
                   .then_inc(misc_free.sem, 1)

            def normalise_y(pair, half, k):
                dve.wait_ge(rs_ready.sem, rs_ready.at(pair, half, k))
                for t in range(QT):
                    own.mark(dve.tensor_scalar(yn[:, t, :], y[:, t, :], mv[:, 1, t, 0:1], rs[:, 1, t:t + 1],
                                               ALU.subtract, ALU.mult))

            def residual(pair, half):
                own.last()
                xs = x_of(pair, half - 1)
                dve.tensor_tensor(xs, xs, yn[:, :, :], ALU.add).then_inc(added.sem, 1)

            dve.memset(psO[:, :], 0.0).then_inc(zeroed, 1)
            dve.wait_ge(zeroed, 7)
            own.begin(dve, 0, 0)
            own.restart(0)
            statistics(0, x_of(0, 0))
            aggregate(0)
            guard(0)
            own.restart(own.k)
            assert own.k == 4
            dve.wait_ge(rs_ready.sem, rs_ready.early(1))
            normalise_x(x_of(0, 0))
            for t in range(QT):
                maxima(0, 0, 0, t)
            with dve.Fori(0, LAST) as pair:
                for half in range(2):
                    own.begin(dve, pair, half)
                    for s in range(H):
                        nxt = (pair, half + (s + 1) // H, (s + 1) % H)
                        if s == 1:
                            sums = sum_absolute(half)
                        maxima(*nxt, 0)
                        maxima(*nxt, 1)
                        if s == 1:
                            sums = guard_sums(half, sums)
                        k = inverse(pair, half, s)
                        absolute(pair, half, s - 1)
                        k = coefficient(pair, half, s, k)
                        if s == 1:
                            denominators(sums)
                        mix(pair, half, s, k)
                        if s in (2, 4):
                            normalise_o(pair, half, s // 2 - 1)
                        if s == 4:
                            statistics(0, x_of(pair, half + 1))
                        if s == 5:
                            aggregate(0)
                        if s == 6:
                            guard(0)
                        if s == 7:
                            dve.wait_ge(rs_ready.sem, rs_ready.at(pair, half, 1))
                            dve.wait_ge(misc_full.sem, misc_full.at(pair, half - 1, P_XNT + 1))
                            normalise_x(x_of(pair, half + 1))
                        if s == 9:
                            dve.wait_ge(misc_free.sem, misc_free.at(pair, half, E_Y + 1))
                            statistics(1, y)
                        if s == 10:
                            aggregate(1)
                        if s == 11:
                            guard(1)
                        if s == 12:
                            normalise_y(pair, half, 2)
                        if s == 13:
                            residual(pair, half)
                    own.end()
            own.begin(dve, LAST, 0)
            absolute(LAST, 0, -1)
            denominators(guard_sums(0, sum_absolute(0)))
            normalise_o(LAST, 0, 0)
            normalise_o(LAST, 0, 1)
            dve.wait_ge(misc_free.sem, misc_free.at(LAST, 0, E_Y + 1))
            statistics(1, y)
            aggregate(1)
            guard(1)
            normalise_y(LAST, 0, 1)
            residual(LAST, 0)

        @block.scalar
        def _(act):
            def exps(pair, half, h, first=False):
                s, p = h % 2, half % 2
                act.wait_ge(maxed.sem, maxed.at(pair, half, h + 1))
                act.wait_ge(mixed.sem, mixed.at(pair, half, h - 1))
                if h == 0:
                    act.wait_ge(den_ready.sem, den_ready.at(pair, half, 0))
                for t, c0, c1 in ((0, 0, P), (1, P, 384)):
                    for m in range(2):
                        ins = act.activation(E[:, s, m, c0:c1], psS[:, s, m, c0:c1], ACT.Exp,
                                             bias=nm[:, s, t, m:m + 1], accum_out=Z[:, p, h, t, m:m + 1])
                ins.then_inc(exped.sem, 1)

            def evac_d(pair, half, h):
                s = h % 2
                act.wait_ge(turned.sem, turned.at(pair, half, h + 1))
                act.wait_ge(pved.sem, pved.at(pair, half, h - 1))
                act.activation(dT[:, s, :], psT[:, s, 0:384], ACT.Copy).then_inc(evaced.sem, 1)

            def move_ot(pair, half, g):
                act.wait_ge(pved.sem, pved.at(pair, half, GH * (g + 1)))
                if g == 0:
                    act.wait_ge(misc_full.sem, misc_full.at(pair, half, E_OT1 + 1))
                act.activation(OT[:, g, :], psO[:, :], ACT.Copy).then_inc(otmoved.sem, 1)

            def copy(dst, src, full, scale=1.0):
                act.wait_ge(misc_full.sem, full)
                act.activation(dst, src, ACT.Copy, scale=scale).then_inc(misc_free.sem, 1)

            def prepare(use, p, full):
                if use == P_XNT:
                    copy(xnT[:, :], psM[:, 0:T], full)
                elif use == P_Q:
                    copy(qT[:, :], psM[:, T:512], full, SCALE)
                elif use == P_K1:
                    copy(kT[:, p, 0, :], psM[:, 0:T], full)
                elif use == P_K2:
                    copy(kT[:, p, 1, :], psM[:, T:512], full)
                elif use == P_V:
                    copy(vp[:, p, :, :, 0:HD],
                         psM[:, 0:T].rearrange("p (t h e) -> p t h e", t=QT, e=HD), full)

            act.wait_ge(zeroed, 7)
            for signal, n in ((exped, 2), (mixed, 2), (turned, 2), (evaced, 2), (pved, 1)):
                act.sem_inc(signal.sem, n)
            for n, use in enumerate((P_XNT, P_Q, P_K1, P_K2, P_V)):
                prepare(use, 0, misc_full.early(n + 1))
            exps(0, 0, 0)
            with act.Fori(0, LAST) as pair:
                for half in range(2):
                    p = (half + 1) % 2
                    for s in range(H):
                        if s == 6:
                            copy(OnT[:, :], psM[:, 0:T], misc_full.at(pair, half, E_ONT + 1))
                        if s == 8:
                            act.wait_ge(added.sem, added.at(pair, half, 0))
                            copy(y[:, :, :], psM[:, T:512].rearrange("p (t n) -> p t n", t=QT),
                                 misc_full.at(pair, half, E_Y + 1))
                        if 9 <= s <= 13:
                            use = P_XNT + s - 9
                            if use == P_Q:
                                act.wait_ge(qm_ready.sem, qm_ready.at(pair, half + 1, 0))
                            if use == P_K1:
                                act.wait_ge(scored.sem, scored.at(pair, half, 0))
                            if use == P_V:
                                act.wait_ge(pved.sem, pved.at(pair, half, 0))
                            prepare(use, p, misc_full.at(pair, half, use + 1))
                        exps(pair, half + (s + 1) // H, (s + 1) % H)
                        if s == 0:
                            move_ot(pair, half - 1, H // GH - 1)
                        evac_d(pair, half, s)
                        if s in (4, 8, 12):
                            move_ot(pair, half, s // 4 - 1)
            move_ot(LAST, -1, H // GH - 1)
            copy(OnT[:, :], psM[:, 0:T], misc_full.at(LAST, 0, E_ONT + 1))
            act.wait_ge(added.sem, added.at(LAST, 0, 0))
            copy(y[:, :, :], psM[:, T:512].rearrange("p (t n) -> p t n", t=QT), misc_full.at(LAST, 0, E_Y + 1))

        @block.tensor
        def _(pe):
            def scores(pair, half, h):
                s, p = h % 2, half % 2
                pe.wait_ge(exped.sem, exped.at(pair, half, h - 1))
                pe.wait_ge(qm_ready.sem, qm_ready.at(pair, half, h + 1))
                for m in range(2):
                    out = psS[:, s, m, :]
                    pe.matmul(out[:, 0:P], qm[:, p, h, 0:P], kT[:, p, m, 0:P], start=True, stop=False)
                    pe.matmul(out[:, 0:P], identb[:, :], causal[:, :], start=False, stop=True)
                    pe.matmul(out[:, P:384], qm[:, p, h, P:T], kT[:, p, m, 0:T], start=True, stop=False)
                    ins = pe.matmul(out[:, T:384], identb[:, :], causal[:, :], start=False, stop=True)
                ins.then_inc(scored.sem, 1)

            def turn(pair, half, h):
                s = h % 2
                pe.wait_ge(mixed.sem, mixed.at(pair, half, h + 1))
                pe.wait_ge(evaced.sem, evaced.at(pair, half, h - 1))
                for c in range(3):
                    ins = pe.transpose(psT[:, s, c * P:(c + 1) * P], d[:, s, c * P:(c + 1) * P], ident[:, :])
                ins.then_inc(turned.sem, 1)

            def outputs(pair, half, h):
                s, p, g, j = h % 2, half % 2, h // GH, h % GH
                pe.wait_ge(evaced.sem, evaced.at(pair, half, h + 1))
                if j == 0:
                    pe.wait_ge(otmoved.sem, otmoved.at(pair, half, g))
                out = psO[32 * j:32 * j + 32, :]
                pe.matmul(out[:, 0:P], vp[:, p, 0, h, :], dT[:, s, 0:P], start=True, stop=True)
                pe.matmul(out[:, P:T], vp[:, p, 0, h, :], dT[:, s, P:T], start=True, stop=False)
                pe.matmul(out[:, P:T], vp[:, p, 1, h, :], dT[:, s, T:384], start=False, stop=True)\
                  .then_inc(pved.sem, 1)

            def use_misc(use, p, free):
                pe.wait_ge(misc_free.sem, free)
                lo, hi = psM[:, 0:T], psM[:, T:512]
                if use in (E_OT0, E_OT1):
                    t = use - E_OT0
                    for g in range(H // GH):
                        ins = pe.transpose(psM[:, g * P:(g + 1) * P], OT[:, g, t * P:(t + 1) * P], ident[:, :])
                elif use == E_ONT:
                    for t in range(QT):
                        ins = pe.transpose(lo[:, t * P:(t + 1) * P], On[:, t, :], ident[:, :])
                elif use == E_Y:
                    for t in range(QT):
                        ins = pe.matmul(hi[:, t * P:(t + 1) * P], OnT[:, t * P:(t + 1) * P], wo[:, :],
                                        start=True, stop=True)
                elif use == P_XNT:
                    for t in range(QT):
                        ins = pe.transpose(lo[:, t * P:(t + 1) * P], xn[:, t, :], ident[:, :])
                elif use == P_Q:
                    ins = pe.matmul(hi, wq[:, :], xnT[:, :], start=True, stop=True)
                elif use == P_K1:
                    ins = pe.matmul(lo, wk1[:, :], xnT[:, :], start=True, stop=True)
                elif use == P_K2:
                    ins = pe.matmul(hi, wk2[:, :], xnT[:, :], start=True, stop=True)
                else:
                    for t in range(QT):
                        ins = pe.matmul(lo[:, t * P:(t + 1) * P], xnT[:, t * P:(t + 1) * P], wv[:, :],
                                        start=True, stop=True)
                ins.then_inc(misc_full.sem, 1)

            pe.wait_ge(zeroed, 7)
            pe.wait_ge(xn_ready.sem, xn_ready.early(1))
            for n, use in enumerate((P_XNT, P_Q, P_K1, P_K2, P_V)):
                use_misc(use, 0, misc_free.early(n))
            pe.wait_ge(misc_free.sem, misc_free.early(PRE))
            scores(0, 0, 0)
            scores(0, 0, 1)
            SCHEDULE = {1: E_OT0, 3: E_OT1, 5: E_ONT, 7: E_Y, 8: P_XNT, 9: P_Q, 10: P_K1, 11: P_K2, 12: P_V}
            with pe.Fori(0, LAST) as pair:
                for half in range(2):
                    for s in range(H):
                        if s == H - 2:
                            pe.wait_ge(misc_free.sem, misc_free.at(pair, half, USES))
                        scores(pair, half + (s + 2) // H, (s + 2) % H)
                        outputs(pair, half - 1 if s == 0 else half, (s - 1) % H)
                        if s in SCHEDULE:
                            use = SCHEDULE[s]
                            if use == E_OT0:
                                pe.wait_ge(otmoved.sem, otmoved.at(pair, half, 0))
                            if use == P_XNT:
                                pe.wait_ge(xn_ready.sem, xn_ready.at(pair, half, 1))
                            use_misc(use, half, misc_free.at(pair, half, use))
                        turn(pair, half, s)
            outputs(LAST, -1, H - 1)
            pe.wait_ge(otmoved.sem, otmoved.at(LAST, 0, 0))
            for use in (E_OT0, E_OT1, E_ONT, E_Y):
                use_misc(use, 0, misc_free.at(LAST, 0, use))


class Layernorms:
    G = 4

    def __init__(self, nc, ctx, name, src, minus_half):
        sem = lambda n: nc.alloc_semaphore(name + n)
        G = self.G
        self.groups = TILES // G
        self.src, self.minus_half = src, minus_half
        self.st = ctx.enter_context(nc.sbuf_tensor(name + "st", [P, G, 6], FP32))
        self.mv = ctx.enter_context(nc.sbuf_tensor(name + "mv", [P, 2, G, 2], FP32))
        self.rs = ctx.enter_context(nc.sbuf_tensor(name + "rs", [P, self.groups, G], FP32))
        self.shift = ctx.enter_context(nc.sbuf_tensor(name + "shift", [P, self.groups, G], FP32))
        self.stats, self.var_ready, self.rs_ready = sem("stats"), sem("var_ready"), sem("rs_ready")
        self.shift_ready = sem("shift_ready")

    def tiles(self, a, g):
        return a[:, QT + g * self.G:QT + (g + 1) * self.G, :]

    def power(self, pool, g):
        pool.wait_ge(self.var_ready, g + 1)
        pool.tensor_tensor(self.rs[:, g], self.mv[:, g % 2, :, 1], self.minus_half[:, 0:self.G], ALU.pow)\
            .then_inc(self.rs_ready, 1)

    def statistics(self, dve, g):
        mv, src = self.mv[:, g % 2], self.tiles(self.src, g)
        for t in range(self.G):
            ins = dve.bn_stats(self.st[:, t, :], src[:, t, :])
        ins.then_inc(self.stats, 1)
        dve.wait_ge(self.stats, g * 2 + 1)
        for t in range(self.G):
            ins = dve.bn_aggr(mv[:, t, :], self.st[:, t, :])
        ins.then_inc(self.stats, 1)
        dve.wait_ge(self.stats, g * 2 + 2)
        dve.tensor_scalar(mv[:, :, 1], mv[:, :, 1], EPS_LN, None, ALU.add).then_inc(self.var_ready, 1)

    def shifts(self, dve, g):
        dve.wait_ge(self.rs_ready, g + 1)
        dve.scalar_tensor_tensor(out=self.shift[:, g], in0=self.mv[:, g % 2, :, 0], scalar=-1.0, in1=self.rs[:, g],
                                 op0=ALU.mult, op1=ALU.mult).then_inc(self.shift_ready, 1)

    def apply(self, act, g, dst):
        act.wait_ge(self.shift_ready, g + 1)
        src = self.tiles(self.src, g)
        for t in range(self.G):
            ins = act.activation(dst[:, t, :], src[:, t, :], ACT.Identity, bias=self.shift[:, g, t:t + 1],
                                 scale=self.rs[:, g, t:t + 1])
        return ins


def normalise_all(nc, name, src, dst, minus_half):
    with ExitStack() as ctx:
        ln = Layernorms(nc, ctx, name, src, minus_half)
        block = ctx.enter_context(nc.Block())

        @block.gpsimd
        def _(pool):
            for g in range(ln.groups):
                ln.power(pool, g)

        @block.vector
        def _(dve):
            for g in range(ln.groups):
                ln.statistics(dve, g)
                if g > 0:
                    ln.shifts(dve, g - 1)
            ln.shifts(dve, ln.groups - 1)

        @block.scalar
        def _(act):
            for g in range(ln.groups):
                ln.apply(act, g, ln.tiles(dst, g))


def add_normalised(nc, name, X, F, minus_half):
    with ExitStack() as ctx:
        inner = Layernorms(nc, ctx, name + "i", F, minus_half)
        outer = Layernorms(nc, ctx, name + "o", X, minus_half)
        groups = inner.groups
        applied, added = nc.alloc_semaphore(name + "applied"), nc.alloc_semaphore(name + "added")
        block = ctx.enter_context(nc.Block())

        @block.gpsimd
        def _(pool):
            for g in range(groups + 2):
                if g < groups:
                    inner.power(pool, g)
                if g >= 2:
                    outer.power(pool, g - 2)

        @block.vector
        def _(dve):
            for g in range(groups + 3):
                if g < groups:
                    inner.statistics(dve, g)
                if 1 <= g <= groups:
                    inner.shifts(dve, g - 1)
                if 2 <= g < groups + 2:
                    dve.wait_ge(applied, g - 1)
                    xs = inner.tiles(X, g - 2)
                    dve.tensor_tensor(xs, xs, inner.tiles(F, g - 2), ALU.add).then_inc(added, 1)
                    dve.wait_ge(added, g - 1)
                    outer.statistics(dve, g - 2)
                if g >= 3:
                    outer.shifts(dve, g - 3)

        @block.scalar
        def _(act):
            for g in range(groups + 2):
                if g < groups:
                    inner.apply(act, g, inner.tiles(F, g)).then_inc(applied, 1)
                if g >= 2:
                    outer.apply(act, g - 2, outer.tiles(F, g - 2))


def window_attention(nc, name, F, consts, w):
    H, HD = 8, 64
    NP = H // 2
    W = H * HD
    NW = T // 64
    KEYS = (0, 0, 64, 128)
    ident, identb, behind = (consts[k] for k in ("ident", "identb", "behind"))
    minus_half = consts["minus_half"]
    wqk, wv, wo = w["wqk"], w["wv"], w["wo"]
    cos, sin = w["cos"], w["sin"]

    with ExitStack() as ctx:
        sb = lambda n, shape, dt=FP32: ctx.enter_context(nc.sbuf_tensor(name + n, shape, dt))
        ps = lambda n, shape: ctx.enter_context(nc.psum_tensor(name + n, shape, FP32))
        sem = lambda n: nc.alloc_semaphore(name + n)

        staged = sb("staged", [P, QT, D])
        hT = sb("hT", [P, 2, T])
        sq = sb("sq", [P, 2 * W])
        ss = sb("ss", [P, QT, 2 * H])
        rn = sb("rn", [P, QT, 2 * H])
        part = sb("part", [P, 2, 2 * W])
        rot = sb("rot", [P, 2 * W])
        qk = sb("qk", [P, QT, 2 * W])
        qm = sb("qm", [P, 2, NP, NW, 2, 64])
        kT = sb("kT", [P, 2, NP, T])
        v = sb("v", [P, 2, 3, W])
        nm = sb("nm", [P, 2, NW])
        Z = sb("Z", [P, 2, NW])
        rz = sb("rz", [P, 2, NW])
        E = sb("E", [P, 2, NW, P])
        d = sb("d", [P, 2, NW, P])
        dT = sb("dT", [P, 2, NW, 2, 64])
        OT = sb("OT", [P, 2, NP, T])

        psQ = ps("psQ", [P, 2 * W])
        psS = ps("psS", [P, 2, 512])
        psT = ps("psT", [P, 512])
        psO = ps("psO", [P, T])
        psM = ps("psM", [P, 2, 512])

        U_TQ0, U_TK0, U_V0, U_TQ1, U_TK1, U_WO, U_V2, U_HT = range(8)
        USES, PRE = 8, 9
        PEELED = ((U_HT, 0), (U_V0, 0), (U_V2, 0), (U_HT, 1), (U_TQ0, 0), (U_TK0, 0), (U_TQ1, 0),
                  (U_TK1, 0), (U_HT, 2))
        bank = lambda use: (PRE + use) % 2
        misc_full = Signal(sem("misc_full"), USES, PRE)
        misc_free = Signal(sem("misc_free"), USES, PRE)
        qk_full = Signal(sem("qk_full"), QT, 2 * QT)
        squared = Signal(sem("squared"), QT, 2 * QT)
        ss_ready = Signal(sem("ss_ready"), QT, 2 * QT)
        rn_ready = Signal(sem("rn_ready"), QT, 2 * QT)
        parts = Signal(sem("parts"), QT, 2 * QT)
        summed = Signal(sem("summed"), QT, 2 * QT)
        qk_ready = Signal(sem("qk_ready"), QT, 2 * QT)
        scored = Signal(sem("scored"), NP)
        maxed = Signal(sem("maxed"), NP)
        exped = Signal(sem("exped"), NP, 2)
        mixed = Signal(sem("mixed"), NP, 2)
        turned = Signal(sem("turned"), NP, 2)
        evaced = Signal(sem("evaced"), NP, 2)
        pved = Signal(sem("pved"), NP, 2)
        otmoved = Signal(sem("otmoved"), NP, 1)
        stage_full = Signal(sem("stage_full"), 1, 3)
        v_moved = [sem("v_moved_even"), sem("v_moved_odd")]
        zeroed = sem("zeroed")
        cleared = sem("cleared")
        own = Chain(sem("own"), CHAIN_B, 4)

        block = ctx.enter_context(nc.Block())
        LAST = BATCH // 2

        def f_of(pair, half):
            return F[:, bass.ds((pair * 2 + (half + 1)) * QT, QT), :]

        @block.sync
        def _(sp):
            open_signals(sp)

            def move_v(p):
                sp.dma_start(v[0:64, p, 1, :], v[64:P, p, 0, :]).then_inc(v_moved[p], 16)
                sp.dma_start(v[64:P, p, 1, :], v[0:64, p, 2, :]).then_inc(v_moved[p], 16)

            sp.wait_ge(cleared, 3)
            sp.wait_ge(misc_free.sem, misc_free.early(3))
            move_v(0)
            with sp.Fori(0, LAST) as pair:
                for half in range(2):
                    sp.wait_ge(misc_free.sem, misc_free.at(pair, half, U_V2 + 1))
                    move_v(1 - half)
            sp.wait_ge(v_moved[0], 32 * (LAST + 1))
            sp.wait_ge(v_moved[1], 32 * LAST)

        @block.gpsimd
        def _(pool):
            def stage(pair, half):
                pool.tensor_copy(staged[:, :, :], f_of(pair, half)).then_inc(stage_full.sem, 1)

            def norms_and_sum(pair, half, t):
                pool.wait_ge(ss_ready.sem, ss_ready.at(pair, half, t + 1))
                pool.tensor_tensor(rn[:, t, :], ss[:, t, :], minus_half[:, 0:2 * H], ALU.pow).then_inc(rn_ready.sem, 1)
                pool.wait_ge(parts.sem, parts.at(pair, half, t + 1))
                pool.wait_ge(qk_ready.sem, qk_ready.at(pair, half, t))
                pool.tensor_tensor(rot[:, :], part[:, 0, :], part[:, 1, :], ALU.add).then_inc(summed.sem, 1)

            stage(0, 0)
            for tile in (dT, v, OT):
                pool.memset(tile[:, 1], 0.0).then_inc(cleared, 1)
            pool.wait_ge(misc_full.sem, misc_full.early(1))
            stage(0, 1)
            for t in range(QT):
                norms_and_sum(0, -2, t)
            pool.wait_ge(misc_full.sem, misc_full.early(4))
            stage(0, 2)
            for t in range(QT):
                norms_and_sum(0, -1, t)
            with pool.Fori(0, LAST) as pair:
                for half in range(2):
                    pool.wait_ge(misc_full.sem, misc_full.at(pair, half - 1, U_HT + 1))
                    stage(pair, half + 3)
                    for t in range(QT):
                        norms_and_sum(pair, half, t)

        @block.vector
        def _(dve):
            src = psQ[:, :].rearrange("p (a h e) -> p a h e", a=2, e=HD)
            out = part[:, :, :].rearrange("p b (a h e) -> p b a h e", a=2, e=HD)
            tab = lambda a, t, lo, n: a[:, t, :, lo:lo + n].unsqueeze(2).broadcast_to([P, 2, H, n])

            def norms(pair, half, t):
                dve.wait_ge(squared.sem, squared.at(pair, half, t + 1))
                dve.wait_ge(rn_ready.sem, rn_ready.at(pair, half, t - 1))
                own.mark(dve.tensor_reduce(ss[:, t, :], sq[:, :].rearrange("p (h e) -> p h e", e=HD),
                                           axis=AX.X, op=ALU.add))
                own.last()
                dve.tensor_scalar(ss[:, t, :], ss[:, t, :], 1e-24, None, ALU.max).then_inc(ss_ready.sem, 1)

            def rotate(pair, half, t):
                dve.wait_ge(summed.sem, summed.at(pair, half, t))
                dve.tensor_tensor(out[:, 0], src, tab(cos, t, 0, HD), ALU.mult)
                R = HD // 2
                dve.tensor_tensor(out[:, 1, :, :, 0:R], src[:, :, :, R:HD], tab(sin, t, 0, R), ALU.mult)
                dve.tensor_tensor(out[:, 1, :, :, R:HD], src[:, :, :, 0:R], tab(sin, t, R, R), ALU.mult)\
                   .then_inc(parts.sem, 1)

            def scale(pair, half, t, used=None):
                dve.wait_ge(summed.sem, summed.at(pair, half, t + 1))
                dve.wait_ge(rn_ready.sem, rn_ready.at(pair, half, t + 1))
                if used is not None:
                    dve.wait_ge(misc_full.sem, used)
                dve.tensor_tensor(qk[:, t, :].rearrange("p (h e) -> p h e", e=HD),
                                  rot[:, :].rearrange("p (h e) -> p h e", e=HD),
                                  rn[:, t, :].unsqueeze(2).broadcast_to([P, 2 * H, HD]), ALU.mult)\
                   .then_inc(qk_ready.sem, 1)

            def maxima(pair, half, g):
                s = g % 2
                dve.wait_ge(scored.sem, scored.at(pair, half, g + 1))
                dve.tensor_reduce(nm[:, s, :], psS[:, s, :].rearrange("p (w k) -> p w k", k=P), axis=AX.X,
                                  op=ALU.max, negate=True).then_inc(maxed.sem, 1)

            def inverse(pair, half, g):
                s = g % 2
                dve.wait_ge(exped.sem, exped.at(pair, half, g + 1))
                return own.mark(dve.reciprocal(rz[:, s, :], Z[:, s, :]))

            def normalise(pair, half, g, k):
                s = g % 2
                dve.wait_ge(turned.sem, turned.at(pair, half, g - 1))
                own.wait(k)
                dve.tensor_tensor(d[:, s], E[:, s], rz[:, s, :].unsqueeze(2).broadcast_to([P, NW, P]), ALU.mult)\
                   .then_inc(mixed.sem, 1)

            def residual(pair, half, full, m):
                dve.wait_ge(misc_full.sem, full)
                fs = f_of(pair, half - 1)
                dve.tensor_tensor(fs, psM[:, m, 0:T].rearrange("p (t n) -> p t n", t=QT), fs, ALU.add)\
                   .then_inc(misc_free.sem, 1)

            dve.memset(hT[:, :, 0:1], 0.0).then_inc(zeroed, 1)
            dve.memset(psO[:, :], 0.0).then_inc(zeroed, 1)
            dve.memset(qm[:], 0.0).then_inc(zeroed, 1)
            own.begin(dve, 0, 0)
            own.restart(0)
            norms(0, -2, 0)
            rotate(0, -2, 0)
            norms(0, -2, 1)
            scale(0, -2, 0)
            rotate(0, -2, 1)
            norms(0, -1, 0)
            scale(0, -2, 1)
            rotate(0, -1, 0)
            maxima(0, 0, 0)
            norms(0, -1, 1)
            scale(0, -1, 0, misc_full.early(PRE))
            rotate(0, -1, 1)
            assert own.k == 4
            own.restart(own.k)
            with dve.Fori(0, LAST) as pair:
                for half in range(2):
                    own.begin(dve, pair, half)
                    for s in range(NP):
                        k = inverse(pair, half, s)
                        maxima(pair, half + (s + 1) // NP, (s + 1) % NP)
                        normalise(pair, half, s, k)
                        if s == 0:
                            scale(pair, half - 1, 1, misc_full.at(pair, half, 0))
                            norms(pair, half, 0)
                        if s == 1:
                            rotate(pair, half, 0)
                        if s == 2:
                            scale(pair, half, 0, misc_full.at(pair, half, U_TK0 + 1))
                            norms(pair, half, 1)
                        if s == 3:
                            residual(pair, half, misc_full.at(pair, half, U_WO + 1), bank(U_WO))
                            rotate(pair, half, 1)
                    own.end()
            residual(LAST, 0, misc_full.at(LAST, 0, 1), bank(0))

        @block.scalar
        def _(act):
            def exps(pair, half, g):
                s = g % 2
                act.wait_ge(maxed.sem, maxed.at(pair, half, g + 1))
                act.wait_ge(mixed.sem, mixed.at(pair, half, g - 1))
                for n in range(NW):
                    ins = act.activation(E[:, s, n, :], psS[:, s, n * P:(n + 1) * P], ACT.Exp, bias=nm[:, s, n:n + 1],
                                         accum_out=Z[:, s, n:n + 1])
                ins.then_inc(exped.sem, 1)

            def evac_d(pair, half, g):
                s = g % 2
                act.wait_ge(turned.sem, turned.at(pair, half, g + 1))
                act.wait_ge(pved.sem, pved.at(pair, half, g - 1))
                act.activation(dT[:, s].rearrange("p w j q -> p (w j q)"), psT[:, :], ACT.Copy)\
                   .then_inc(evaced.sem, 1)

            def move_ot(pair, half, g, p):
                act.wait_ge(pved.sem, pved.at(pair, half, g + 1))
                if g == 0:
                    act.wait_ge(misc_full.sem, misc_full.at(pair, half - 1, U_WO + 1))
                act.activation(OT[:, p, g, :], psO[:, :], ACT.Copy).then_inc(otmoved.sem, 1)

            def square(pair, half, t):
                act.wait_ge(qk_full.sem, qk_full.at(pair, half, t + 1))
                act.wait_ge(ss_ready.sem, ss_ready.at(pair, half, t))
                act.activation(sq[:, :], psQ[:, :], ACT.Square).then_inc(squared.sem, 1)

            def use_copy(use, p, full, m):
                act.wait_ge(misc_full.sem, full)
                if use == U_HT:
                    act.activation(hT[0:64, p, :], psM[0:64, m, 0:T], ACT.Copy)
                    ins = act.activation(hT[64:P, p, 1:T], psM[64:P, m, 0:T - 1], ACT.Copy)
                elif use in (U_V0, U_V2):
                    ins = act.activation(v[:, p, 2 * (use == U_V2), :], psM[:, m, :], ACT.Copy)
                elif use in (U_TQ0, U_TQ1):
                    n = 2 * (use == U_TQ1)
                    for j in range(2):
                        rows = slice(64 * j, 64 * j + 64)
                        ins = act.activation(qm[rows, p, :, n:n + 2, j, :],
                                             psM[rows, m, :].rearrange("p (g w q) -> p g w q", w=2, q=64), ACT.Copy)
                else:
                    c = P * (use == U_TK1)
                    ins = act.activation(kT[:, p, :, c:c + P], psM[:, m, :].rearrange("p (n t) -> p n t", t=P), ACT.Copy)
                ins.then_inc(misc_free.sem, 1)

            act.wait_ge(zeroed, 1)
            for signal, n in ((exped, 2), (mixed, 2), (turned, 2), (evaced, 2), (pved, 1)):
                act.sem_inc(signal.sem, n)
            for n, (use, batch) in enumerate(PEELED):
                if use == U_TQ0:
                    act.wait_ge(zeroed, 3)
                    act.wait_ge(cleared, 3)
                use_copy(use, batch % 2, misc_full.early(n + 1), n % 2)
                if n < 2:
                    square(0, -2, n)
                if use == U_TK0:
                    square(0, -1, 0)
            exps(0, 0, 0)
            square(0, -1, 1)
            with act.Fori(0, LAST) as pair:
                for half in range(2):
                    copy = lambda use: use_copy(use, 1 - half, misc_full.at(pair, half, use + 1), bank(use))
                    for s in range(NP):
                        exps(pair, half + (s + 1) // NP, (s + 1) % NP)
                        if s in (0, 2):
                            square(pair, half, s // 2)
                        if s != 2:
                            copy((U_TQ0, U_TQ1, None, U_V2)[s])
                        evac_d(pair, half, s)
                        if s < 2:
                            copy((U_TK0, U_TK1)[s])
                        if s == 3:
                            copy(U_HT)
                        move_ot(pair, half - (s == 0), (s - 1) % NP, 1 - half if s == 0 else half)
                        if s == 0:
                            act.wait_ge(pved.sem, pved.at(pair, half, 0))
                            copy(U_V0)
            move_ot(LAST, -1, NP - 1, 1)

        @block.tensor
        def _(pe):
            def scores(pair, half, g):
                s, p = g % 2, half % 2
                pe.wait_ge(exped.sem, exped.at(pair, half, g - 1))
                pe.matmul(psS[:, s, :], identb[:, :], behind[:, :], start=True, stop=False)
                for n in range(NW):
                    ins = pe.matmul(psS[:, s, n * P:(n + 1) * P], qm[:, p, g, n].rearrange("p j q -> p (j q)"),
                                    kT[:, p, g, KEYS[n]:KEYS[n] + P], start=False, stop=(n == NW - 1))
                ins.then_inc(scored.sem, 1)

            def turn(pair, half, g):
                s = g % 2
                pe.wait_ge(mixed.sem, mixed.at(pair, half, g + 1))
                pe.wait_ge(evaced.sem, evaced.at(pair, half, g))
                for n in range(NW):
                    ins = pe.transpose(psT[:, n * P:(n + 1) * P], d[:, s, n, :], ident[:, :])
                ins.then_inc(turned.sem, 1)

            def outputs(pair, half, g):
                s, p = g % 2, half % 2
                pe.wait_ge(evaced.sem, evaced.at(pair, half, g + 1))
                pe.wait_ge(otmoved.sem, otmoved.at(pair, half, g))
                for j in range(2):
                    h = 2 * g + j
                    out = psO[64 * j:64 * j + 64, :]
                    vh = lambda t: v[:, p, t, h * HD:(h + 1) * HD]
                    pe.matmul(out[:, 0:P], vh(0), dT[:, s, 0:2, j, :], start=True, stop=True)
                    pe.matmul(out[:, P:192], vh(1), dT[:, s, 2, j, :], start=True, stop=True)
                    ins = pe.matmul(out[:, 192:T], vh(2), dT[:, s, 3, j, :], start=True, stop=True)
                ins.then_inc(pved.sem, 1)

            def project(pair, half, t):
                p = half % 2
                pe.wait_ge(parts.sem, parts.at(pair, half, t))
                for n in range(2):
                    ins = pe.matmul(psQ[:, n * W:(n + 1) * W], hT[:, p, t * P:(t + 1) * P],
                                    wqk[:, n * W:(n + 1) * W], start=True, stop=True)
                ins.then_inc(qk_full.sem, 1)

            def use_misc(use, free, p, m):
                out = psM[:, m, :]
                pe.wait_ge(misc_free.sem, free)
                if use == U_HT:
                    for t in range(QT):
                        ins = pe.transpose(out[:, t * P:(t + 1) * P], staged[:, t, :], ident[:, :])
                elif use == U_WO:
                    for t in range(QT):
                        for n in range(NP):
                            ins = pe.matmul(out[:, t * P:(t + 1) * P], OT[:, p, n, t * P:(t + 1) * P], wo[:, n, :],
                                            start=(n == 0), stop=(n == NP - 1))
                elif use in (U_V0, U_V2):
                    t = P * (use == U_V2)
                    ins = pe.matmul(out, hT[:, p, t:t + P], wv[:, :], start=True, stop=True)
                else:
                    t, a = int(use in (U_TQ1, U_TK1)), int(use in (U_TK0, U_TK1))
                    for n in range(NP):
                        ins = pe.transpose(out[:, n * P:(n + 1) * P],
                                           qk[:, t, a * W + n * P:a * W + (n + 1) * P], ident[:, :])
                ins.then_inc(misc_full.sem, 1)

            for n, (use, batch) in enumerate(PEELED):
                if n == 1:
                    pe.wait_ge(misc_free.sem, misc_free.early(1))
                    project(0, -2, 0)
                if n == 2:
                    project(0, -2, 1)
                if use == U_HT:
                    pe.wait_ge(stage_full.sem, stage_full.early(1 + batch))
                if use in (U_TQ0, U_TQ1):
                    pe.wait_ge(qk_ready.sem, qk_ready.early(1 + (use == U_TQ1)))
                if n < 2:
                    use_misc(use, misc_free.early(0), 0, n)
                else:
                    use_misc(use, misc_free.early(n - 1), 0, n % 2)
                if use == U_TK0:
                    pe.wait_ge(misc_free.sem, misc_free.early(4))
                    project(0, -1, 0)
            pe.wait_ge(misc_free.sem, misc_free.early(PRE))
            pe.wait_ge(zeroed, 3)
            pe.wait_ge(cleared, 3)
            scores(0, 0, 0)
            scores(0, 0, 1)
            project(0, -1, 1)
            project(0, 0, 0)
            with pe.Fori(0, LAST) as pair:
                for half in range(2):
                    use = lambda u: use_misc(u, misc_free.at(pair, half, u - 1 + (u in (U_V2, U_HT))), 1 - half,
                                             bank(u))
                    for s in range(NP):
                        if s == 2:
                            pe.wait_ge(misc_free.sem, misc_free.at(pair, half, U_TK1 + 1))
                        scores(pair, half + (s + 2) // NP, (s + 2) % NP)
                        if s < 2:
                            pe.wait_ge(qk_ready.sem, qk_ready.at(pair, half - 1, s + 1))
                        if s != 2:
                            use((U_TQ0, U_TQ1, None, U_V2)[s])
                        turn(pair, half, s)
                        if s == 2:
                            pe.wait_ge(otmoved.sem, otmoved.at(pair, half, 0))
                        if s == 3:
                            pe.wait_ge(stage_full.sem, stage_full.at(pair, half, 1))
                        use((U_TK0, U_TK1, U_WO, U_HT)[s])
                        if s == 1:
                            pe.wait_ge(v_moved[half], pair * 32 + 32)
                        outputs(pair, half - 1 if s == 0 else half, (s - 1) % NP)
                        if s == 0:
                            use(U_V0)
                        if s == 1:
                            project(pair, half, 1)
                        if s == 3:
                            pe.wait_ge(misc_free.sem, misc_free.at(pair, half, U_HT + 1))
                            project(pair, half + 1, 0)
            outputs(LAST, -1, NP - 1)
            pe.wait_ge(otmoved.sem, otmoved.at(LAST, 0, 0))
            use_misc(U_WO, misc_free.at(LAST, 0, 0), 1, bank(0))


def feed_forward(nc, name, F, consts, w):
    NT = 4
    N = NT * P
    PAIRS = TILES // NT // 2
    HID = 341
    parts = [(j, min(P, HID - P * j)) for j in range((HID + P - 1) // P)]
    J = len(parts)
    ident, minus_half = consts["ident"], consts["minus_half"]
    w1, b1, w2, b2, lg, lb = (w[k] for k in ("w1", "b1", "w2", "b2", "ln_g", "ln_b"))

    with ExitStack() as ctx:
        sb = lambda n, shape, dt=FP32: ctx.enter_context(nc.sbuf_tensor(name + n, shape, dt))
        ps = lambda n, shape: ctx.enter_context(nc.psum_tensor(name + n, shape, FP32))
        sem = lambda n: nc.alloc_semaphore(name + n)
        z = sb("z", [P, 2, NT, D])
        st = sb("st", [P, NT, 6])
        mv = sb("mv", [P, NT, 2])
        rs = sb("rs", [P, NT])
        xn = sb("xn", [P, NT, D])
        hT = sb("hT", [P, N])
        gg = sb("gg", [P, J, N])
        u = sb("u", [P, J, N])
        fb = sb("fb", [P, NT, D])
        psG = ps("psG", [P, J, N])
        psA = ps("psA", [P, J, N])
        psX = ps("psX", [P, N])
        psY = ps("psY", [P, N])

        shifted = [sem("shifted"), sem("shifted_odd")]
        g_full = Signal(sem("g_full"), J)
        a_full = Signal(sem("a_full"), J)
        gelued = Signal(sem("gelued"), J)
        gated = Signal(sem("gated"), J)
        var_ready = Signal(sem("var_ready"), 1, 1)
        rs_ready = Signal(sem("rs_ready"), 1, 1)
        xn_ready = Signal(sem("xn_ready"), 1, 1)
        x_full = Signal(sem("x_full"), 1, 1)
        h_ready = Signal(sem("h_ready"), 1, 1)
        y_full = Signal(sem("y_full"), 1)
        added = Signal(sem("added"), 1)
        fb_ready = Signal(sem("fb_ready"), 1)
        zeroed = sem("zeroed")
        own = Chain(sem("own"), CHAIN_F, 2)
        block = ctx.enter_context(nc.Block())

        def f_of(pair, half):
            return F[:, bass.ds((pair * 2 + half) * NT + QT, NT), :]

        def z_landed(eng, pair, half):
            eng.wait_ge(shifted[half % 2], (pair + half // 2) * 48 + 48)

        @block.sync
        def _(sp):
            open_signals(sp)
            def shift(pair, half):
                done = shifted[half % 2]
                p, fs = half % 2, f_of(pair, half)
                sp.dma_start(z[:, p, :, 0:64], fs[:, :, 0:64]).then_inc(done, 16)
                sp.dma_start(z[1:P, p, :, 64:D], fs[0:P - 1, :, 64:D]).then_inc(done, 16)
                sp.dma_start(z[0:1, p, 1::2, 64:D], fs[P - 1:P, 0::2, 64:D]).then_inc(done, 16)

            sp.wait_ge(zeroed, 1)
            shift(0, 0)
            shift(0, 1)
            with sp.Fori(0, PAIRS - 1) as pair:
                for half in range(2):
                    sp.wait_ge(xn_ready.sem, xn_ready.at(pair, half, 0))
                    shift(pair, half + 2)
            sp.wait_ge(xn_ready.sem, xn_ready.at(PAIRS - 1, 0, 0))
            shift(PAIRS - 1, 2)

        @block.gpsimd
        def _(pool):
            pool.memset(z[0:1, :, 0::2, 64:D], 0.0).then_inc(zeroed, 1)

            def rstd(pair, half, k):
                pool.wait_ge(var_ready.sem, var_ready.at(pair, half, k))
                pool.tensor_tensor(rs[:, :], mv[:, :, 1], minus_half[:, 0:NT], ALU.pow).then_inc(rs_ready.sem, 1)

            rstd(0, 0, 0)
            with pool.Fori(0, PAIRS) as pair:
                for half in range(2):
                    rstd(pair, half, 1)
                    pool.wait_ge(added.sem, added.at(pair, half, 0))
                    pool.tensor_tensor(fb[:, :, :], f_of(pair, half), b2[:, :].unsqueeze(1).broadcast_to([P, NT, D]),
                                       ALU.add).then_inc(fb_ready.sem, 1)

        @block.vector
        def _(dve):
            def variance(pair, half):
                z_landed(dve, pair, half)
                for t in range(NT):
                    ins = dve.bn_stats(st[:, t, :], z[:, half % 2, t, :])
                own.mark(ins)
                own.last()
                apart(dve, APART["dve"])
                for t in range(NT):
                    ins = dve.bn_aggr(mv[:, t, :], st[:, t, :])
                own.mark(ins)
                own.last()
                dve.tensor_scalar(mv[:, :, 1], mv[:, :, 1], EPS_LN, None, ALU.add).then_inc(var_ready.sem, 1)

            def normalise(pair, half, k):
                dve.wait_ge(rs_ready.sem, rs_ready.at(pair, half, k))
                if k:
                    dve.wait_ge(x_full.sem, x_full.at(pair, half, 0))
                for t in range(NT):
                    ins = dve.tensor_scalar(xn[:, t, :], z[:, (half + k) % 2, t, :], mv[:, t, 0:1], rs[:, t:t + 1],
                                            ALU.subtract, ALU.mult)
                ins.then_inc(xn_ready.sem, 1)

            own.begin(dve, 0, 0)
            own.restart(0)
            variance(0, 0)
            own.restart(own.k)
            normalise(0, 0, 0)
            with dve.Fori(0, PAIRS) as pair:
                for half in range(2):
                    own.begin(dve, pair, half)
                    variance(pair, half + 1)
                    for j, m in parts:
                        dve.wait_ge(gelued.sem, gelued.at(pair, half, j + 1))
                        dve.wait_ge(a_full.sem, a_full.at(pair, half, j + 1))
                        dve.wait_ge(y_full.sem, y_full.at(pair, half, 0))
                        dve.scalar_tensor_tensor(out=u[0:m, j, :], in0=psA[0:m, j, :], scalar=b1[0:m, j:j + 1],
                                                 in1=gg[0:m, j, :], op0=ALU.add, op1=ALU.mult).then_inc(gated.sem, 1)
                        if j == 0:
                            normalise(pair, half, 1)
                    dve.wait_ge(y_full.sem, y_full.at(pair, half, 1))
                    dve.wait_ge(fb_ready.sem, fb_ready.at(pair, half, 1))
                    dve.tensor_tensor(f_of(pair, half), psY[:, :].rearrange("p (t n) -> p t n", t=NT), fb[:, :, :],
                                      ALU.add).then_inc(added.sem, 1)
                    own.end()

        @block.scalar
        def _(act):
            def take_x(full):
                act.wait_ge(x_full.sem, full)
                act.activation(hT[:, :], psX[:, :], ACT.Identity, scale=lg[:, 0:1], bias=lb[:, 0:1])\
                   .then_inc(h_ready.sem, 1)

            take_x(x_full.early(1))
            with act.Fori(0, PAIRS) as pair:
                for half in range(2):
                    for j, m in parts:
                        act.wait_ge(g_full.sem, g_full.at(pair, half, j + 1))
                        act.wait_ge(gated.sem, gated.at(pair, half, 0))
                        act.activation(gg[0:m, j, :], psG[0:m, j, :], ACT.Gelu, bias=b1[0:m, J + j:J + j + 1])\
                           .then_inc(gelued.sem, 1)
                    take_x(x_full.at(pair, half, 1))

        @block.tensor
        def _(pe):
            def turn_x(full):
                pe.wait_ge(xn_ready.sem, full)
                for t in range(NT):
                    ins = pe.transpose(psX[:, t * P:(t + 1) * P], xn[:, t, :], ident[:, :])
                ins.then_inc(x_full.sem, 1)

            turn_x(xn_ready.early(1))
            with pe.Fori(0, PAIRS) as pair:
                for half in range(2):
                    pe.wait_ge(h_ready.sem, h_ready.at(pair, half, 0))
                    pe.wait_ge(gelued.sem, gelued.at(pair, half, 0))
                    pe.wait_ge(gated.sem, gated.at(pair, half, 0))
                    for j in range(J + 1):
                        if j < J:
                            c, m = HID + parts[j][0] * P, parts[j][1]
                            pe.matmul(psG[0:m, j, :], w1[:, c:c + m], hT[:, :], start=True, stop=True)\
                              .then_inc(g_full.sem, 1)
                        if j >= 1:
                            c, m = parts[j - 1][0] * P, parts[j - 1][1]
                            pe.matmul(psA[0:m, j - 1, :], w1[:, c:c + m], hT[:, :], start=True, stop=True)\
                              .then_inc(a_full.sem, 1)
                    turn_x(xn_ready.at(pair, half, 1))
                    pe.wait_ge(gated.sem, gated.at(pair, half, J))
                    pe.wait_ge(added.sem, added.at(pair, half, 0))
                    for t in range(NT):
                        for j, m in parts:
                            ins = pe.matmul(psY[:, t * P:(t + 1) * P], u[0:m, j, t * P:(t + 1) * P], w2[0:m, j, :],
                                            start=(j == 0), stop=(j == J - 1))
                    ins.then_inc(y_full.sem, 1)


def state_space(nc, F, consts, w):
    NS, GROUPS = 32, 4
    SEQ = BATCH // GROUPS
    N = SEQ * T
    LEVELS = T.bit_length() - 1
    ident = consts["ident"]
    win, bin_, bm, am, amT, cT, dv = (w[k] for k in ("W_in", "b_in", "Bm", "A", "AT", "C", "D"))

    with ExitStack() as ctx:
        sb = lambda n, shape, dt=FP32: ctx.enter_context(nc.sbuf_tensor("s_" + n, shape, dt))
        ps = lambda n, shape: ctx.enter_context(nc.psum_tensor("s_" + n, shape, FP32))
        sem = lambda n: nc.alloc_semaphore("s_" + n)
        xT = sb("xT", [P, 2, T])
        U = sb("U", [P, N])
        Hs = sb("H", [P, SEQ, T])
        pw = sb("pw", [P, 2, 2, P])
        psX = ps("psX", [P, 2, 512])
        psU = ps("psU", [P, 2, 512])
        psH = ps("psH", [P, 2, 512])
        psP = ps("psP", [P, 512])

        x_full, xT_ready, u_full, u_ready = (
            sem(n) for n in ("x_full", "xT_ready", "u_full", "u_ready"))
        b_full, h_ready, level_full, p_full, p_ready = (
            sem(n) for n in ("b_full", "h_ready", "level_full", "p_full", "p_ready"))
        y_full, y_ready = sem("y_full"), sem("y_ready")
        block = ctx.enter_context(nc.Block())

        def f_of(b):
            return F[:, QT + b * QT:QT + (b + 1) * QT, :]

        @block.scalar
        def _(act):
            for b in range(BATCH):
                act.wait_ge(x_full, b + 1)
                if b >= 2:
                    act.wait_ge(u_full, b - 1)
                act.activation(xT[:, b % 2, :], psX[:, b % 2, 0:T], ACT.Copy).then_inc(xT_ready, 1)
            for c in range(2):
                act.wait_ge(u_full, BATCH)
                act.activation(U[:, c * 512:(c + 1) * 512], psU[:, c, :], ACT.Identity, bias=bin_[:, 0:1])\
                   .then_inc(u_ready, 1)
            for l in range(LEVELS - 1):
                act.wait_ge(p_full, l + 1)
                if l >= 1:
                    act.wait_ge(level_full, 2 * l)
                act.activation(pw[:, (l + 1) % 2, :, :], psP[:, 0:T].rearrange("p (a n) -> p a n", a=2), ACT.Copy)\
                   .then_inc(p_ready, 1)

        @block.vector
        def _(dve):
            dve.tensor_copy(pw[:, 0, 0, :], am[:, :]).then_inc(p_ready, 1)
            dve.tensor_copy(pw[:, 0, 1, :], amT[:, :]).then_inc(p_ready, 1)
            for c in range(2):
                dve.wait_ge(b_full, c + 1)
                dve.tensor_copy(Hs[:, 2 * c:2 * c + 2, :], psH[:, c, :].rearrange("p (a t) -> p a t", a=2))\
                   .then_inc(h_ready, 1)
            for l in range(LEVELS):
                k = 2 ** l
                for c in range(2):
                    dve.wait_ge(level_full, 2 * l + c + 1)
                    dve.wait_ge(h_ready, 2 * l + c + 1)
                    hs = Hs[:, 2 * c:2 * c + 2, k:T]
                    dve.tensor_tensor(hs, psH[:, c, 0:2 * (T - k)].rearrange("p (a t) -> p a t", a=2), hs, ALU.add)\
                       .then_inc(h_ready, 1)
            for b in range(BATCH):
                dve.wait_ge(y_full, b + 1)
                dve.tensor_tensor(f_of(b), psX[:, b % 2, 0:T].rearrange("p (t n) -> p t n", t=QT),
                                  dv[:, :].unsqueeze(1).broadcast_to([P, QT, D]), ALU.add).then_inc(y_ready, 1)

        @block.tensor
        def _(pe):
            def inputs(b):
                g, j = divmod(b, SEQ)
                pe.wait_ge(xT_ready, b + 1)
                pe.matmul(psU[NS * g:NS * g + NS, j // 2, (j % 2) * T:(j % 2) * T + T], win[:, :], xT[:, b % 2, :],
                          start=True, stop=True).then_inc(u_full, 1)

            for b in range(BATCH):
                if b >= 2:
                    pe.wait_ge(xT_ready, b - 1)
                for t in range(QT):
                    ins = pe.transpose(psX[:, b % 2, t * P:(t + 1) * P], f_of(b)[:, t, :], ident[:, :])
                ins.then_inc(x_full, 1)
                if b >= 1:
                    inputs(b - 1)
            inputs(BATCH - 1)
            for c in range(2):
                pe.wait_ge(u_ready, c + 1)
                pe.matmul(psH[:, c, :], bm[:, :], U[:, c * 512:(c + 1) * 512], start=True, stop=True).then_inc(b_full, 1)
            pe.wait_ge(p_ready, 2)
            for l in range(LEVELS):
                k = 2 ** l
                if l:
                    pe.wait_ge(p_ready, 2 + l)
                a, aT = pw[:, l % 2, 0, :], pw[:, l % 2, 1, :]
                for c in range(2):
                    pe.wait_ge(h_ready, 2 * l + c + 1)
                    pe.matmul(psH[:, c, 0:2 * (T - k)], a, Hs[:, 2 * c:2 * c + 2, 0:T - k], start=True, stop=True)\
                      .then_inc(level_full, 1)
                    if c == 0 and l < LEVELS - 1:
                        pe.matmul(psP[:, 0:P], aT, a, start=True, stop=True)
                        pe.matmul(psP[:, P:T], a, aT, start=True, stop=True).then_inc(p_full, 1)
            pe.wait_ge(h_ready, 2 * LEVELS + 2)
            for b in range(BATCH):
                g, j = divmod(b, SEQ)
                if b >= 2:
                    pe.wait_ge(y_ready, b - 1)
                for t in range(QT):
                    rows = slice(NS * g, NS * g + NS)
                    ins = pe.matmul(psX[:, b % 2, t * P:(t + 1) * P], Hs[rows, j, t * P:(t + 1) * P], cT[rows, :],
                                    start=True, stop=True)
                ins.then_inc(y_full, 1)


def mixture_of_experts(nc, X, F, out, consts, w):
    NT = 4
    N = NT * P
    PAIRS = TILES // NT // 2
    NE, HID = 8, 256
    J = HID // P
    ident, minus_half, eid = consts["ident"], consts["minus_half"], consts["expert_id"]
    wr, wg, wu, wd = w["router"], w["gate"], w["up"], w["down"]

    with ExitStack() as ctx:
        sb = lambda n, shape, dt=FP32: ctx.enter_context(nc.sbuf_tensor("mx_" + n, shape, dt))
        ps = lambda n, shape: ctx.enter_context(nc.psum_tensor("mx_" + n, shape, FP32))
        sem = lambda n: nc.alloc_semaphore("mx_" + n)
        staged = sb("staged", [P, NT, D])
        hT = sb("hT", [P, 2, N])
        lo = sb("lo", [P, NT, NE])
        top = sb("top", [P, NT, 8])
        idx = sb("idx", [P, NT, 8], mybir.dt.uint32)
        idf = sb("idf", [P, NT, 2])
        sg = sb("sg", [P, NT, 2])
        gs = sb("gs", [P, NT])
        gate = sb("gate", [P, 2, NT, NE])
        pick = sb("pick", [P, NT, NE])
        sl = sb("sl", [P, 2, J, N])
        h = sb("h", [P, 2, J, N])
        Y = sb("Y", [P, 2, NT, D])
        yn = sb("yn", [P, NT, D])
        res = sb("res", [P, 2, NT, D])
        st = sb("st", [P, NT, 6])
        mv = sb("mv", [P, NT, 2])
        rs = sb("rs", [P, NT])
        psG = ps("psG", [P, J, N])
        psU = ps("psU", [P, J, N])
        psY = ps("psY", [P, 2, N])
        psX = ps("psX", [P, N])
        psR = ps("psR", [P, 512])

        stage_full = Signal(sem("stage_full"), 1, 1)
        x_full = Signal(sem("x_full"), 1, 1)
        h_ready = Signal(sem("h_ready"), 1, 1)
        r_full = Signal(sem("r_full"), 1, 1)
        picked = Signal(sem("picked"), 1, 1)
        expd = Signal(sem("expd"), 1, 1)
        gated = Signal(sem("gated"), 1, 1)
        g_full = Signal(sem("g_full"), NE * J)
        u_full = Signal(sem("u_full"), NE * J)
        silued = Signal(sem("silued"), NE * J)
        h_full = Signal(sem("h_full"), NE * J)
        y_full = Signal(sem("y_full"), NE)
        y_used = Signal(sem("y_used"), NE)
        var_ready = Signal(sem("var_ready"), 1)
        rs_ready = Signal(sem("rs_ready"), 1)
        x_moved = Signal(sem("x_moved"), 1)
        res_ready = Signal(sem("res_ready"), 1)
        stored = [sem("stored_even"), sem("stored_odd")]
        cleared = sem("cleared")
        own = Chain(sem("own"), CHAIN_M, CHAIN_M_PRE)
        block = ctx.enter_context(nc.Block())

        def tiles(a, pair, half):
            return a[:, bass.ds((pair * 2 + half) * NT + QT, NT), :]

        @block.sync
        def _(sp):
            open_signals(sp)
            o = out.rearrange("b (t p) d -> p (b t) d", p=P)
            for s in stored:
                sp.sem_inc(s, 1)
            with sp.Fori(0, PAIRS) as pair:
                for half in range(2):
                    sp.wait_ge(res_ready.sem, res_ready.at(pair, half, 2))
                    sp.dma_start(o[:, bass.ds((pair * 2 + half) * NT, NT), :], res[:, half, :, :])\
                      .then_inc(stored[half], 16)
            for s in stored:
                sp.wait_ge(s, 16 * PAIRS + 1)

        @block.gpsimd
        def _(pool):
            def power(pair, half):
                pool.wait_ge(var_ready.sem, var_ready.at(pair, half, 1))
                pool.tensor_tensor(rs[:, :], mv[:, :, 1], minus_half[:, 0:NT], ALU.pow).then_inc(rs_ready.sem, 1)

            pool.tensor_copy(staged[:, :, :], tiles(F, 0, 0)).then_inc(stage_full.sem, 1)
            with pool.Fori(0, PAIRS) as pair:
                for half in range(2):
                    pool.wait_ge(x_full.sem, x_full.at(pair, half, 0))
                    pool.tensor_copy(staged[:, :, :], tiles(F, pair, half + 1)).then_inc(stage_full.sem, 1)
                    power(pair, half)
                    pool.wait_ge(stored[half], pair * 16 + 1)
                    pool.tensor_copy(res[:, half, :, :], tiles(X, pair, half)).then_inc(x_moved.sem, 1)
            power(PAIRS, 0)

        @block.scalar
        def _(act):
            def prepare(pair, half):
                act.wait_ge(x_full.sem, x_full.at(pair, half, 0))
                act.activation(hT[:, half % 2, :], psX[:, :], ACT.Copy).then_inc(h_ready.sem, 1)

            def sigmoid_of(pair, half):
                act.wait_ge(picked.sem, picked.at(pair, half, 0))
                act.activation(sg[:, :, :], top[:, :, 0:2], ACT.Exp, scale=-1.0).then_inc(expd.sem, 1)

            prepare(0, 0)
            sigmoid_of(0, 0)
            with act.Fori(0, PAIRS) as pair:
                for half in range(2):
                    for e in range(NE):
                        for j in range(J):
                            k = e * J + j
                            act.wait_ge(g_full.sem, g_full.at(pair, half, k + 1))
                            act.wait_ge(h_full.sem, h_full.at(pair, half, max(k + 1 - 2 * J, 0)))
                            act.activation(sl[:, e % 2, j, :], psG[:, j, :], ACT.Silu).then_inc(silued.sem, 1)
                        if e == 1:
                            prepare(pair, half + 1)
                        if e == 5:
                            sigmoid_of(pair, half + 1)

        @block.vector
        def _(dve):
            def choose(pair, half):
                dve.wait_ge(r_full.sem, r_full.at(pair, half, 0))
                own.mark(dve.tensor_copy(lo[:, :, :], psR[:, 0:NT * NE].rearrange("p (t e) -> p t e", t=NT)))
                own.last()
                apart(dve, APART["dve"])
                for t in range(NT):
                    ins = dve.max(top[:, t, :], lo[:, t, :])
                ins.then_inc(picked.sem, 1)

            def experts_of(pair, half):
                dve.wait_ge(picked.sem, picked.at(pair, half, 0))
                apart(dve, APART["dve"])
                for t in range(NT):
                    ins = dve.max_index(idx[:, t, :], top[:, t, :], lo[:, t, :])
                own.mark(ins)

            def gates(pair, half):
                own.last()
                own.mark(dve.tensor_copy(idf[:, :, :], idx[:, :, 0:2]))
                dve.wait_ge(expd.sem, expd.at(pair, half, 0))
                own.mark(dve.tensor_scalar(sg[:, :, :], sg[:, :, :], 1.0, None, ALU.add))
                own.last()
                own.mark(dve.reciprocal(sg[:, :, :], sg[:, :, :]))
                own.last()
                own.mark(dve.tensor_tensor(gs[:, :], sg[:, :, 0], sg[:, :, 1], ALU.add))
                own.last()
                own.mark(dve.tensor_scalar(gs[:, :], gs[:, :], 1e-10, None, ALU.add))
                own.last()
                own.mark(dve.reciprocal(gs[:, :], gs[:, :]))
                own.last()
                own.mark(dve.tensor_tensor(sg[:, :, :], sg[:, :, :], gs[:, :].unsqueeze(2).broadcast_to([P, NT, 2]),
                                           ALU.mult))

            def spread_gates(pair, half):
                p = half % 2
                own.last()
                for t in range(NT):
                    dve.tensor_scalar(gate[:, p, t, :], eid[:, :], idf[:, t, 0:1], sg[:, t, 0:1],
                                      ALU.is_equal, ALU.mult)
                    ins = dve.tensor_scalar(pick[:, t, :], eid[:, :], idf[:, t, 1:2], sg[:, t, 1:2],
                                            ALU.is_equal, ALU.mult)
                own.mark(ins)
                own.last()
                dve.tensor_tensor(gate[:, p, :, :], gate[:, p, :, :], pick[:, :, :], ALU.add).then_inc(gated.sem, 1)

            def accumulate(pair, half, e):
                p = half % 2
                dve.wait_ge(y_full.sem, y_full.at(pair, half, e + 1))
                if e == 0:
                    dve.wait_ge(gated.sem, gated.at(pair, half, 0))
                else:
                    dve.wait_ge(y_used.sem, y_used.at(pair, half, e))
                for t in range(NT):
                    src, g = psY[:, e % 2, t * P:(t + 1) * P], gate[:, p, t, e:e + 1]
                    if e == 0:
                        ins = dve.tensor_scalar(Y[:, p, t, :], src, g, None, ALU.mult)
                    else:
                        ins = dve.scalar_tensor_tensor(out=Y[:, p, t, :], in0=src, scalar=g, in1=Y[:, p, t, :],
                                                       op0=ALU.mult, op1=ALU.add)
                ins.then_inc(y_used.sem, 1)

            def finish(pair, half, stage):
                q = (half - 1) % 2
                if stage == 0:
                    dve.wait_ge(y_used.sem, y_used.at(pair, half, 0))
                    for t in range(NT):
                        ins = dve.bn_stats(st[:, t, :], Y[:, q, t, :])
                    own.mark(ins)
                if stage == 1:
                    own.last()
                    apart(dve, APART["dve"])
                    for t in range(NT):
                        ins = dve.bn_aggr(mv[:, t, :], st[:, t, :])
                    own.mark(ins)
                if stage == 2:
                    own.last()
                    dve.tensor_scalar(mv[:, :, 1], mv[:, :, 1], EPS_LN, None, ALU.add).then_inc(var_ready.sem, 1)
                if stage == 3:
                    dve.wait_ge(rs_ready.sem, rs_ready.at(pair, half, 1))
                    for t in range(NT):
                        ins = dve.tensor_scalar(yn[:, t, :], Y[:, q, t, :], mv[:, t, 0:1], rs[:, t:t + 1],
                                                ALU.subtract, ALU.mult)
                    own.mark(ins)
                if stage == 4:
                    own.last()
                    dve.wait_ge(x_moved.sem, x_moved.at(pair, half, 0))
                    dve.tensor_tensor(res[:, q, :, :], yn[:, :, :], res[:, q, :, :], ALU.add)\
                       .then_inc(res_ready.sem, 1)

            dve.memset(Y[:, 1, :, :], 0.0)
            dve.memset(res[:, 1, :, :], 0.0).then_inc(cleared, 1)
            dve.wait_ge(cleared, 1)
            own.begin(dve, 0, 0)
            own.restart(0)
            choose(0, 0)
            experts_of(0, 0)
            gates(0, 0)
            spread_gates(0, 0)
            own.restart(own.k)
            assert own.k == CHAIN_M_PRE, own.k
            with dve.Fori(0, PAIRS) as pair:
                for half in range(2):
                    own.begin(dve, pair, half)
                    for e in range(NE):
                        for j in range(J):
                            k = e * J + j
                            dve.wait_ge(silued.sem, silued.at(pair, half, k + 1))
                            dve.wait_ge(u_full.sem, u_full.at(pair, half, k + 1))
                            dve.wait_ge(y_full.sem, y_full.at(pair, half, max(e - 1, 0)))
                            dve.tensor_tensor(h[:, e % 2, j, :], psU[:, j, :], sl[:, e % 2, j, :], ALU.mult)\
                               .then_inc(h_full.sem, 1)
                        if e >= 1:
                            accumulate(pair, half, e - 1)
                        if e < 5:
                            finish(pair, half, e)
                        if e == 4:
                            choose(pair, half + 1)
                        if e == 5:
                            experts_of(pair, half + 1)
                        if e == 6:
                            gates(pair, half + 1)
                        if e == 7:
                            spread_gates(pair, half + 1)
                    accumulate(pair, half, NE - 1)
                    own.end()
            own.begin(dve, PAIRS, 0)
            for stage in range(5):
                finish(PAIRS, 0, stage)

        @block.tensor
        def _(pe):
            def prepare(pair, half):
                pe.wait_ge(stage_full.sem, stage_full.at(pair, half, 0))
                for t in range(NT):
                    ins = pe.transpose(psX[:, t * P:(t + 1) * P], staged[:, t, :], ident[:, :])
                ins.then_inc(x_full.sem, 1)

            def route(pair, half):
                pe.wait_ge(h_ready.sem, h_ready.at(pair, half, 0))
                for t in range(NT):
                    ins = pe.matmul(psR[:, t * NE:(t + 1) * NE], hT[:, half % 2, t * P:(t + 1) * P], wr[:, :],
                                    start=True, stop=True)
                ins.then_inc(r_full.sem, 1)

            def down(pair, half, e):
                pe.wait_ge(h_full.sem, h_full.at(pair, half, (e + 1) * J))
                pe.wait_ge(y_used.sem, y_used.at(pair, half, max(e - 1, 0)))
                for t in range(NT):
                    for j in range(J):
                        ins = pe.matmul(psY[:, e % 2, t * P:(t + 1) * P], h[:, e % 2, j, t * P:(t + 1) * P],
                                        wd[:, e, j, :], start=(j == 0), stop=(j == J - 1))
                ins.then_inc(y_full.sem, 1)

            prepare(0, 0)
            route(0, 0)
            with pe.Fori(0, PAIRS) as pair:
                for half in range(2):
                    x = hT[:, half % 2, :]
                    for e in range(NE):
                        for j in range(J):
                            k = e * J + j
                            cols = slice(j * P, (j + 1) * P)
                            pe.wait_ge(silued.sem, silued.at(pair, half, max(k + 1 - J, 0)))
                            pe.matmul(psG[:, j, :], wg[:, e, cols], x, start=True, stop=True).then_inc(g_full.sem, 1)
                            pe.wait_ge(h_full.sem, h_full.at(pair, half, max(k + 1 - J, 0)))
                            pe.matmul(psU[:, j, :], wu[:, e, cols], x, start=True, stop=True).then_inc(u_full.sem, 1)
                        if e >= 1:
                            down(pair, half, e - 1)
                        if e == 1:
                            prepare(pair, half + 1)
                        if e == 3:
                            pe.wait_ge(picked.sem, picked.at(pair, half, 0))
                            route(pair, half + 1)
                    down(pair, half, NE - 1)


def build(nc, ins, consts_in, out, stop=None):
    with ExitStack() as ctx:
        sb = lambda name, shape, dt=FP32: ctx.enter_context(nc.sbuf_tensor(name, shape, dt))
        sem = lambda name: nc.alloc_semaphore(name)
        APART["dve"], APART["pool"] = sb("apart_dve", [P, 1])[:, :], sb("apart_pool", [P, 1])[:, :]
        X = sb("X", [P, TILES + 2 * QT, D])
        F = sb("F", [P, QT + TILES + 4 * QT, D])

        first, later = [], []
        first.append((X[:, QT:QT + TILES, :], ins["x"].rearrange("b (t p) d -> p (b t) d", p=P)))
        wA = {}
        for k in ("Wq", "Wk1", "Wk2", "Wv", "Wo"):
            wA[k] = sb(k, [P, D])
            first.append((wA[k][:, :], ins[k]))
        consts = {}
        for k, shape, group in (("ident", [P, P], first), ("headrow", [P, 16], first), ("expert_id", [P, 8], later)):
            consts[k] = sb(k, shape)
            group.append((consts[k][:, :], consts_in[k]))
        casts = []
        for k, n, src, at in (("identb", P, "ident", 0), ("causal", P, "causal", 1), ("behind", 4 * P, "behind", 2)):
            consts[k] = sb(k, [P, n], BF16)
            wide = F[:, QT + at:QT + at + n // P, :]
            first.append((wide, consts_in[src].rearrange("p (a n) -> p a n", n=P)))
            casts.append((consts[k][:, :].rearrange("p (a n) -> p a n", n=P), wide))
        neglam = consts["neglam"] = sb("neglam", [P, 16])
        first.append((neglam[:, :], ins["lambda_logit"].unsqueeze(0).broadcast_to([P, 16])))
        minus_half = consts["minus_half"] = sb("minus_half", [P, TILES])

        row = lambda a: a.unsqueeze(0).broadcast_to([P, a.shape[0]])
        wB, wF = [], []
        for l in range(2):
            n = str(l)
            w = {"wqk": sb("wqk" + n, [P, 1024]), "wv": sb("wv" + n, [P, 512]), "wo": sb("wo" + n, [P, 4, D]),
                 "cos": sb("cos" + n, [P, QT, 2, 64]), "sin": sb("sin" + n, [P, QT, 2, 64]),
                 "scale": sb("scale" + n, [P, 2, 64]), "scaler": sb("scaler" + n, [P, 2, 64])}
            later += [(w["wqk"][:, :], ins["wqkv"][l, :, 0:1024]), (w["wv"][:, :], ins["wqkv"][l, :, 1024:1536]),
                      (w["wo"][:, :, :], ins["wo"][l].rearrange("(n p) d -> p n d", p=P)),
                      (w["cos"][:, :, :, :], consts_in["cos"]), (w["sin"][:, :, :, :], consts_in["sin"])]
            for a, k in enumerate(("q_scale", "k_scale")):
                s = ins[k][l, :]
                later += [(w["scale"][:, a, :], row(s)), (w["scaler"][:, a, 0:32], row(s[32:64])),
                          (w["scaler"][:, a, 32:64], row(s[0:32]))]
            wB.append(w)
            w = {"w1": sb("w1" + n, [P, 682]), "b1": sb("b1" + n, [P, 6]), "w2": sb("w2" + n, [P, 3, D]),
                 "b2": sb("b2" + n, [P, D]), "ln_g": sb("lng" + n, [P, 1]), "ln_b": sb("lnb" + n, [P, 1])}
            later += [(w["w1"][:, :], ins["w1"][l]), (w["b1"][:, :], ins["b1"][l]), (w["w2"][:, :, :], ins["w2"][l]),
                      (w["b2"][:, :], row(ins["b2"][l, :])), (w["ln_g"][:, :], ins["ln_g"][l, :].unsqueeze(1)),
                      (w["ln_b"][:, :], ins["ln_b"][l, :].unsqueeze(1))]
            wF.append(w)
        wS = {}
        for k, shape in (("W_in", [P, 32]), ("b_in", [P, 1]), ("Bm", [P, P]), ("A", [P, P]), ("AT", [P, P]),
                         ("C", [P, D])):
            wS[k] = sb("s_w" + k, shape)
            later.append((wS[k][:, :], ins["s_" + k]))
        wS["D"] = sb("s_wD", [P, D])
        later.append((wS["D"][:, :], row(ins["s_D"])))
        wM = {"router": sb("m_router", [P, 8]), "gate": sb("m_gate", [P, 8, 256]), "up": sb("m_up", [P, 8, 256]),
              "down": sb("m_down", [P, 8, 2, D])}
        later += [(wM["router"][:, :], ins["router"]), (wM["gate"][:, :, :], ins["w_gate"].rearrange("e d h -> d e h")),
                  (wM["up"][:, :, :], ins["w_up"].rearrange("e d h -> d e h")),
                  (wM["down"][:, :, :, :], ins["w_down"].rearrange("e (j p) d -> p e j d", p=P))]

        loaded, loaded_later, ready = sem("loaded"), sem("loaded_later"), sem("ready")
        with nc.Block() as block:
            @block.sync
            def _(sp):
                for dst, src in first:
                    sp.dma_start(dst, src).then_inc(loaded, 16)
                sp.wait_ge(loaded, 16 * len(first))

            @block.gpsimd
            def _(pool):
                pool.memset(minus_half[:, :], -0.5)
                pool.memset(APART["dve"], 0.0)
                pool.memset(APART["pool"], 0.0)
                pool.memset(X[:, 0:QT, :], 0.0)
                pool.memset(X[:, QT + TILES:TILES + 2 * QT, :], 0.0)
                pool.memset(F[:, 0:QT, :], 0.0)
                pool.memset(F[:, QT + TILES:, :], 0.0).then_inc(ready, 1)

            @block.scalar
            def _(act):
                act.wait_ge(loaded, 16 * len(first))
                act.activation(neglam[:, :], neglam[:, :], ACT.Exp, scale=-1.0).then_inc(ready, 1)

            @block.vector
            def _(dve):
                dve.wait_ge(ready, 2)
                dve.tensor_scalar(neglam[:, :], neglam[:, :], -1.0, -1.0, ALU.mult, ALU.add).then_inc(ready, 1)
                for narrow, wide in casts:
                    dve.tensor_copy(narrow, wide)
                dve.wait_ge(ready, 3)
                dve.reciprocal(neglam[:, :], neglam[:, :]).then_inc(ready, 1)

        def load_later(sp):
            for dst, src in later:
                sp.dma_start(dst, src).then_inc(loaded_later, 16)

        differential_attention(nc, X, consts, wA, load_later)

        if stop != "A":
            with nc.Block() as block:
                @block.vector
                def _(dve):
                    dve.wait_ge(loaded_later, 16 * len(later))
                    for w in wB:
                        for tab, s in (("cos", "scale"), ("sin", "scaler")):
                            for t in range(QT):
                                dve.tensor_tensor(w[tab][:, t], w[tab][:, t], w[s][:, :, :], ALU.mult)
            normalise_all(nc, "n0", X, F, minus_half)
            for l in range(2):
                window_attention(nc, f"b{l}", F, consts, wB[l])
                if stop == "B0":
                    break
                feed_forward(nc, f"f{l}", F, consts, wF[l])
                if stop == "F0":
                    break
            if stop in ("B0", "F0"):
                X = F
            else:
                add_normalised(nc, "n1", X, F, minus_half)
        if stop in (None, "S"):
            state_space(nc, F, consts, wS)
            add_normalised(nc, "n2", X, F, minus_half)
        if stop is None:
            mixture_of_experts(nc, X, F, out, consts, wM)
            return

        stored = nc.alloc_semaphore("stored")
        with nc.Block() as block:
            @block.sync
            def _(sp):
                sp.dma_start(out.rearrange("b (t p) d -> p (b t) d", p=P), X[:, QT:QT + TILES, :]).then_inc(stored, 16)
                sp.wait_ge(stored, 16)


def constants():
    r = np.arange(128)
    c = {
        "ident": np.eye(128, dtype=np.float32),
        "causal": np.where(r[None, :] <= r[:, None], 0.0, -1e37).astype(np.float32),
        "headrow": (r[:, None] // 8 == np.arange(16)[None, :]).astype(np.float32),
    }
    keys = []
    for n, first in enumerate((0, 0, 64, 128)):
        i, j = n * 64 + r[:, None] % 64, first + r[None, :]
        keys.append(np.where((j <= i) & (i <= j + 64), 0.0, -1e37))
    c["behind"] = np.concatenate(keys, 1).astype(np.float32)
    c["expert_id"] = np.tile(np.arange(8, dtype=np.float32), (128, 1))
    f = np.float32
    half = np.arange(0, 64, 2).astype(f)
    inv = f(1) / f(10000) ** (half / f(64))
    t = np.arange(256).astype(f)
    freqs = np.concatenate([t[:, None] * inv[None]] * 2, -1)
    base = (half + f(25.6)) / f(89.6)
    scale = base[None] ** ((t - f(128)) / f(32))[:, None]
    scale = np.concatenate([scale] * 2, -1)
    sign = np.where(np.arange(64) < 32, -1, 1).astype(f)
    both = lambda a: np.stack([f(8) * a * scale, a / scale], 1)
    tiles = lambda a: np.ascontiguousarray(both(a).reshape(2, 128, 2, 64).transpose(1, 0, 2, 3)).astype(f)
    c["cos"] = tiles(np.cos(freqs))
    c["sin"] = tiles(np.sin(freqs) * sign)
    return c


def layout(inputs):
    a = {k: np.asarray(v) for k, v in inputs.items()}
    c = np.ascontiguousarray
    b1 = np.zeros((2, 2, 384), np.float32)
    b1[:, :, :341] = a["L0_ffn_b1"].reshape(2, 2, 341)
    b1 = c(b1.reshape(2, 6, 128).transpose(0, 2, 1))
    w2 = np.zeros((2, 384, 128), np.float32)
    w2[:, :341] = a["L0_ffn_w2"]
    w2 = c(w2.reshape(2, 3, 128, 128).transpose(0, 2, 1, 3))

    def diagonal(m):
        big = np.zeros((128, 128), np.float32)
        for g in range(4):
            big[32 * g:32 * g + 32, 32 * g:32 * g + 32] = m
        return big

    return {
        "x": c(a["L0_attn_x"]),
        **{k: c(a["L0_attn_" + k].T) for k in ("Wq", "Wk1", "Wk2", "Wv", "Wo")},
        "lambda_logit": c(a["L0_attn_lambda_logit"]),
        **{k: c(a["L0_ffn_" + k]) for k in ("wqkv", "q_scale", "k_scale", "wo", "w1", "b2", "ln_g", "ln_b")},
        "b1": b1,
        "w2": w2,
        "s_W_in": c(a["L1_attn_W_in"].T),
        "s_b_in": c(np.tile(a["L1_attn_b_in"], 4)[:, None]),
        "s_Bm": diagonal(a["L1_attn_Bm"].T),
        "s_A": diagonal(a["L1_attn_A"]),
        "s_AT": diagonal(a["L1_attn_A"].T),
        "s_C": c(np.tile(a["L1_attn_C"].T, (4, 1))),
        "s_D": c(a["L1_attn_D"]),
        "router": c(a["L1_ffn_router_w"].T),
        **{k: c(a["L1_ffn_" + k]) for k in ("w_gate", "w_up", "w_down")},
    }


def kernel(**inputs):
    import concourse.bacc as bacc
    from concourse.bass_utils import run_bass_kernel_spmd as run

    nc = bacc.Bacc("TRN2", target_bir_lowering=False, num_devices=1)
    arrays, ins, consts = {}, {}, {}
    for group, into in ((layout(inputs), ins), (constants(), consts)):
        for name, a in group.items():
            full = f"in_{name}_dram"
            arrays[full] = a
            into[name] = nc.dram_tensor(full, a.shape, mybir.dt.from_np(a.dtype), kind="ExternalInput").ap()
    out = nc.dram_tensor("out_0_dram", (16, 256, 128), FP32, kind="ExternalOutput").ap()
    build(nc, ins, consts, out)
    r = run(nc, [arrays], core_ids=[0])
    return r.results[0]["out_0_dram"]
```
